# Optimizing a Trainium2 kernel written in Bass

```python
import numpy as np
import jax
import jax.numpy as jnp

def _softmax(x, axis=-1):
    return jax.nn.softmax(x, axis=axis)

def _gelu(x):
    return jax.nn.gelu(x, approximate=True)

def _silu(x):
    return jax.nn.silu(x)

def _sigmoid(x):
    return jax.nn.sigmoid(x)

def _layernorm(x, axis=-1, eps=1e-05):
    m = jnp.mean(x, axis=axis, keepdims=True)
    v = jnp.var(x, axis=axis, keepdims=True)
    return (x - m) / jnp.sqrt(v + eps)

def _scatter_add(tgt, idx, src, axis=0):
    return tgt.at[idx].add(src)

def _segment_sum(src, seg, n):
    return jax.ops.segment_sum(src, seg, n)
kernel_name = 'mk_lm_tower_d1_tok_ids256_r4_1cde92'

def setup_inputs(seed: int=0):
    np.random.seed(seed)
    _w = jnp.asarray

    def _rec_inputs():
        import jax
        import jax.numpy as jnp
        _rk = jax.random.key(seed)
        x = jax.random.randint(jax.random.fold_in(_rk, 1), (64, 128), 0, 64, jnp.int32)
        return x
    x = _rec_inputs()

    def _L0_tok_setup():
        import jax, jax.numpy as jnp
        import numpy as np
        B, T, D = (32, 1024, 64)
        LN_EPS = 1e-05
        key = jax.random.key(seed)
        k0, k1, k2 = jax.random.split(key, 3)
        byte_ids = jax.random.randint(k0, (B, T), 0, 64, dtype=jnp.int32)
        freq_bands = jnp.ones((D // 2,), jnp.float32)
        w1 = jax.random.normal(k1, (D, 2 * D), jnp.float32) * (1.0 / np.sqrt(D))
        b1 = jnp.zeros((2 * D,), jnp.float32)
        gamma = jnp.ones((2 * D,), jnp.float32)
        beta = jnp.zeros((2 * D,), jnp.float32)
        w2 = jax.random.normal(k2, (2 * D, D), jnp.float32) * (1.0 / np.sqrt(2 * D))
        b2 = jnp.zeros((D,), jnp.float32)
        return dict(byte_ids=byte_ids, freq_bands=freq_bands, w1=w1, b1=b1, gamma=gamma, beta=beta, w2=w2, b2=b2)
    _L0_tok_all = _L0_tok_setup()
    _L0_tok_in = {k: v for k, v in _L0_tok_all.items() if k in ('freq_bands', 'w1', 'b1', 'gamma', 'beta', 'w2', 'b2')}
    del _L0_tok_all

    def _L0_attn_setup():
        import jax, jax.numpy as jnp
        import numpy as np
        D_MODEL = 64
        D_STATE = 64
        D_CONV = 4
        EXPAND = 4
        HEADDIM = 64
        CHUNK = 64
        D_INNER = EXPAND * D_MODEL
        NHEADS = D_INNER // HEADDIM
        CONV_DIM = D_INNER + 2 * D_STATE
        D_IN_PROJ = 2 * D_INNER + 2 * D_STATE + NHEADS
        BATCH = 4
        SEQLEN = 1024

        def _segsum_exp(x):
            T = x.shape[-1]
            cs = jnp.cumsum(x, axis=-1)
            seg = cs[..., :, None] - cs[..., None, :]
            mask = jnp.tril(jnp.ones((T, T), dtype=bool))
            return jnp.where(mask, jnp.exp(seg), 0.0)

        def _ssd(x, A, B, C, chunk):
            b, l, h, p = x.shape
            c = l // chunk
            xc = x.reshape(b, c, chunk, h, p)
            Ac = A.reshape(b, c, chunk, h).transpose(0, 3, 1, 2)
            Bc = B.reshape(b, c, chunk, -1)
            Cc = C.reshape(b, c, chunk, -1)
            A_cs = jnp.cumsum(Ac, axis=-1)
            L = _segsum_exp(Ac)
            Y_diag = jnp.einsum('bcln,bcsn,bhcls,bcshp->bclhp', Cc, Bc, L, xc)
            decay_states = jnp.exp(A_cs[..., -1:] - A_cs)
            states = jnp.einsum('bcln,bhcl,bclhp->bchpn', Bc, decay_states, xc)
            states = jnp.concatenate([jnp.zeros_like(states[:, :1]), states], axis=1)
            A_last = jnp.pad(A_cs[..., -1], ((0, 0), (0, 0), (1, 0)))
            decay_chunk = _segsum_exp(A_last)
            new_states = jnp.einsum('bhzc,bchpn->bzhpn', decay_chunk, states)
            states_prev, final_state = (new_states[:, :-1], new_states[:, -1])
            state_decay_out = jnp.exp(A_cs)
            Y_off = jnp.einsum('bcln,bchpn,bhcl->bclhp', Cc, states_prev, state_decay_out)
            Y = (Y_diag + Y_off).reshape(b, l, h, p)
            return (Y, final_state)

        def _silu(x):
            return x * jax.nn.sigmoid(x)
        key = jax.random.key(seed)
        ks = jax.random.split(key, 8)
        return {'u': jax.random.normal(ks[0], (BATCH, SEQLEN, D_MODEL), jnp.float32), 'in_proj_w': jax.random.normal(ks[1], (D_IN_PROJ, D_MODEL), jnp.float32) * 0.02, 'conv_w': jax.random.normal(ks[2], (CONV_DIM, 1, D_CONV), jnp.float32) * 0.2, 'conv_b': jnp.zeros((CONV_DIM,), jnp.float32), 'dt_bias': jax.random.normal(ks[3], (NHEADS,), jnp.float32) * 0.1, 'A_log': jax.random.normal(ks[4], (NHEADS,), jnp.float32) * 0.1, 'D': jax.random.normal(ks[5], (NHEADS,), jnp.float32) * 0.1, 'norm_w': jnp.ones((D_INNER,), jnp.float32), 'out_proj_w': jax.random.normal(ks[6], (D_MODEL, D_INNER), jnp.float32) * 0.02}
    _L0_attn_all = _L0_attn_setup()
    _L0_attn_in = {k: v for k, v in _L0_attn_all.items() if k in ('in_proj_w', 'conv_w', 'conv_b', 'dt_bias', 'A_log', 'D', 'norm_w', 'out_proj_w')}
    del _L0_attn_all

    def _L0_ffn_setup():
        import jax, jax.numpy as jnp
        import numpy as np
        B, S, D, H, E, K = (8, 2048, 64, 256, 8, 2)
        key = jax.random.key(seed)
        ks = jax.random.split(key, 7)
        s_in = 1.0 / np.sqrt(D)
        s_hid = 1.0 / np.sqrt(H)
        return {'x': jax.random.normal(ks[0], (B, S, D), dtype=jnp.float32), 'Wg': jax.random.uniform(ks[1], (E, D), jnp.float32, -s_in, s_in), 'bg': jax.random.uniform(ks[2], (E,), jnp.float32, -s_in, s_in), 'W1': jax.random.uniform(ks[3], (E, H, D), jnp.float32, -s_in, s_in), 'b1': jax.random.uniform(ks[4], (E, H), jnp.float32, -s_in, s_in), 'W2': jax.random.uniform(ks[5], (E, D, H), jnp.float32, -s_hid, s_hid), 'b2': jax.random.uniform(ks[6], (E, D), jnp.float32, -s_hid, s_hid)}
    _L0_ffn_all = _L0_ffn_setup()
    _L0_ffn_in = {k: v for k, v in _L0_ffn_all.items() if k in ('Wg', 'bg', 'W1', 'b1', 'W2', 'b2')}
    del _L0_ffn_all
    return {'x': x, 'L0_tok_freq_bands': _L0_tok_in['freq_bands'], 'L0_tok_w1': _L0_tok_in['w1'], 'L0_tok_b1': _L0_tok_in['b1'], 'L0_tok_gamma': _L0_tok_in['gamma'], 'L0_tok_beta': _L0_tok_in['beta'], 'L0_tok_w2': _L0_tok_in['w2'], 'L0_tok_b2': _L0_tok_in['b2'], 'L0_attn_in_proj_w': _L0_attn_in['in_proj_w'], 'L0_attn_conv_w': _L0_attn_in['conv_w'], 'L0_attn_conv_b': _L0_attn_in['conv_b'], 'L0_attn_dt_bias': _L0_attn_in['dt_bias'], 'L0_attn_A_log': _L0_attn_in['A_log'], 'L0_attn_D': _L0_attn_in['D'], 'L0_attn_norm_w': _L0_attn_in['norm_w'], 'L0_attn_out_proj_w': _L0_attn_in['out_proj_w'], 'L0_ffn_Wg': _L0_ffn_in['Wg'], 'L0_ffn_bg': _L0_ffn_in['bg'], 'L0_ffn_W1': _L0_ffn_in['W1'], 'L0_ffn_b1': _L0_ffn_in['b1'], 'L0_ffn_W2': _L0_ffn_in['W2'], 'L0_ffn_b2': _L0_ffn_in['b2']}

def reference(x, L0_tok_freq_bands, L0_tok_w1, L0_tok_b1, L0_tok_gamma, L0_tok_beta, L0_tok_w2, L0_tok_b2, L0_attn_in_proj_w, L0_attn_conv_w, L0_attn_conv_b, L0_attn_dt_bias, L0_attn_A_log, L0_attn_D, L0_attn_norm_w, L0_attn_out_proj_w, L0_ffn_Wg, L0_ffn_bg, L0_ffn_W1, L0_ffn_b1, L0_ffn_W2, L0_ffn_b2):
    import jax
    import jax.numpy as jnp

    def _L0_tok_ref(byte_ids, freq_bands, w1, b1, gamma, beta, w2, b2):
        import jax, jax.numpy as jnp
        import numpy as np
        B, T, D = (32, 1024, 64)
        LN_EPS = 1e-05
        Bsz, Tlen = byte_ids.shape
        Dm = w1.shape[0]
        k = min(Dm // 2, Tlen // 2)
        signal = byte_ids.astype(jnp.float32) / 127.5 - 1.0
        X = jnp.fft.fft(signal, axis=1)[:, :k]
        mag = jnp.abs(X) * freq_bands[:k]
        phase0 = jnp.angle(X)
        pos = jnp.arange(Tlen, dtype=jnp.float32)
        f = jnp.arange(k, dtype=jnp.float32)
        shift = 2.0 * np.pi / Tlen * pos[:, None] * f[None, :]
        phase = phase0[:, None, :] + shift[None, :, :]
        mag_bt = jnp.broadcast_to(mag[:, None, :], (Bsz, Tlen, k))
        feats = jnp.concatenate([mag_bt, jnp.sin(phase), jnp.cos(phase)], axis=-1)
        if feats.shape[-1] < Dm:
            feats = jnp.pad(feats, ((0, 0), (0, 0), (0, Dm - feats.shape[-1])))
        else:
            feats = feats[..., :Dm]
        h = feats @ w1 + b1
        mu = jnp.mean(h, axis=-1, keepdims=True)
        var = jnp.var(h, axis=-1, keepdims=True)
        h = (h - mu) * jax.lax.rsqrt(var + LN_EPS) * gamma + beta
        h = jax.nn.gelu(h, approximate=False)
        return h @ w2 + b2

    def _L0_attn_ref(u, in_proj_w, conv_w, conv_b, dt_bias, A_log, D, norm_w, out_proj_w):
        import jax, jax.numpy as jnp
        import numpy as np
        D_MODEL = 64
        D_STATE = 64
        D_CONV = 4
        EXPAND = 4
        HEADDIM = 64
        CHUNK = 64
        D_INNER = EXPAND * D_MODEL
        NHEADS = D_INNER // HEADDIM
        CONV_DIM = D_INNER + 2 * D_STATE
        D_IN_PROJ = 2 * D_INNER + 2 * D_STATE + NHEADS
        BATCH = 4
        SEQLEN = 1024

        def _segsum_exp(x):
            T = x.shape[-1]
            cs = jnp.cumsum(x, axis=-1)
            seg = cs[..., :, None] - cs[..., None, :]
            mask = jnp.tril(jnp.ones((T, T), dtype=bool))
            return jnp.where(mask, jnp.exp(seg), 0.0)

        def _ssd(x, A, B, C, chunk):
            b, l, h, p = x.shape
            c = l // chunk
            xc = x.reshape(b, c, chunk, h, p)
            Ac = A.reshape(b, c, chunk, h).transpose(0, 3, 1, 2)
            Bc = B.reshape(b, c, chunk, -1)
            Cc = C.reshape(b, c, chunk, -1)
            A_cs = jnp.cumsum(Ac, axis=-1)
            L = _segsum_exp(Ac)
            Y_diag = jnp.einsum('bcln,bcsn,bhcls,bcshp->bclhp', Cc, Bc, L, xc)
            decay_states = jnp.exp(A_cs[..., -1:] - A_cs)
            states = jnp.einsum('bcln,bhcl,bclhp->bchpn', Bc, decay_states, xc)
            states = jnp.concatenate([jnp.zeros_like(states[:, :1]), states], axis=1)
            A_last = jnp.pad(A_cs[..., -1], ((0, 0), (0, 0), (1, 0)))
            decay_chunk = _segsum_exp(A_last)
            new_states = jnp.einsum('bhzc,bchpn->bzhpn', decay_chunk, states)
            states_prev, final_state = (new_states[:, :-1], new_states[:, -1])
            state_decay_out = jnp.exp(A_cs)
            Y_off = jnp.einsum('bcln,bchpn,bhcl->bclhp', Cc, states_prev, state_decay_out)
            Y = (Y_diag + Y_off).reshape(b, l, h, p)
            return (Y, final_state)

        def _silu(x):
            return x * jax.nn.sigmoid(x)
        b, l, _ = u.shape
        A = -jnp.exp(A_log)
        zxbcdt = u @ in_proj_w.T
        z = zxbcdt[..., :D_INNER]
        xBC = zxbcdt[..., D_INNER:D_INNER + CONV_DIM]
        dt = jax.nn.softplus(zxbcdt[..., -NHEADS:] + dt_bias)
        xp = jnp.pad(xBC, ((0, 0), (D_CONV - 1, 0), (0, 0)))
        conv = conv_b
        for w in range(D_CONV):
            conv = conv + xp[:, w:w + l, :] * conv_w[:, 0, w]
        xBC = _silu(conv)
        x = xBC[..., :D_INNER].reshape(b, l, NHEADS, HEADDIM)
        Bm = xBC[..., D_INNER:D_INNER + D_STATE]
        Cm = xBC[..., -D_STATE:]
        y, _final_state = _ssd(x * dt[..., None], A * dt, Bm, Cm, CHUNK)
        y = y + x * D[:, None]
        y = y.reshape(b, l, D_INNER)
        y = y * _silu(z)
        y = y * jax.lax.rsqrt(jnp.mean(y * y, axis=-1, keepdims=True) + 1e-05) * norm_w
        return y @ out_proj_w.T

    def _L0_ffn_ref(x, Wg, bg, W1, b1, W2, b2):
        import jax, jax.numpy as jnp
        import numpy as np
        B, S, D, H, E, K = (8, 2048, 64, 256, 8, 2)
        gate_scores = jnp.einsum('bsd,ed->bse', x, Wg) + bg
        topk_scores, topk_idx = jax.lax.top_k(gate_scores, K)
        topk_probs = jax.nn.softmax(topk_scores, axis=-1)
        combine = jnp.sum(topk_probs[..., None] * jax.nn.one_hot(topk_idx, E, dtype=x.dtype), axis=-2)
        out = jnp.zeros_like(x)
        for e in range(E):
            h = jax.nn.relu(jnp.einsum('bsd,hd->bsh', x, W1[e]) + b1[e])
            y = jnp.einsum('bsh,dh->bsd', h, W2[e]) + b2[e]
            out = out + combine[..., e:e + 1] * y
        return out
    h = _L0_tok_ref(x, L0_tok_freq_bands, L0_tok_w1, L0_tok_b1, L0_tok_gamma, L0_tok_beta, L0_tok_w2, L0_tok_b2)
    h = h + _L0_attn_ref(_layernorm(h, axis=-1), L0_attn_in_proj_w, L0_attn_conv_w, L0_attn_conv_b, L0_attn_dt_bias, L0_attn_A_log, L0_attn_D, L0_attn_norm_w, L0_attn_out_proj_w)
    h = h + _L0_ffn_ref(_layernorm(h, axis=-1), L0_ffn_Wg, L0_ffn_bg, L0_ffn_W1, L0_ffn_b1, L0_ffn_W2, L0_ffn_b2)
    return h

_drawn_inputs = setup_inputs


def setup_inputs(seed=0):
    import zlib

    import numpy as np

    out = dict(_drawn_inputs(seed))
    spreads = {'L0_tok_freq_bands': (1.0, 0.2),
     'L0_tok_b1': (0.0, 0.8),
     'L0_tok_gamma': (1.0, 0.2),
     'L0_tok_beta': (0.0, 0.1),
     'L0_tok_b2': (0.0, 0.1),
     'L0_attn_conv_b': (0.0, 0.1),
     'L0_attn_norm_w': (1.0, 0.6)}
    factors = {'L0_attn_dt_bias': 27.224, 'L0_attn_A_log': 30.484, 'L0_ffn_bg': 8.0, 'L0_ffn_b1': 2.999}
    for name, (base, spread) in spreads.items():
        noise = np.random.default_rng([zlib.crc32(name.encode()), seed]).standard_normal(out[name].shape)
        drawn = base * np.exp(spread * noise) if base else spread * noise
        out[name] = jnp.asarray(drawn.astype(out[name].dtype))
    for name, factor in factors.items():
        out[name] = (out[name] * factor).astype(out[name].dtype)
    return out
```

```python
from contextlib import ExitStack

import numpy as np
import concourse.bass as bass
from concourse import mybir

F32 = mybir.dt.float32
F16 = mybir.dt.float16
I32 = mybir.dt.int32
U32 = mybir.dt.uint32
ALU = mybir.AluOpType
ACT = mybir.ActivationFunctionType
AX = mybir.AxisListType

NSEQ, T = 64, 128
D, HID = 64, 128
NF = 32
DI, NH, HD, NS, KW = 256, 4, 64, 64, 4
NXBC = DI + 2 * NS
E, EH = 8, 256
GB = 4
NG = NSEQ // GB
GT = GB * T
NK = 3 * NF + 1
PAD = 3
SW = PAD + T + 1
NQ = 2 * E
LN_EPS = 1e-5
WSCALE = 256.0
MASKED = -1e30


def constants():
    t = np.arange(T, dtype=np.float64)
    f = np.arange(NF, dtype=np.float64)
    ang = 2 * np.pi / T * ((t[:, None] * f[None, :]) % T)
    cos, sin = np.cos(ang), np.sin(ang)
    dft = np.zeros((T, 2, 3 * NF), np.float32)
    dft[:, 0] = np.tile(cos, (1, 3))
    dft[:, 1] = np.tile(-sin, (1, 3))
    shift = np.ones((NK, T), np.float32)
    shift[NF:2 * NF] = cos.T
    shift[2 * NF:3 * NF] = sin.T
    dc = np.zeros((3 * NF, 1), np.float32)
    dc[::NF] = -float(T)
    s = np.arange(T)
    upto = (s[:, None] <= s[None, :])
    return {
        "dft": dft.reshape(T, -1), "shift": shift, "dc": dc,
        "upto": upto.astype(np.float32),
        "mask": np.where(upto, 0.0, MASKED).astype(np.float32),
        "ident": np.eye(128, dtype=np.float32),
        "iota": np.tile(np.arange(E, dtype=np.float32), (128, 1)),
    }


def build(nc, inp, out):
    with ExitStack() as ctx:
        def sb(name, shape, dt=F32):
            return ctx.enter_context(nc.sbuf_tensor(name, shape, dt))

        def sem(name):
            return ctx.enter_context(nc.semaphore(name))

        bank = [ctx.enter_context(nc.psum_tensor(f"bank{i}", [128, 512], F32)) for i in range(8)]

        ident = sb("ident", [128, 128])
        mask = sb("mask", [128, T])
        upto = sb("upto", [128, T])
        iota = sb("iota", [128, E])
        dft = sb("dft_sb", [128, 2, 3 * NF])
        shift = sb("shift_sb", [NK, T])
        dc = sb("dc_sb", [3 * NF, 1])
        ids = sb("ids", [128, NSEQ], I32)
        idsf = sb("idsf", [128, NSEQ])
        freq = sb("freq", [NF, 1])
        w1x = sb("w1x", [NK, HID])
        w1c = sb("w1c", [NK, HID])
        gamma = sb("gamma", [HID, 1])
        beta = sb("beta", [HID, 1])
        w2x = sb("w2x", [HID, 2, D])
        b2x = sb("b2x", [128, 2, D])
        wc_hi = sb("wc_hi", [128, 2, NXBC], F16)
        wc_lo = sb("wc_lo", [128, 2, NXBC], F16)
        wz_hi = sb("wz_hi", [128, DI + NH], F16)
        wz_lo = sb("wz_lo", [128, DI + NH], F16)
        convb_row = sb("convb_row", [1, DI])
        convb_hi = sb("convb_hi", [128, DI], F16)
        convb_lo = sb("convb_lo", [128, DI], F16)
        convb_bc = sb("convb_bc", [128, 1])
        ones16 = sb("ones16", [128, 128], F16)
        ones = sb("ones_col", [128, 1])
        dtbias = sb("dtbias", [128, NH])
        aneg = sb("aneg", [128, NH])
        dskip = sb("dskip", [128, NH])
        normw = sb("normw", [128, 2])
        wo = sb("wo", [128, 2, 2, D])
        wg = sb("wg", [128, E])
        wg_hi = sb("wg_hi", [128, E], F16)
        wg_lo = sb("wg_lo", [128, E], F16)
        bg = sb("bg", [128, E])
        ew1_hi = sb("ew1_hi", [128, E * EH], F16)
        ew1_lo = sb("ew1_lo", [128, E * EH], F16)
        eb1 = sb("eb1", [128, NQ])
        ew2 = sb("ew2", [128, NQ, D])
        eb2 = sb("eb2", [GB * E, GB, D])
        mhalf = sb("mhalf", [128, GB])
        euler = sb("euler", [128, GB])
        rowsum = sb("rowsum", [128, 8])

        re = sb("re", [3 * NF, NSEQ])
        im = sb("im", [3 * NF, NSEQ])
        m2 = sb("m2", [3 * NF, NSEQ])
        im2 = sb("im2", [3 * NF, NSEQ])
        zero = sb("zero", [3 * NF, NSEQ])
        mhalf_w = sb("mhalf_w", [3 * NF, NSEQ])
        inv = sb("inv", [3 * NF, NSEQ])
        coef = sb("coef", [NK, NSEQ])

        h = sb("h", [128, NG, GB, 2, D])
        ut_hi = sb("ut_hi", [128, NSEQ, SW], F16)
        ut_lo = sb("ut_lo", [128, NSEQ, SW], F16)
        dt = sb("dt", [128, NSEQ * NH])
        cs = sb("cs", [128, NSEQ * NH])

        wsc = sb("wsc", [NK, 2, GB, HID])
        hsq = sb("hsq", [128, 2, GB, HID])
        ssq1 = sb("ssq1", [128, 2, GB])
        var1 = sb("var1", [128, 2, GB])
        rstd1 = sb("rstd1", [128, 2, GB])
        hn = sb("hn", [128, 2, GB, HID])
        gel = sb("gel", [HID, 2, GT])
        csq = sb("csq", [128, 2, GB, D])
        ssq2 = sb("ssq2", [128, 2, GB])
        var2 = sb("var2", [128, 2, GB])
        rstd2 = sb("rstd2", [128, 2, GB])
        udup = sb("udup", [128, 2, GB, 2, D])

        csT = sb("csT", [128, 2, T])
        cs_dram = nc.dram_tensor("cs_dram", [NSEQ * NH, T], F32).ap()

        csb = sb("csb", [128, GB * NH, T])
        dec = sb("dec", [128, GB, NH, T])
        xs = sb("xs", [128, GB, NH, HD])
        xdt = sb("xdt", [128, GB, NH, HD])
        xd = sb("xd", [128, GB, NH, HD])
        zs = sb("zs", [128, 2, GT])
        bT = sb("bT", [NS, GT])
        cT = sb("cT", [NS, GT])
        yg = sb("yg", [128, 2, GT])
        ysq = sb("ysq", [128, 2, GT])
        yvar = sb("yvar", [128, GB])
        yrstd = sb("yrstd", [128, GB])
        hadd = sb("hadd", [128, GB, 2, D])
        hsq2 = sb("hsq2", [128, GB, D])
        ssq3 = sb("ssq3", [128, GB])
        var3 = sb("var3", [128, GB])
        rstd3 = sb("rstd3", [128, GB])
        u2 = sb("u2", [128, GB, 2, D])
        u2T = sb("u2T", [128, GT], F16)
        score = sb("score", [128, GB, E])
        top = sb("top", [128, GB, 8])
        topi = sb("topi", [128, GB, 8], U32)
        topf = sb("topf", [128, GB, 2])
        gap = sb("gap", [128, GB])
        egap = sb("egap", [128, GB])
        gsum = sb("gsum", [128, GB])
        prob = sb("prob", [128, 2, GB])
        pick = sb("pick", [128, 2, GB, E])
        comb = sb("comb", [128, GB, E])
        combT = sb("combT", [GB * E, T])
        hb = sb("hb", [128, GB, D])
        hid = sb("hid", [128, 4, GT])
        prod = sb("prod", [128, 4, GB, 2, D])
        sum2 = sb("sum2", [128, 2, GB, 2, D])
        sum1 = sb("sum1", [128, GB, 2, D])
        sum0 = sb("sum0", [128, GB, D])
        res = sb("res", [128, GB, D])

        ew1 = dec[:, :, :, :].rearrange("p b h t -> p (b h t)")
        win = csb[:, :, :].rearrange("p a t -> p (a t)")[:, 0:2 * DI + 2 * NS + NH]
        prod_flat = prod[:, :].rearrange("p a b e d -> p (a b e d)")
        taps = prod_flat[:, 0:2 * NXBC].rearrange("p (a c) -> p a c", a=2)
        wtmp = prod_flat[:, 2 * NXBC:3 * NXBC]
        xdt_flat = xdt[:, :, :, :].rearrange("p b h d -> p (b h d)")
        sp = [xdt_flat[:, i * NSEQ * NH:(i + 1) * NSEQ * NH] for i in range(3)]

        loaded = sem("loaded")
        bigloaded = sem("bigloaded")
        poolset = sem("poolset")
        poolc = sem("poolc")
        dvec = sem("dvec")
        weights_ready = sem("weights_ready")
        spec_ps = sem("spec_ps")
        m2_ready = sem("m2_ready")
        inv_ready = sem("inv_ready")
        coef_ready = sem("coef_ready")
        ids_ready = sem("ids_ready")
        bias_rows = sem("bias_rows")
        aexp = sem("aexp")
        wsc_ready = sem("wsc_ready")
        h_ps = sem("h_ps")
        hsq_ready = sem("hsq_ready")
        ssq1_ready = sem("ssq1_ready")
        var1_ready = sem("var1_ready")
        rstd1_ready = sem("rstd1_ready")
        hn_ready = sem("hn_ready")
        hnT_ps = sem("hnT_ps")
        gel_ready = sem("gel_ready")
        h1_ps = sem("h1_ps")
        h1_ready = sem("h1_ready")
        csq_ready = sem("csq_ready")
        ssq2_ready = sem("ssq2_ready")
        var2_ready = sem("var2_ready")
        rstd2_ready = sem("rstd2_ready")
        u_ready = sem("u_ready")
        uT_ps = sem("uT_ps")
        uhi_ready = sem("uhi_ready")
        ulo_ready = sem("ulo_ready")
        dt_ps = sem("dt_ps")
        dt_copied = sem("dt_copied")
        sp_dve = sem("sp_dve")
        sp_act = sem("sp_act")
        cs_ps = sem("cs_ps")
        cs_ready = sem("cs_ready")
        csT_ps = sem("csT_ps")
        csT_ready = sem("csT_ready")
        cs_saved = sem("cs_saved")
        csb_loaded = sem("csb_loaded")
        exponent_ready = sem("exponent_ready")
        decay_ready = sem("decay_ready")
        x_ps = sem("x_ps")
        xs_ready = sem("xs_ready")
        z_ps = sem("z_ps")
        zs_ready = sem("zs_ready")
        bc_ps = sem("bc_ps")
        bc_ready = sem("bc_ready")
        xdt_ready = sem("xdt_ready")
        xd_ready = sem("xd_ready")
        g_ps = sem("g_ps")
        mix_ready = sem("mix_ready")
        y_ps = sem("y_ps")
        yg_ready = sem("yg_ready")
        ysq_ready = sem("ysq_ready")
        yssq_ps = sem("yssq_ps")
        yvar_ready = sem("yvar_ready")
        yrstd_ready = sem("yrstd_ready")
        o_ps = sem("o_ps")
        hadd_ready = sem("hadd_ready")
        h2_ready = sem("h2_ready")
        hsq2_ready = sem("hsq2_ready")
        ssq3_ready = sem("ssq3_ready")
        var3_ready = sem("var3_ready")
        rstd3_ready = sem("rstd3_ready")
        u2_ready = sem("u2_ready")
        u2T_ps = sem("u2T_ps")
        u2hi_ready = sem("u2hi_ready")
        u2lo_ready = sem("u2lo_ready")
        s_ps = sem("s_ps")
        gate = sem("gate")
        gate_sum = sem("gate_sum")
        gate_mul = sem("gate_mul")
        gap_ready = sem("gap_ready")
        egap_ready = sem("egap_ready")
        combT_ps = sem("combT_ps")
        combT_ready = sem("combT_ready")
        b2_ps = sem("b2_ps")
        hb_ready = sem("hb_ready")
        hid_ps = sem("hid_ps")
        hid_act = sem("hid_act")
        hid_dve = sem("hid_dve")
        down_done = sem("down_done")
        prod_ready = sem("prod_ready")
        tree = sem("tree")
        res_ready = sem("res_ready")
        stored = sem("stored")

        block = ctx.enter_context(nc.Block())

        small_loads = [
            (ids[:, :], inp["ids"]), (dft[:, :, :].rearrange("p a b -> p (a b)"), inp["dft"]),
            (dc[:, :], inp["dc"]), (shift[:, :], inp["shift"]),
            (freq[:, :], inp["freq"].rearrange("(p a) -> p a", a=1)),
            (w1x[0:2 * NF, :], inp["tw1"]), (w1x[2 * NF:3 * NF, :], inp["tw1"][NF:2 * NF, :]),
            (w1x[3 * NF:NK, :], inp["tb1"].rearrange("(a p) -> a p", a=1)),
            (gamma[:, :], inp["gamma"].rearrange("(p a) -> p a", a=1)),
            (beta[:, :], inp["beta"].rearrange("(p a) -> p a", a=1)),
            (w2x[:, 0, :], inp["tw2"]), (b2x[:, 0, :], inp["tb2"].partition_broadcast(128)),
            (ident[:, :], inp["ident"]), (mask[:, :], inp["mask"]), (upto[:, :], inp["upto"]),
            (iota[:, :], inp["iota"]),
            (win[0:D, :], inp["winT"]), (win[D:128, :], inp["winT"]),
            (taps[0:D, 0, :], inp["convT"][3].partition_broadcast(D)),
            (taps[D:128, 0, :], inp["convT"][2].partition_broadcast(D)),
            (taps[0:D, 1, :], inp["convT"][1].partition_broadcast(D)),
            (taps[D:128, 1, :], inp["convT"][0].partition_broadcast(D)),
            (convb_row[:, :], inp["convb"][0:DI].rearrange("(a c) -> a c", a=1)),
            (convb_bc[:, :], inp["convb"][DI:NXBC].rearrange("(p a) -> p a", a=1)),
            (dtbias[:, :], inp["dtbias"].partition_broadcast(128)),
            (aneg[:, :], inp["alog"].partition_broadcast(128)),
            (dskip[:, :], inp["dskip"].partition_broadcast(128)),
        ]
        big_loads = [
            (normw[:, :], inp["normw"].rearrange("(a p) -> p a", a=2)),
            (wo[:, 0, 0, :], inp["woT"][0:128, :]), (wo[:, 1, 0, :], inp["woT"][128:256, :]),
            (wg[0:D, :], inp["wgT"]), (wg[D:128, :], inp["wgT"]),
            (bg[:, :], inp["bg"].partition_broadcast(128)),
            (ew1[0:D, :], inp["ew1T"]), (ew1[D:128, :], inp["ew1T"]),
            (eb1[:, :], inp["eb1"].rearrange("e (j p) -> p (e j)", j=2)),
            (ew2[:, :, :], inp["ew2T"].rearrange("(q p) d -> p q d", p=128)),
        ]
        NSMALL, NBIG = len(small_loads), len(big_loads) + GB

        def live(g):
            return not isinstance(g, int) or 0 <= g < NG

        def after(g, n):
            return not isinstance(g, int) or g >= n

        def stretch(eng, step, lead, unroll, tail):
            for k in range(lead):
                step(k, k % unroll)
            with eng.Fori(0, (NG - lead) // unroll) as i:
                for s in range(unroll):
                    step(i * unroll + (lead + s), (lead + s) % unroll)
            for k in range(NG, NG + tail):
                step(k, k % unroll)

        T_LEAD, T_TAIL = 4, 2
        L_LEAD, L_TAIL = 4, 3

        @block.sync
        def _(sp_):
            for dst, src in small_loads:
                sp_.dma_start(dst, src, allow_slow_non_contiguous=True).then_inc(loaded, 16)
            for dst, src in big_loads:
                sp_.dma_start(dst, src, allow_slow_non_contiguous=True).then_inc(bigloaded, 16)
            sp_.wait_ge(poolset, 1)
            for b in range(GB):
                sp_.dma_start(eb2[b * E:(b + 1) * E, b, :], inp["eb2"]).then_inc(bigloaded, 16)

            sp_.wait_ge(csT_ready, 1)
            sp_.dma_start(cs_dram.rearrange("(a p) t -> p a t", a=2), csT[:, :, :]).then_inc(cs_saved, 16)
            sp_.wait_ge(cs_saved, 16)

            def step(k, slot):
                m, r = k, k - 3
                if live(m):
                    if after(m, 1):
                        sp_.wait_ge(exponent_ready, m * GB)
                    sp_.dma_start(csb[:, :, :], cs_dram[bass.ts(m, GB * NH), :].partition_broadcast(128)) \
                       .then_inc(csb_loaded, 16)
                if live(r):
                    sp_.wait_ge(res_ready, r + 1)
                    sp_.dma_start(out[bass.ts(r, GB)].rearrange("b t d -> t b d"), res[:, :, :]) \
                       .then_inc(stored, 16)

            stretch(sp_, step, L_LEAD, 1, L_TAIL)
            sp_.wait_ge(stored, 16 * NG)

        @block.gpsimd
        def _(pool):
            pool.memset(eb2[:, :, :], 0.0).then_inc(poolset, 1)
            pool.memset(convb_hi[:, :], 0.0).then_inc(poolset, 1)
            pool.memset(convb_lo[:, :], 0.0).then_inc(poolset, 1)
            pool.memset(ones16[:, :], 0.0).then_inc(poolset, 1)
            pool.memset(wz_hi[:, :], 0.0).then_inc(poolset, 1)
            pool.memset(wz_lo[:, :], 0.0).then_inc(poolset, 1)
            pool.memset(ut_hi[:, :, :], 0.0).then_inc(poolset, 1)
            pool.memset(ut_lo[:, :, :], 0.0).then_inc(poolset, 1)
            pool.memset(ones[:, :], 1.0).then_inc(poolset, 1)
            pool.memset(coef[:, :], 1.0).then_inc(poolset, 1)
            pool.memset(mhalf[:, :], -0.5).then_inc(poolc, 1)
            pool.memset(euler[:, :], float(np.e)).then_inc(poolc, 1)
            pool.memset(mhalf_w[:, :], -0.5).then_inc(poolc, 1)
            pool.wait_ge(poolc, 3)
            pool.wait_ge(m2_ready, 1)
            pool.tensor_tensor(inv[:, :], m2[:, :], mhalf_w[:, :], ALU.pow).then_inc(inv_ready, 1)

            def step(k, slot):
                f, b = k, k - 1
                fs, bs = slot, (slot - 1) % 2
                if live(f):
                    pool.wait_ge(coef_ready, 1)
                    if after(f, 2):
                        pool.wait_ge(h_ps, f - 1)
                    pool.tensor_tensor(wsc[:, fs], w1c[:, None, :].to_broadcast([NK, GB, HID]),
                                       coef[:, bass.ts(f, GB), None].to_broadcast([NK, GB, HID]),
                                       ALU.mult).then_inc(wsc_ready, 1)
                if live(b):
                    pool.wait_ge(h1_ready, b + 1)
                    if after(b, 2):
                        pool.wait_ge(ssq2_ready, b - 1)
                    pool.tensor_tensor(csq[:, bs], h[:, b, :, 1, :], h[:, b, :, 1, :], ALU.mult) \
                        .then_inc(csq_ready, 1)
                    pool.wait_ge(var2_ready, b + 1)
                    if after(b, 2):
                        pool.wait_ge(u_ready, b - 1)
                    pool.tensor_tensor(rstd2[:, bs], var2[:, bs], mhalf[:, :], ALU.pow).then_inc(rstd2_ready, 1)
                if live(f):
                    pool.wait_ge(var1_ready, f + 1)
                    if after(f, 2):
                        pool.wait_ge(hn_ready, f - 1)
                    pool.tensor_tensor(rstd1[:, fs], var1[:, fs], mhalf[:, :], ALU.pow).then_inc(rstd1_ready, 1)

            stretch(pool, step, T_LEAD, 2, T_TAIL)
            pool.wait_ge(cs_ready, 1)

            def lstep(k, slot):
                m, o, f, r = k, k - 1, k - 2, k - 3
                if live(o):
                    pool.wait_ge(yg_ready, 2 * o + 2)
                    if after(o, 1):
                        pool.wait_ge(yssq_ps, o)
                    pool.tensor_tensor(ysq[:, :, :], yg[:, :, :], yg[:, :, :], ALU.mult).then_inc(ysq_ready, 1)
                if live(f):
                    pool.wait_ge(gap_ready, f + 1)
                    pool.tensor_tensor(egap[:, :], euler[:, :], gap[:, :], ALU.pow).then_inc(egap_ready, 1)
                if live(m):
                    pool.wait_ge(xs_ready, 2 * m + 2)
                    if after(m, 1):
                        pool.wait_ge(y_ps, 2 * m)
                    pool.tensor_tensor(xdt[:, :, :, :].rearrange("p b h d -> p (b h) d"),
                                       xs[:, :, :, :].rearrange("p b h d -> p (b h) d"),
                                       dt[:, bass.ts(m, GB * NH), None].to_broadcast([128, GB * NH, HD]),
                                       ALU.mult).then_inc(xdt_ready, 1)
                    pool.tensor_tensor(xd[:, :, :, :], xs[:, :, :, :],
                                       dskip[:, None, :, None].to_broadcast([128, GB, NH, HD]),
                                       ALU.mult).then_inc(xd_ready, 1)
                if live(r):
                    pool.wait_ge(prod_ready, 4 * r + 4)
                    pool.tensor_tensor(sum2[:, :], prod[:, 0:2], prod[:, 2:4], ALU.add).then_inc(tree, 1)
                    pool.wait_ge(tree, 3 * r + 1)
                    pool.tensor_tensor(sum1[:, :], sum2[:, 0], sum2[:, 1], ALU.add).then_inc(tree, 1)
                    pool.wait_ge(tree, 3 * r + 2)
                    pool.tensor_tensor(sum0[:, :], sum1[:, :, 0, :], sum1[:, :, 1, :], ALU.add).then_inc(tree, 1)
                    pool.wait_ge(tree, 3 * r + 3)
                    pool.wait_ge(hb_ready, r + 1)
                    if after(r, 1):
                        pool.wait_ge(stored, 16 * r)
                    pool.tensor_tensor(res[:, :, :], sum0[:, :, :], hb[:, :, :], ALU.add).then_inc(res_ready, 1)
                if live(o):
                    pool.wait_ge(yvar_ready, o + 1)
                    pool.tensor_tensor(yrstd[:, :], yvar[:, :], mhalf[:, :], ALU.pow).then_inc(yrstd_ready, 1)
                    pool.wait_ge(h2_ready, o + 1)
                    pool.tensor_tensor(hsq2[:, :, :], h[:, o, :, 1, :], h[:, o, :, 1, :], ALU.mult) \
                        .then_inc(hsq2_ready, 1)
                    pool.wait_ge(var3_ready, o + 1)
                    pool.tensor_tensor(rstd3[:, :], var3[:, :], mhalf[:, :], ALU.pow).then_inc(rstd3_ready, 1)

            stretch(pool, lstep, L_LEAD, 1, L_TAIL)

        @block.scalar
        def _(act):
            act.wait_ge(loaded, 16 * NSMALL)
            act.activation(aneg[:, :], aneg[:, :], ACT.Exp).then_inc(aexp, 1)

            def step(k, slot):
                f, b, c = k, k - 1, k - 2
                fs, bs = slot, (slot - 1) % 2
                if live(b):
                    act.wait_ge(hnT_ps, b + 1)
                    if after(b, 2):
                        act.wait_ge(h1_ps, b - 1)
                    act.activation(gel[:, bs, :], bank[2 + bs][:, :], ACT.Gelu, bias=beta[:, :],
                                   scale=gamma[:, :]).then_inc(gel_ready, 1)
                if live(c):
                    act.wait_ge(uT_ps, c + 1)
                    act.wait_ge(poolset, 10)
                    uT = bank[5][:, :].rearrange("p (b t) -> p b t", b=GB)
                    act.activation(ut_hi[0:D, bass.ts(c, GB), PAD:PAD + T], uT[0:D], ACT.Copy) \
                       .then_inc(uhi_ready, 1)
                    act.activation(ut_hi[D:128, bass.ts(c, GB), PAD + 1:PAD + T], uT[D:128, :, 0:T - 1], ACT.Copy) \
                       .then_inc(uhi_ready, 1)
                if live(f):
                    act.wait_ge(h_ps, f + 1)
                    if after(f, 2):
                        act.wait_ge(ssq1_ready, f - 1)
                    act.activation(hsq[:, fs].rearrange("p b c -> p (b c)"), bank[fs][:, :], ACT.Square) \
                       .then_inc(hsq_ready, 1)

            stretch(act, step, T_LEAD, 2, T_TAIL)

            act.wait_ge(sp_dve, 1)
            act.activation(sp[1][:, :], sp[1][:, :], ACT.Exp).then_inc(sp_act, 1)
            act.wait_ge(sp_dve, 2)
            act.activation(sp[0][:, :], sp[2][:, :], ACT.Ln).then_inc(sp_act, 1)

            def lstep(k, slot):
                m, o, f = k, k - 1, k - 2

                def relu(q):
                    if live(f):
                        act.wait_ge(hid_ps, NQ * f + (q + 1))
                        if q >= 4 or after(f, 1):
                            act.wait_ge(down_done, NQ * f + (q - 3))
                        act.activation(hid[:, q % 4, :], bank[4 + q % 2][:, :], ACT.Relu, bias=eb1[:, q:q + 1]) \
                           .then_inc(hid_act, 1)

                def silu_x(i):
                    act.wait_ge(x_ps, 2 * m + (i + 1))
                    if i == 0 and after(m, 1):
                        act.wait_ge(xd_ready, m)
                    act.activation(xs[:, 2 * i:2 * i + 2].rearrange("p b h d -> p (b h d)"), bank[i][:, :],
                                   ACT.Silu, scale=1.0 / WSCALE).then_inc(xs_ready, 1)

                def silu_z(i):
                    act.wait_ge(z_ps, 2 * m + (i + 1))
                    if i == 0 and after(m, 1):
                        act.wait_ge(yg_ready, 2 * m)
                    act.activation(zs[:, i, :], bank[2 + i][:, :], ACT.Silu, scale=1.0 / WSCALE) \
                       .then_inc(zs_ready, 1)

                if live(f):
                    act.wait_ge(u2T_ps, f + 1)
                    if after(f, 1):
                        act.wait_ge(hid_ps, NQ * f)
                    act.activation(u2T[:, :], bank[2][:, :], ACT.Copy).then_inc(u2hi_ready, 1)
                if live(m):
                    silu_x(0)
                    silu_x(1)
                    silu_z(0)
                relu(0)
                if live(m):
                    silu_z(1)
                relu(2)
                if live(m):
                    act.wait_ge(bc_ps, m + 1)
                    if after(m, 1):
                        act.wait_ge(g_ps, m)
                    act.activation(bT[:, :], bank[0][0:NS, :], ACT.Silu, bias=convb_bc[0:NS, :],
                                   scale=1.0 / WSCALE).then_inc(bc_ready, 1)
                    act.activation(cT[:, :], bank[0][NS:128, :], ACT.Silu, bias=convb_bc[NS:128, :],
                                   scale=1.0 / WSCALE).then_inc(bc_ready, 1)
                for b in range(GB):
                    if b:
                        relu(2 + 2 * b)
                    if live(m):
                        act.wait_ge(exponent_ready, GB * m + (b + 1))
                        act.activation(dec[:, b], dec[:, b], ACT.Exp).then_inc(decay_ready, 1)
                for q in range(10, NQ, 2):
                    relu(q)

            stretch(act, lstep, L_LEAD, 1, L_TAIL)

        @block.vector
        def _(dve):
            count = [0]

            def link(ins):
                count[0] += 1
                ins.then_inc(dvec, 1)
                dve.wait_ge(dvec, count[0])

            dve.wait_ge(loaded, 16 * NSMALL)
            dve.tensor_copy(idsf[:, :], ids[:, :]).then_inc(ids_ready, 1)
            link(dve.tensor_reduce(rowsum[0:NK, 0:1], w1x[:, :], AX.X, ALU.add))
            link(dve.tensor_scalar(rowsum[0:NK, 1:2], rowsum[0:NK, 0:1], -1.0 / HID, None, ALU.mult))
            link(dve.tensor_scalar(w1c[:, :], w1x[:, :], rowsum[0:NK, 1:2], None, ALU.add))
            dve.wait_ge(spec_ps, 1)
            link(dve.tensor_scalar(re[:, :], bank[0][0:3 * NF, 0:NSEQ], 1.0 / 127.5, dc[:, :], ALU.mult, ALU.add))
            link(dve.tensor_scalar(im[:, :], bank[0][0:3 * NF, NSEQ:2 * NSEQ], 1.0 / 127.5, None, ALU.mult))
            link(dve.tensor_tensor(m2[:, :], re[:, :], re[:, :], ALU.mult))
            link(dve.tensor_tensor(im2[:, :], im[:, :], im[:, :], ALU.mult))
            link(dve.tensor_tensor(m2[:, :], m2[:, :], im2[:, :], ALU.add))
            link(dve.tensor_scalar(zero[:, :], m2[:, :], 0.0, None, ALU.is_equal))
            link(dve.tensor_tensor(im2[:, :], m2[:, :], zero[:, :], ALU.add))
            link(dve.tensor_copy(m2[:, :], im2[:, :]))
            dve.sem_inc(m2_ready, 1)
            dve.wait_ge(inv_ready, 1)
            dve.wait_ge(poolset, 10)
            link(dve.tensor_tensor(im2[0:NF, :], m2[0:NF, :], zero[0:NF, :], ALU.subtract))
            link(dve.scalar_tensor_tensor(coef[0:NF, :], im2[0:NF, :], freq[:, :], inv[0:NF, :],
                                          ALU.mult, ALU.mult))
            link(dve.tensor_tensor(coef[NF:2 * NF, :], im[NF:2 * NF, :], inv[NF:2 * NF, :], ALU.mult))
            link(dve.tensor_tensor(re[2 * NF:, :], re[2 * NF:, :], inv[2 * NF:, :], ALU.mult))
            dve.tensor_tensor(coef[2 * NF:3 * NF, :], re[2 * NF:, :], zero[2 * NF:, :], ALU.add) \
               .then_inc(coef_ready, 1)
            for src, dst in ((w2x[:, 0, :], w2x[:, 1, :]), (b2x[:, 0, :], b2x[:, 1, :])):
                link(dve.tensor_reduce(rowsum[:, 0:1], src, AX.X, ALU.add))
                link(dve.tensor_scalar(rowsum[:, 1:2], rowsum[:, 0:1], -1.0 / D, None, ALU.mult))
                link(dve.tensor_scalar(dst, src, rowsum[:, 1:2], None, ALU.add))
            link(dve.tensor_scalar(win[:, :], win[:, :], WSCALE, None, ALU.mult))
            for a in range(2):
                link(dve.tensor_tensor(wtmp[:, :], win[:, DI:DI + NXBC], taps[:, a, :], ALU.mult))
                link(dve.tensor_copy(wc_hi[:, a, :], wtmp[:, :]))
                link(dve.tensor_tensor(wc_lo[:, a, :], wtmp[:, :], wc_hi[:, a, :], ALU.subtract))
            for d0, s0, n in ((0, 0, DI), (DI, DI + NXBC, NH)):
                link(dve.tensor_copy(wz_hi[0:D, d0:d0 + n], win[0:D, s0:s0 + n]))
                link(dve.tensor_tensor(wz_lo[0:D, d0:d0 + n], win[0:D, s0:s0 + n], wz_hi[0:D, d0:d0 + n],
                                       ALU.subtract))
            link(dve.tensor_scalar(convb_row[:, :], convb_row[:, :], WSCALE, None, ALU.mult))
            link(dve.tensor_copy(convb_hi[0:1, :], convb_row[:, :]))
            link(dve.tensor_tensor(convb_lo[0:1, :], convb_row[:, :], convb_hi[0:1, :], ALU.subtract))
            link(dve.memset(ones16[0:1, :], 1.0))
            dve.sem_inc(weights_ready, 1)

            def step(k, slot):
                f, b, c = k, k - 1, k - 2
                fs, bs, cs_ = slot, (slot - 1) % 2, slot
                if live(b):
                    dve.wait_ge(rstd1_ready, b + 1)
                    if after(b, 2):
                        dve.wait_ge(hnT_ps, b - 1)
                    dve.tensor_tensor(hn[:, bs], bank[bs][:, :].rearrange("p (b c) -> p b c", b=GB),
                                      rstd1[:, bs, :, None].to_broadcast([128, GB, HID]),
                                      ALU.mult).then_inc(hn_ready, 1)
                if live(c):
                    dve.wait_ge(rstd2_ready, c + 1)
                    if after(c, 2):
                        dve.wait_ge(uT_ps, c - 1)
                    for i in range(2):
                        ins = dve.tensor_tensor(udup[:, cs_, :, i, :], h[:, c, :, 1, :],
                                                rstd2[:, cs_, :, None].to_broadcast([128, GB, D]), ALU.mult)
                    ins.then_inc(u_ready, 1)
                    uT = bank[5][:, :].rearrange("p (b t) -> p b t", b=GB)
                    dve.wait_ge(uhi_ready, 2 * c + 1)
                    dve.tensor_tensor(ut_lo[0:D, bass.ts(c, GB), PAD:PAD + T], uT[0:D],
                                      ut_hi[0:D, bass.ts(c, GB), PAD:PAD + T], ALU.subtract) \
                       .then_inc(ulo_ready, 1)
                    dve.wait_ge(uhi_ready, 2 * c + 2)
                    dve.tensor_tensor(ut_lo[D:128, bass.ts(c, GB), PAD + 1:PAD + T], uT[D:128, :, 0:T - 1],
                                      ut_hi[D:128, bass.ts(c, GB), PAD + 1:PAD + T], ALU.subtract) \
                       .then_inc(ulo_ready, 1)
                if live(b):
                    dve.wait_ge(h1_ps, b + 1)
                    dve.tensor_tensor(h[:, b], bank[4][:, :].rearrange("p (b i d) -> p b i d", b=GB, i=2),
                                      b2x[:, None, :, :].to_broadcast([128, GB, 2, D]), ALU.add) \
                       .then_inc(h1_ready, 1)
                    dve.wait_ge(csq_ready, b + 1)
                    dve.tensor_reduce(ssq2[:, bs], csq[:, bs], AX.X, ALU.add).then_inc(ssq2_ready, 1)
                    dve.wait_ge(ssq2_ready, b + 1)
                    dve.tensor_scalar(var2[:, bs], ssq2[:, bs], 1.0 / D, LN_EPS, ALU.mult, ALU.add) \
                       .then_inc(var2_ready, 1)
                if live(c):
                    dve.wait_ge(dt_ps, c + 1)
                    dve.tensor_scalar(dt[:, bass.ts(c, GB * NH)], bank[6][:, 0:GB * NH], 1.0 / WSCALE, None,
                                      ALU.mult).then_inc(dt_copied, 1)
                if live(f):
                    dve.wait_ge(hsq_ready, f + 1)
                    dve.tensor_reduce(ssq1[:, fs], hsq[:, fs], AX.X, ALU.add).then_inc(ssq1_ready, 1)
                    dve.wait_ge(ssq1_ready, f + 1)
                    dve.tensor_scalar(var1[:, fs], ssq1[:, fs], 1.0 / HID, LN_EPS, ALU.mult, ALU.add) \
                       .then_inc(var1_ready, 1)

            stretch(dve, step, T_LEAD, 2, T_TAIL)

            dve.wait_ge(dt_copied, NG)
            dve.wait_ge(aexp, 1)
            link(dve.tensor_scalar(aneg[:, :], aneg[:, :], -1.0, None, ALU.mult))
            v = dt[:, :].rearrange("p (b h) -> p b h", h=NH)
            link(dve.tensor_tensor(v, v, dtbias[:, None, :].to_broadcast([128, NSEQ, NH]), ALU.add))
            dve.scalar_tensor_tensor(sp[1][:, :], dt[:, :], -1.0, dt[:, :], ALU.mult, ALU.min).then_inc(sp_dve, 1)
            dve.wait_ge(sp_act, 1)
            dve.tensor_scalar(sp[2][:, :], sp[1][:, :], 1.0, None, ALU.add).then_inc(sp_dve, 1)
            dve.wait_ge(sp_act, 2)
            w, e_, lnw = sp[2], sp[1], sp[0]
            link(dve.tensor_scalar(csT[:, :, :].rearrange("p a t -> p (a t)"), w[:, :], 1.0, None, ALU.is_equal))
            one = csT[:, :, :].rearrange("p a t -> p (a t)")
            link(dve.tensor_tensor(lnw[:, :], lnw[:, :], one, ALU.add))
            link(dve.tensor_tensor(lnw[:, :], lnw[:, :], e_[:, :], ALU.mult))
            link(dve.scalar_tensor_tensor(w[:, :], w[:, :], -1.0, one, ALU.add, ALU.add))
            link(dve.reciprocal(e_[:, :], w[:, :]))
            link(dve.tensor_tensor(lnw[:, :], lnw[:, :], e_[:, :], ALU.mult))
            link(dve.scalar_tensor_tensor(dt[:, :], dt[:, :], 0.0, lnw[:, :], ALU.max, ALU.add))
            link(dve.tensor_tensor(sp[1][:, :].rearrange("p (b h) -> p b h", h=NH), v,
                                   aneg[:, None, :].to_broadcast([128, NSEQ, NH]), ALU.mult))
            dve.sem_inc(sp_dve, 1)
            dve.wait_ge(cs_ps, 1)
            dve.tensor_copy(cs[:, :], bank[0][:, 0:NSEQ * NH]).then_inc(cs_ready, 1)
            dve.wait_ge(csT_ps, 1)
            dve.tensor_copy(csT[:, :, :].rearrange("p a t -> p (a t)"), bank[1][:, 0:2 * T]).then_inc(csT_ready, 1)

            dve.wait_ge(bigloaded, 16 * NBIG)
            for a in range(2):
                link(dve.tensor_scalar(wo[:, a, 0, :], wo[:, a, 0, :], normw[:, a:a + 1], None, ALU.mult))
                link(dve.tensor_reduce(rowsum[:, 0:1], wo[:, a, 0, :], AX.X, ALU.add))
                link(dve.tensor_scalar(rowsum[:, 1:2], rowsum[:, 0:1], -1.0 / D, None, ALU.mult))
                link(dve.tensor_scalar(wo[:, a, 1, :], wo[:, a, 0, :], rowsum[:, 1:2], None, ALU.add))
            for src, hi, lo in ((wg, wg_hi, wg_lo), (ew1, ew1_hi, ew1_lo)):
                link(dve.tensor_scalar(src[:, :], src[:, :], WSCALE, None, ALU.mult))
                link(dve.tensor_copy(hi[:, :], src[:, :]))
                link(dve.tensor_tensor(lo[:, :], src[:, :], hi[:, :], ALU.subtract))
            link(dve.tensor_scalar(eb1[:, :], eb1[:, :], WSCALE, None, ALU.mult))
            link(dve.tensor_scalar(ew2[:, :, :], ew2[:, :, :], 1.0 / WSCALE, None, ALU.mult))
            dve.sem_inc(weights_ready, 1)

            def lstep(k, slot):
                m, o, f = k, k - 1, k - 2

                def relu(q):
                    if live(f):
                        dve.wait_ge(hid_ps, NQ * f + (q + 1))
                        if q >= 4 or after(f, 1):
                            dve.wait_ge(down_done, NQ * f + (q - 3))
                        dve.tensor_scalar(hid[:, q % 4, :], bank[4 + q % 2][:, :], eb1[:, q:q + 1], 0.0,
                                          ALU.add, ALU.max).then_inc(hid_dve, 1)

                def weigh(p):
                    if live(f):
                        dve.wait_ge(down_done, NQ * f + (4 * p + 4))
                        if p == 0:
                            if after(f, 1):
                                dve.wait_ge(tree, 3 * f - 2)
                            dve.wait_ge(gate, 7 * f + 7)
                        dve.tensor_tensor(prod[:, p], bank[6 + p % 2][:, :].rearrange("p (b e d) -> p b e d", b=GB, e=2),
                                          comb[:, :, 2 * p:2 * p + 2, None].to_broadcast([128, GB, 2, D]),
                                          ALU.mult).then_inc(prod_ready, 1)

                def exponents(b):
                    if live(m):
                        if b == 0:
                            dve.wait_ge(csb_loaded, 16 * m + 16)
                            if after(m, 1):
                                dve.wait_ge(y_ps, 2 * m)
                        for i in range(NH):
                            col = (b * NH + i)
                            ins = dve.scalar_tensor_tensor(dec[:, b, i, :], csb[:, col, :],
                                                           cs[:, bass.ds(m * (GB * NH) + col, 1)], mask[:, :],
                                                           ALU.subtract, ALU.min)
                        ins.then_inc(exponent_ready, 1)

                def mix(b):
                    if live(m):
                        if b == 0:
                            dve.wait_ge(g_ps, m + 1)
                        dve.wait_ge(decay_ready, GB * m + (b + 1))
                        dve.tensor_tensor(dec[:, b], dec[:, b],
                                          bank[1][:, None, b * T:(b + 1) * T].to_broadcast([128, NH, T]),
                                          ALU.mult).then_inc(mix_ready, 1)

                def gate_y(i):
                    if live(m):
                        dve.wait_ge(y_ps, 2 * m + (i + 1))
                        dve.wait_ge(zs_ready, 2 * m + 2)
                        if i == 0 and after(m, 1):
                            dve.wait_ge(o_ps, m)
                        dve.tensor_tensor(yg[:, i, :], bank[2 + i][:, :], zs[:, i, :], ALU.mult) \
                           .then_inc(yg_ready, 1)

                if live(f):
                    dve.wait_ge(u2hi_ready, f + 1)
                    dve.tensor_tensor(u2T[D:128, :], bank[2][D:128, :], u2T[D:128, :], ALU.subtract) \
                       .then_inc(u2lo_ready, 1)
                exponents(0)
                if live(f):
                    dve.wait_ge(s_ps, f + 1)
                    dve.scalar_tensor_tensor(score[:, :, :], bank[3][:, 0:GB * E].rearrange("p (b e) -> p b e", b=GB),
                                             1.0 / WSCALE, bg[:, None, :].to_broadcast([128, GB, E]),
                                             ALU.mult, ALU.add).then_inc(gate, 1)
                    dve.wait_ge(gate, 7 * f + 1)
                exponents(1)
                if live(f):
                    for b in range(GB):
                        ins = dve.max(top[:, b, :], score[:, b, :])
                    ins.then_inc(gate, 1)
                    dve.wait_ge(gate, 7 * f + 2)
                    if after(f, 1):
                        dve.wait_ge(egap_ready, f)
                    dve.tensor_tensor(gap[:, :], top[:, :, 1], top[:, :, 0], ALU.subtract).then_inc(gap_ready, 1)
                    for b in range(GB):
                        ins = dve.max_index(topi[:, b, :], top[:, b, :], score[:, b, :])
                    ins.then_inc(gate, 1)
                relu(1)
                if live(f):
                    dve.wait_ge(gate, 7 * f + 3)
                    dve.tensor_copy(topf[:, :, :], topi[:, :, 0:2]).then_inc(gate, 1)
                    dve.wait_ge(egap_ready, f + 1)
                    dve.tensor_scalar(gsum[:, :], egap[:, :], 1.0, None, ALU.add).then_inc(gate_sum, 1)
                    dve.wait_ge(gate_sum, 2 * f + 1)
                    dve.reciprocal(prob[:, 0, :], gsum[:, :]).then_inc(gate_sum, 1)
                    dve.wait_ge(gate_sum, 2 * f + 2)
                    dve.tensor_tensor(prob[:, 1, :], egap[:, :], prob[:, 0, :], ALU.mult).then_inc(gate, 1)
                    dve.wait_ge(gate, 7 * f + 4)
                    for i in range(2):
                        ins = dve.tensor_tensor(pick[:, i], iota[:, None, :].to_broadcast([128, GB, E]),
                                                topf[:, :, i, None].to_broadcast([128, GB, E]), ALU.is_equal)
                    ins.then_inc(gate, 1)
                    dve.wait_ge(gate, 7 * f + 6)
                    ins = dve.tensor_tensor(pick[:, :], pick[:, :],
                                            prob[:, :, :, None].to_broadcast([128, 2, GB, E]), ALU.mult)
                    ins.then_inc(gate_mul, 1)
                    dve.wait_ge(gate_mul, f + 1)
                    if after(f, 1):
                        dve.wait_ge(prod_ready, 4 * f)
                    dve.tensor_tensor(comb[:, :, :], pick[:, 0], pick[:, 1], ALU.add).then_inc(gate, 1)
                exponents(2)
                relu(3)
                exponents(3)
                relu(5)
                if live(o):
                    dve.wait_ge(yssq_ps, o + 1)
                    dve.tensor_scalar(yvar[:, :], bank[1][:, 0:GB], 1.0 / DI, LN_EPS, ALU.mult, ALU.add) \
                       .then_inc(yvar_ready, 1)
                weigh(0)
                relu(7)
                if live(o):
                    dve.wait_ge(o_ps, o + 1)
                    dve.wait_ge(yrstd_ready, o + 1)
                    dve.tensor_tensor(hadd[:, :, :, :], bank[0][:, :].rearrange("p (b i d) -> p b i d", b=GB, i=2),
                                      yrstd[:, :, None, None].to_broadcast([128, GB, 2, D]),
                                      ALU.mult).then_inc(hadd_ready, 1)
                    dve.wait_ge(hadd_ready, o + 1)
                    dve.tensor_tensor(h[:, o], h[:, o], hadd[:, :, :, :], ALU.add).then_inc(h2_ready, 1)
                if live(f):
                    dve.wait_ge(combT_ps, f + 1)
                    dve.tensor_copy(combT[:, :], bank[1][0:GB * E, 0:T]).then_inc(combT_ready, 1)
                relu(9)
                weigh(1)
                if live(f):
                    dve.wait_ge(b2_ps, f + 1)
                    if after(f, 1):
                        dve.wait_ge(res_ready, f)
                    dve.wait_ge(h2_ready, f + 1)
                    dve.tensor_tensor(hb[:, :, :], bank[1][:, 0:GB * D].rearrange("p (b d) -> p b d", b=GB),
                                      h[:, f, :, 0, :], ALU.add).then_inc(hb_ready, 1)
                mix(0)
                relu(11)
                mix(1)
                if live(o):
                    dve.wait_ge(hsq2_ready, o + 1)
                    dve.tensor_reduce(ssq3[:, :], hsq2[:, :, :], AX.X, ALU.add).then_inc(ssq3_ready, 1)
                    dve.wait_ge(ssq3_ready, o + 1)
                    dve.tensor_scalar(var3[:, :], ssq3[:, :], 1.0 / D, LN_EPS, ALU.mult, ALU.add) \
                       .then_inc(var3_ready, 1)
                mix(2)
                relu(13)
                mix(3)
                weigh(2)
                relu(15)
                if live(o):
                    dve.wait_ge(rstd3_ready, o + 1)
                    if after(o, 1):
                        dve.wait_ge(u2T_ps, o)
                    for i in range(2):
                        ins = dve.tensor_tensor(u2[:, :, i, :], h[:, o, :, 1, :],
                                                rstd3[:, :, None].to_broadcast([128, GB, D]), ALU.mult)
                    ins.then_inc(u2_ready, 1)
                gate_y(0)
                gate_y(1)
                weigh(3)

            stretch(dve, lstep, L_LEAD, 1, L_TAIL)

        @block.tensor
        def _(pe):
            pe.wait_ge(loaded, 16 * NSMALL)
            pe.wait_ge(ids_ready, 1)
            pe.matmul(bank[0][0:3 * NF, 0:NSEQ], dft[:, 0, :], idsf[:, :], start=True, stop=True)
            pe.matmul(bank[0][0:3 * NF, NSEQ:2 * NSEQ], dft[:, 1, :], idsf[:, :], start=True, stop=True) \
              .then_inc(spec_ps, 1)
            pe.wait_ge(weights_ready, 1)

            def step(k, slot):
                f, b, c = k, k - 1, k - 2
                fs, bs, cs_ = slot, (slot - 1) % 2, slot
                if live(b):
                    pe.wait_ge(hn_ready, b + 1)
                    if after(b, 2):
                        pe.wait_ge(gel_ready, b - 1)
                    for j in range(GB):
                        ins = pe.transpose(bank[2 + bs][:, j * T:(j + 1) * T], hn[:, bs, j, :], ident[:, :])
                    ins.then_inc(hnT_ps, 1)
                if live(c):
                    pe.wait_ge(u_ready, c + 1)
                    if after(c, 1):
                        pe.wait_ge(ulo_ready, 2 * c)
                    for j in range(GB):
                        ins = pe.transpose(bank[5][:, j * T:(j + 1) * T],
                                           udup[:, cs_, j].rearrange("p i d -> p (i d)"), ident[:, :])
                    ins.then_inc(uT_ps, 1)
                if live(b):
                    pe.wait_ge(gel_ready, b + 1)
                    if after(b, 1):
                        pe.wait_ge(h1_ready, b)
                    for j in range(GB):
                        ins = pe.matmul(bank[4][:, j * 2 * D:(j + 1) * 2 * D], gel[:, bs, j * T:(j + 1) * T],
                                        w2x[:, :, :].rearrange("p i d -> p (i d)"), start=True, stop=True)
                    ins.then_inc(h1_ps, 1)
                if live(c):
                    pe.wait_ge(ulo_ready, 2 * c + 2)
                    if after(c, 1):
                        pe.wait_ge(dt_copied, c)
                    for j in range(GB):
                        for n, (u, w_) in enumerate(((ut_hi, wz_hi), (ut_lo, wz_hi), (ut_hi, wz_lo))):
                            ins = pe.matmul(bank[6][:, j * NH:(j + 1) * NH], u[:, c * GB + j, PAD:PAD + T],
                                            w_[:, DI:DI + NH], start=(n == 0), stop=(n == 2))
                    ins.then_inc(dt_ps, 1)
                if live(f):
                    pe.wait_ge(wsc_ready, f + 1)
                    if after(f, 2):
                        pe.wait_ge(hn_ready, f - 1)
                        pe.wait_ge(hsq_ready, f - 1)
                    pe.matmul(bank[fs][:, :], shift[:, :], wsc[:, fs].rearrange("p b c -> p (b c)"),
                              start=True, stop=True).then_inc(h_ps, 1)

            stretch(pe, step, T_LEAD, 2, T_TAIL)

            pe.wait_ge(sp_dve, 3)
            pe.matmul(bank[0][:, 0:NSEQ * NH], upto[:, :], sp[1][:, :], start=True, stop=True).then_inc(cs_ps, 1)
            pe.wait_ge(cs_ready, 1)
            for a in range(2):
                ins = pe.transpose(bank[1][:, a * T:(a + 1) * T], cs[:, a * 128:(a + 1) * 128], ident[:, :])
            ins.then_inc(csT_ps, 1)
            pe.wait_ge(csT_ready, 1)
            pe.wait_ge(weights_ready, 2)

            def lstep(k, slot):
                m, o, f = k, k - 1, k - 2

                def project_x(i):
                    if i == 0 and after(m, 2):
                        pe.wait_ge(hadd_ready, m - 1)
                    elif i == 0 and after(m, 1):
                        pe.wait_ge(bc_ready, 2 * m)
                    if i == 1 and after(m, 1):
                        pe.wait_ge(mix_ready, GB * m)
                    for n, bias in enumerate((convb_hi, convb_lo)):
                        pe.matmul(bank[i][:, :], ones16[:, :], bias[:, None, :].to_broadcast([128, 2, DI]),
                                  start=(n == 0), stop=False, skip_group_check=True)
                    for j in range(2):
                        seq = m * GB + (2 * i + j)
                        for a, c0 in ((0, PAD), (1, PAD - 2)):
                            for u, w_ in ((ut_hi, wc_hi), (ut_hi, wc_lo), (ut_lo, wc_hi)):
                                ins = pe.matmul(bank[i][:, j * DI:(j + 1) * DI], u[:, seq, c0:c0 + T],
                                                w_[:, a, 0:DI], start=False,
                                                stop=(a == 1 and u is ut_lo), skip_group_check=True)
                    ins.then_inc(x_ps, 1)

                def project_z(i):
                    for n, (u, w_) in enumerate(((ut_hi, wz_hi), (ut_lo, wz_hi), (ut_hi, wz_lo))):
                        ins = pe.matmul(bank[2 + i][:, :], w_[:, i * 128:(i + 1) * 128],
                                        u[:, bass.ts(m, GB), PAD:PAD + T], start=(n == 0), stop=(n == 2))
                    ins.then_inc(z_ps, 1)

                def project_bc():
                    pe.wait_ge(xs_ready, 2 * m + 1)
                    n = 0
                    for a, c0 in ((0, PAD), (1, PAD - 2)):
                        for u, w_ in ((ut_hi, wc_hi), (ut_lo, wc_hi), (ut_hi, wc_lo)):
                            ins = pe.matmul(bank[0][:, :], w_[:, a, DI:NXBC], u[:, bass.ts(m, GB), c0:c0 + T],
                                            start=(n == 0), stop=(n == 5))
                            n += 1
                    ins.then_inc(bc_ps, 1)

                def up(q):
                    if q == 0:
                        pe.wait_ge(u2lo_ready, f + 1)
                    if q >= 2 or after(f, 1):
                        done = hid_act if q % 2 == 0 else hid_dve
                        pe.wait_ge(done, (NQ // 2) * f + q // 2)
                    for n, w_ in enumerate((ew1_hi, ew1_lo)):
                        ins = pe.matmul(bank[4 + q % 2][:, :], w_[:, q * 128:(q + 1) * 128], u2T[:, :],
                                        start=(n == 0), stop=(n == 1))
                    ins.then_inc(hid_ps, 1)

                def down(q):
                    e, j = q // 2, q % 2
                    p = e // 2
                    done = hid_act if q % 2 == 0 else hid_dve
                    pe.wait_ge(done, (NQ // 2) * f + (q // 2 + 1))
                    if q % 4 == 0 and (p >= 2 or after(f, 1)):
                        pe.wait_ge(prod_ready, 4 * f + (p - 1))
                    for b in range(GB):
                        c0 = (b * 2 + e % 2) * D
                        ins = pe.matmul(bank[6 + p % 2][:, c0:c0 + D], hid[:, q % 4, b * T:(b + 1) * T],
                                        ew2[:, q, :], start=(q % 4 == 0 and b == 0), stop=(j == 1),
                                        skip_group_check=True)
                    ins.then_inc(down_done, 1)

                if live(f):
                    pe.wait_ge(u2_ready, f + 1)
                    if live(o):
                        pe.wait_ge(yg_ready, 2 * o + 2)
                    elif after(f, 1):
                        pe.wait_ge(u2lo_ready, f)
                    for j in range(GB):
                        ins = pe.transpose(bank[2][:, j * T:(j + 1) * T], u2[:, j].rearrange("p i d -> p (i d)"),
                                           ident[:, :])
                    ins.then_inc(u2T_ps, 1)
                if live(m):
                    project_x(0)
                    project_x(1)
                if live(f):
                    pe.wait_ge(u2lo_ready, f + 1)
                    if after(f, 1):
                        pe.wait_ge(gate, 7 * f - 6)
                    for j in range(GB):
                        for n, w_ in enumerate((wg_hi, wg_lo)):
                            ins = pe.matmul(bank[3][:, j * E:(j + 1) * E], u2T[:, j * T:(j + 1) * T], w_[:, :],
                                            start=(n == 0), stop=(n == 1))
                    ins.then_inc(s_ps, 1)
                if live(m):
                    if live(f):
                        pe.wait_ge(u2lo_ready, f + 1)
                    elif after(m, 1):
                        pe.wait_ge(yg_ready, 2 * m)
                    project_z(0)
                for q in range(NQ):
                    if live(f):
                        up(q)
                        if q >= 2:
                            down(q - 2)
                    if q == 1 and live(m):
                        if live(f):
                            pe.wait_ge(gate, 7 * f + 1)
                        elif after(m, 1):
                            pe.wait_ge(yg_ready, 2 * m)
                        project_z(1)
                    if q == 3 and live(m):
                        project_bc()
                    if q == 4 and live(o):
                        pe.wait_ge(ysq_ready, o + 1)
                        if live(m):
                            pe.wait_ge(xs_ready, 2 * m + 2)
                        for j in range(GB):
                            for i in range(2):
                                ins = pe.matmul(bank[1][:, j:j + 1], ysq[:, i, j * T:(j + 1) * T], ones[:, :],
                                                start=(i == 0), stop=(i == 1))
                        ins.then_inc(yssq_ps, 1)
                    if q == 5 and live(o):
                        if live(m):
                            pe.wait_ge(bc_ready, 2 * m + 2)
                        elif after(o, 1):
                            pe.wait_ge(hadd_ready, o)
                        for j in range(GB):
                            for i in range(2):
                                ins = pe.matmul(bank[0][:, j * 2 * D:(j + 1) * 2 * D], yg[:, i, j * T:(j + 1) * T],
                                                wo[:, i].rearrange("p i d -> p (i d)"), start=(i == 0), stop=(i == 1))
                        ins.then_inc(o_ps, 1)
                    if q == 7 and live(f):
                        pe.wait_ge(gate, 7 * f + 7)
                        if live(o):
                            pe.wait_ge(yvar_ready, o + 1)
                        elif after(f, 1):
                            pe.wait_ge(hb_ready, f)
                        pe.transpose(bank[1][0:GB * E, 0:T], comb[:, :, :].rearrange("p b e -> p (b e)"),
                                     ident[:, :]).then_inc(combT_ps, 1)
                    if q == 9 and live(f):
                        pe.wait_ge(combT_ready, f + 1)
                        pe.matmul(bank[1][:, 0:GB * D], combT[:, :], eb2[:, :, :].rearrange("p b d -> p (b d)"),
                                  start=True, stop=True).then_inc(b2_ps, 1)
                    if q == 10 and live(m):
                        pe.wait_ge(bc_ready, 2 * m + 2)
                        if live(f):
                            pe.wait_ge(hb_ready, f + 1)
                        elif live(o):
                            pe.wait_ge(yvar_ready, o + 1)
                        for j in range(GB):
                            ins = pe.matmul(bank[1][:, j * T:(j + 1) * T], bT[:, j * T:(j + 1) * T],
                                            cT[:, j * T:(j + 1) * T], start=True, stop=True)
                        ins.then_inc(g_ps, 1)
                if live(f):
                    down(NQ - 2)
                    down(NQ - 1)
                if live(m):
                    pe.wait_ge(mix_ready, GB * m + GB)
                    pe.wait_ge(xdt_ready, m + 1)
                    pe.wait_ge(xd_ready, m + 1)
                    pe.wait_ge(zs_ready, 2 * m + 2)
                    for i in range(2):
                        for j in range(GB):
                            pe.matmul(bank[2 + i][:, j * T:(j + 1) * T],
                                      xd[:, j, 2 * i:2 * i + 2, :].rearrange("p h d -> p (h d)"), ident[:, :],
                                      start=(j == 0), stop=False, skip_group_check=True)
                            for hh in range(2):
                                ins = pe.matmul(bank[2 + i][hh * HD:(hh + 1) * HD, j * T:(j + 1) * T],
                                                xdt[:, j, 2 * i + hh, :], dec[:, j, 2 * i + hh, :],
                                                start=False, stop=True, skip_group_check=True)
                        ins.then_inc(y_ps, 1)

            stretch(pe, lstep, L_LEAD, 1, L_TAIL)


CONSTS = constants()


def kernel(**a):
    from concourse import bacc
    from concourse.bass_utils import run_bass_kernel_spmd

    def lay(x):
        return np.ascontiguousarray(np.asarray(x))

    arrays = {
        "ids": lay(np.asarray(a["x"]).T),
        "freq": lay(a["L0_tok_freq_bands"]), "tw1": lay(a["L0_tok_w1"]), "tb1": lay(a["L0_tok_b1"]),
        "gamma": lay(a["L0_tok_gamma"]), "beta": lay(a["L0_tok_beta"]),
        "tw2": lay(a["L0_tok_w2"]), "tb2": lay(a["L0_tok_b2"]),
        "winT": lay(np.asarray(a["L0_attn_in_proj_w"]).T),
        "convT": lay(np.asarray(a["L0_attn_conv_w"])[:, 0, :].T), "convb": lay(a["L0_attn_conv_b"]),
        "dtbias": lay(a["L0_attn_dt_bias"]), "alog": lay(a["L0_attn_A_log"]), "dskip": lay(a["L0_attn_D"]),
        "normw": lay(a["L0_attn_norm_w"]), "woT": lay(np.asarray(a["L0_attn_out_proj_w"]).T),
        "wgT": lay(np.asarray(a["L0_ffn_Wg"]).T), "bg": lay(a["L0_ffn_bg"]),
        "ew1T": lay(np.asarray(a["L0_ffn_W1"]).transpose(2, 0, 1).reshape(D, E * EH)),
        "eb1": lay(a["L0_ffn_b1"]),
        "ew2T": lay(np.asarray(a["L0_ffn_W2"]).transpose(0, 2, 1).reshape(E * EH, D)),
        "eb2": lay(a["L0_ffn_b2"]),
        **CONSTS,
    }
    nc = bacc.Bacc("TRN2", target_bir_lowering=False, num_devices=1)
    inp = {n: nc.dram_tensor(f"in_{n}", list(x.shape), mybir.dt.from_np(x.dtype), kind="ExternalInput").ap()
           for n, x in arrays.items()}
    out = nc.dram_tensor("out_tower", [NSEQ, T, D], F32, kind="ExternalOutput").ap()
    build(nc, inp, out)
    r = run_bass_kernel_spmd(nc, [{f"in_{n}": x for n, x in arrays.items()}], core_ids=[0])
    return r.results[0]["out_tower"]
```

```python
from contextlib import ExitStack

import numpy as np
import concourse.bass as bass
from concourse import mybir

F32 = mybir.dt.float32
F16 = mybir.dt.float16
I32 = mybir.dt.int32
U32 = mybir.dt.uint32
ALU = mybir.AluOpType
ACT = mybir.ActivationFunctionType
AX = mybir.AxisListType

NSEQ, T = 64, 128
D, HID = 64, 128
NF = 32
DI, NH, HD, NS, KW = 256, 4, 64, 64, 4
NXBC = DI + 2 * NS
E, EH = 8, 256
GB = 4
NG = NSEQ // GB
GT = GB * T
NK = 3 * NF + 1
PAD = 3
SW = PAD + T + 1
NQ = 2 * E
LN_EPS = 1e-5
WSCALE = 256.0
MASKED = -1e30
LOW = 32
NP = E // 2


def constants():
    t = np.arange(T, dtype=np.float64)
    f = np.arange(NF, dtype=np.float64)
    ang = 2 * np.pi / T * ((t[:, None] * f[None, :]) % T)
    cos, sin = np.cos(ang), np.sin(ang)
    dft = np.zeros((T, 2, 3 * NF), np.float32)
    dft[:, 0] = np.tile(cos, (1, 3))
    dft[:, 1] = np.tile(-sin, (1, 3))
    shift = np.ones((NK, T), np.float32)
    shift[NF:2 * NF] = cos.T
    shift[2 * NF:3 * NF] = sin.T
    dc = np.zeros((3 * NF, 1), np.float32)
    dc[::NF] = -float(T)
    s = np.arange(T)
    upto = (s[:, None] <= s[None, :])
    select = np.zeros((2 * LOW, E // 2, 128), np.float16)
    for e in range(E):
        for row in (e, LOW + e):
            select[row, e // 2, (e % 2) * D:(e % 2 + 1) * D] = 1.0
    return {
        "dft": dft.reshape(T, -1), "shift": shift, "dc": dc,
        "upto": upto.astype(np.float32),
        "mask": np.where(upto, 0.0, MASKED).astype(np.float32),
        "ident": np.eye(128, dtype=np.float32),
        "pairs": np.concatenate([np.eye(D, dtype=np.float32)] * 2),
        "select": select,
        "iota": np.tile(np.arange(E, dtype=np.float32), (128, 1)),
    }


def build(nc, inp, out):
    with ExitStack() as ctx:
        def sb(name, shape, dt=F32):
            return ctx.enter_context(nc.sbuf_tensor(name, shape, dt))

        def sem(name):
            return ctx.enter_context(nc.semaphore(name))

        bank = [ctx.enter_context(nc.psum_tensor(f"bank{i}", [128, 512], F32)) for i in range(8)]

        ident = sb("ident", [128, 128])
        mask = sb("mask", [128, T])
        upto = sb("upto", [128, T])
        iota = sb("iota", [128, E])
        dft = sb("dft_sb", [128, 2, 3 * NF])
        shift = sb("shift_sb", [NK, T])
        dc = sb("dc_sb", [3 * NF, 1])
        ids = sb("ids", [128, NSEQ], I32)
        idsf = sb("idsf", [128, NSEQ])
        freq = sb("freq", [NF, 1])
        w1x = sb("w1x", [NK, HID])
        w1c = sb("w1c", [NK, HID])
        gamma = sb("gamma", [HID, 1])
        beta = sb("beta", [HID, 1])
        w2x = sb("w2x", [HID, 2, D])
        b2x = sb("b2x", [128, 2, D])
        wc_hi = sb("wc_hi", [128, 2, NXBC], F16)
        wc_lo = sb("wc_lo", [128, 2, NXBC], F16)
        wz_hi = sb("wz_hi", [128, DI + NH], F16)
        wz_lo = sb("wz_lo", [128, DI + NH], F16)
        convb_row = sb("convb_row", [1, DI])
        convb16 = sb("convb16", [128, DI], F16)
        convb_bc = sb("convb_bc", [128, 1])
        ones16 = sb("ones16", [128, 128], F16)
        ones = sb("ones_col", [128, 1])
        dtbias = sb("dtbias", [128, NH])
        aneg = sb("aneg", [128, NH])
        dskip = sb("dskip", [128, NH])
        normw = sb("normw", [128, 2])
        wo = sb("wo", [128, 2, 2, D])
        wg = sb("wg", [128, E])
        wg_hi = sb("wg_hi", [128, E], F16)
        wg_lo = sb("wg_lo", [128, E], F16)
        bg = sb("bg", [128, E])
        ew1_hi = sb("ew1_hi", [128, E * EH], F16)
        ew1_lo = sb("ew1_lo", [128, E * EH], F16)
        eb1 = sb("eb1", [128, NQ])
        ew2 = sb("ew2", [128, NQ, D])
        eb2 = sb("eb2", [128, NP])
        pairs = sb("pairs_sb", [128, D])
        select = sb("select_sb", [2 * LOW, NP, 128], F16)
        mhalf = sb("mhalf", [128, GB])
        euler = sb("euler", [128, GB])
        rowsum = sb("rowsum", [128, 8])

        re = sb("re", [3 * NF, NSEQ])
        im = sb("im", [3 * NF, NSEQ])
        m2 = sb("m2", [3 * NF, NSEQ])
        im2 = sb("im2", [3 * NF, NSEQ])
        zero = sb("zero", [3 * NF, NSEQ])
        mhalf_w = sb("mhalf_w", [3 * NF, NSEQ])
        inv = sb("inv", [3 * NF, NSEQ])
        coef = sb("coef", [NK, NSEQ])

        h = sb("h", [128, NG, GB, 2, D])
        ut_hi = sb("ut_hi", [128, NSEQ, SW], F16)
        ut_lo = sb("ut_lo", [128, NSEQ, SW], F16)
        dt = sb("dt", [128, NSEQ * NH])
        cs = sb("cs", [128, NSEQ * NH])

        wsc = sb("wsc", [NK, 2, GB, HID])
        hsq = sb("hsq", [128, 2, GB, HID])
        ssq1 = sb("ssq1", [128, 2, GB])
        var1 = sb("var1", [128, 2, GB])
        rstd1 = sb("rstd1", [128, 2, GB])
        hn = sb("hn", [128, 2, GB, HID])
        gel = sb("gel", [HID, 2, GT])
        csq = sb("csq", [128, 2, GB, D])
        ssq2 = sb("ssq2", [128, 2, GB])
        var2 = sb("var2", [128, 2, GB])
        rstd2 = sb("rstd2", [128, 2, GB])
        udup = sb("udup", [128, 2, GB, 2, D])

        csT = sb("csT", [128, 2, T])
        cs_dram = nc.dram_tensor("cs_dram", [NSEQ * NH, T], F32).ap()

        csb = sb("csb", [128, GB * NH, T])
        dec = sb("dec", [128, GB, NH, T])
        xs = sb("xs", [128, GB, NH, HD])
        xdt = sb("xdt", [128, GB, NH, HD])
        xd = sb("xd", [128, GB, NH, HD])
        zs = sb("zs", [128, 2, GT])
        bT = sb("bT", [NS, GT])
        cT = sb("cT", [NS, GT])
        yg = sb("yg", [128, 2, GT])
        ysq = sb("ysq", [128, 2, GT])
        ysum = sb("ysum", [128, GT])
        yvar = sb("yvar", [128, GB])
        yrstd = sb("yrstd", [128, GB])
        hadd = sb("hadd", [128, GB, 2, D])
        hsq2 = sb("hsq2", [128, GB, D])
        ssq3 = sb("ssq3", [128, GB])
        var3 = sb("var3", [128, GB])
        rstd3 = sb("rstd3", [128, GB])
        u2 = sb("u2", [128, GB, 2, D])
        u2T = sb("u2T", [128, GT], F16)
        score = sb("score", [128, GB, E])
        top = sb("top", [128, GB, 8])
        topi = sb("topi", [128, GB, 8], U32)
        topf = sb("topf", [128, GB, 2])
        gap = sb("gap", [128, GB])
        egap = sb("egap", [128, GB])
        gsum = sb("gsum", [128, GB])
        prob = sb("prob", [128, 2, GB])
        pick = sb("pick", [128, 2, GB, E])
        comb = sb("comb", [128, GB, E])
        combT = sb("combT", [2 * LOW, GT], F16)
        share = sb("share", [128, NP, GT])
        hid = sb("hid", [128, 4, GT])
        prod = sb("prod", [128, NP, GT])
        acc = sb("acc", [128, GT])
        res = sb("res", [128, GB, D])

        ew1 = dec[:, :, :, :].rearrange("p b h t -> p (b h t)")
        win = csb[:, :, :].rearrange("p a t -> p (a t)")[:, 0:2 * DI + 2 * NS + NH]
        prod_flat = prod[:, :, :].rearrange("p a t -> p (a t)")
        taps = prod_flat[:, 0:2 * NXBC].rearrange("p (a c) -> p a c", a=2)
        wtmp = prod_flat[:, 2 * NXBC:3 * NXBC]
        xdt_flat = xdt[:, :, :, :].rearrange("p b h d -> p (b h d)")
        sp = [xdt_flat[:, i * NSEQ * NH:(i + 1) * NSEQ * NH] for i in range(3)]

        ids_loaded = sem("ids_loaded")
        loaded = sem("loaded")
        bigloaded = sem("bigloaded")
        poolset = sem("poolset")
        utset = sem("utset")
        poolc = sem("poolc")
        dvec = sem("dvec")
        tok_weights = sem("tok_weights")
        dt_weights = sem("dt_weights")
        mix_weights = sem("mix_weights")
        scaled = sem("scaled")
        expert_weights = sem("expert_weights")
        spec_ps = sem("spec_ps")
        m2_ready = sem("m2_ready")
        inv_ready = sem("inv_ready")
        coef_ready = sem("coef_ready")
        ids_ready = sem("ids_ready")
        bias_rows = sem("bias_rows")
        aexp = sem("aexp")
        wsc_ready = sem("wsc_ready")
        h_ps = sem("h_ps")
        hsq_ready = sem("hsq_ready")
        ssq1_ready = sem("ssq1_ready")
        var1_ready = sem("var1_ready")
        rstd1_ready = sem("rstd1_ready")
        hn_ready = sem("hn_ready")
        hnT_ps = sem("hnT_ps")
        gel_ready = sem("gel_ready")
        h1_ps = sem("h1_ps")
        h1_ready = sem("h1_ready")
        csq_ready = sem("csq_ready")
        ssq2_ready = sem("ssq2_ready")
        var2_ready = sem("var2_ready")
        rstd2_ready = sem("rstd2_ready")
        u_ready = sem("u_ready")
        uT_ps = sem("uT_ps")
        uhi_ready = sem("uhi_ready")
        ulo_ready = sem("ulo_ready")
        dt_ps = sem("dt_ps")
        dt_copied = sem("dt_copied")
        sp_dve = sem("sp_dve")
        sp_act = sem("sp_act")
        cs_ps = sem("cs_ps")
        cs_ready = sem("cs_ready")
        csT_ps = sem("csT_ps")
        csT_ready = sem("csT_ready")
        cs_saved = sem("cs_saved")
        csb_loaded = sem("csb_loaded")
        exponent_ready = sem("exponent_ready")
        decay_ready = sem("decay_ready")
        x_ps = sem("x_ps")
        xs_ready = sem("xs_ready")
        z_ps = sem("z_ps")
        zs_ready = sem("zs_ready")
        bc_ps = sem("bc_ps")
        bc_ready = sem("bc_ready")
        xdt_ready = sem("xdt_ready")
        xd_ready = sem("xd_ready")
        g_ps = sem("g_ps")
        mix_ready = sem("mix_ready")
        y_ps = sem("y_ps")
        yg_ready = sem("yg_ready")
        ysq_ready = sem("ysq_ready")
        ysum_ready = sem("ysum_ready")
        yssq_ps = sem("yssq_ps")
        yvar_ready = sem("yvar_ready")
        yrstd_ready = sem("yrstd_ready")
        o_ps = sem("o_ps")
        hadd_ready = sem("hadd_ready")
        h2_ready = sem("h2_ready")
        hsq2_ready = sem("hsq2_ready")
        ssq3_ready = sem("ssq3_ready")
        var3_ready = sem("var3_ready")
        rstd3_ready = sem("rstd3_ready")
        u2_ready = sem("u2_ready")
        u2T_ps = sem("u2T_ps")
        u2hi_ready = sem("u2hi_ready")
        u2lo_ready = sem("u2lo_ready")
        s_ps = sem("s_ps")
        gate = sem("gate")
        gate_sum = sem("gate_sum")
        gate_mul = sem("gate_mul")
        gap_ready = sem("gap_ready")
        egap_ready = sem("egap_ready")
        combT_ps = sem("combT_ps")
        combT_hi = sem("combT_hi")
        combT_lo = sem("combT_lo")
        share_ps = sem("share_ps")
        share_ready = sem("share_ready")
        hid_ps = sem("hid_ps")
        hid_act = sem("hid_act")
        hid_dve = sem("hid_dve")
        down_done = sem("down_done")
        prod_ready = sem("prod_ready")
        acc_sum = sem("acc_sum")
        out_ps = sem("out_ps")
        res_ready = sem("res_ready")
        stored = sem("stored")

        block = ctx.enter_context(nc.Block())

        ids_loads = [
            (ids[:, :], inp["ids"]), (dft[:, :, :].rearrange("p a b -> p (a b)"), inp["dft"]),
            (dc[:, :], inp["dc"]), (freq[:, :], inp["freq"].rearrange("(p a) -> p a", a=1)),
            (w1x[0:2 * NF, :], inp["tw1"]), (w1x[2 * NF:3 * NF, :], inp["tw1"][NF:2 * NF, :]),
            (w1x[3 * NF:NK, :], inp["tb1"].rearrange("(a p) -> a p", a=1)),
        ]
        small_loads = [
            (shift[:, :], inp["shift"]), (ident[:, :], inp["ident"]),
            (w2x[:, 0, :], inp["tw2"]), (b2x[:, 0, :], inp["tb2"].partition_broadcast(128)),
            (gamma[:, :], inp["gamma"].rearrange("(p a) -> p a", a=1)),
            (beta[:, :], inp["beta"].rearrange("(p a) -> p a", a=1)),
            (win[0:D, :], inp["winT"]), (win[D:128, :], inp["winT"]),
            (taps[0:D, 0, :], inp["convT"][3].partition_broadcast(D)),
            (taps[D:128, 0, :], inp["convT"][2].partition_broadcast(D)),
            (taps[0:D, 1, :], inp["convT"][1].partition_broadcast(D)),
            (taps[D:128, 1, :], inp["convT"][0].partition_broadcast(D)),
            (convb_row[:, :], inp["convb"][0:DI].rearrange("(a c) -> a c", a=1)),
        ]
        big_loads = [
            (convb_bc[:, :], inp["convb"][DI:NXBC].rearrange("(p a) -> p a", a=1)),
            (dtbias[:, :], inp["dtbias"].partition_broadcast(128)),
            (aneg[:, :], inp["alog"].partition_broadcast(128)),
            (dskip[:, :], inp["dskip"].partition_broadcast(128)),
            (mask[:, :], inp["mask"]), (upto[:, :], inp["upto"]), (iota[:, :], inp["iota"]),
            (pairs[:, :], inp["pairs"]), (select[:, :, :], inp["select"]),
            (normw[:, :], inp["normw"].rearrange("(a p) -> p a", a=2)),
            (wo[:, 0, 0, :], inp["woT"][0:128, :]), (wo[:, 1, 0, :], inp["woT"][128:256, :]),
            (wg[0:D, :], inp["wgT"]), (wg[D:128, :], inp["wgT"]),
            (bg[:, :], inp["bg"].partition_broadcast(128)),
            (ew1[0:D, :], inp["ew1T"]), (ew1[D:128, :], inp["ew1T"]),
            (eb1[:, :], inp["eb1"].rearrange("e (j p) -> p (e j)", j=2)),
            (ew2[:, :, :], inp["ew2T"].rearrange("(q p) d -> p q d", p=128)),
            (eb2[:, :], inp["eb2"].rearrange("(p e) d -> (e d) p", e=2)),
        ]

        NIDS, NSMALL, NBIG = len(ids_loads), len(small_loads), len(big_loads)
        SHARE_BANK = [1, 3, 2, 3]

        def half(q):
            return 2 * (2 * (q // 4) + q % 2) + (q % 4) // 2

        def live(g):
            return not isinstance(g, int) or 0 <= g < NG

        def at(k, n):
            return isinstance(k, int) and k == n

        def after(g, n):
            return not isinstance(g, int) or g >= n

        def stretch(eng, step, lead, unroll, tail):
            for k in range(lead):
                step(k, k % unroll)
            with eng.Fori(0, (NG - lead) // unroll) as i:
                for s in range(unroll):
                    step(i * unroll + (lead + s), (lead + s) % unroll)
            for k in range(NG, NG + tail):
                step(k, k % unroll)

        T_LEAD, T_TAIL = 6, 5
        L_LEAD, L_TAIL = 4, 3

        @block.sync
        def _(sp_):
            for dst, src in ids_loads:
                sp_.dma_start(dst, src, allow_slow_non_contiguous=True).then_inc(ids_loaded, 16)
            for dst, src in small_loads:
                sp_.dma_start(dst, src, allow_slow_non_contiguous=True).then_inc(loaded, 16)

            sp_.wait_ge(csT_ready, 1)
            sp_.dma_start(cs_dram.rearrange("(a p) t -> p a t", a=2), csT[:, :, :]).then_inc(cs_saved, 16)
            sp_.wait_ge(cs_saved, 16)

            def step(k, slot):
                m, r = k, k - 3
                if live(m):
                    if after(m, 1):
                        sp_.wait_ge(exponent_ready, m * GB)
                    sp_.dma_start(csb[:, :, :], cs_dram[bass.ts(m, GB * NH), :].partition_broadcast(128)) \
                       .then_inc(csb_loaded, 16)
                if live(r):
                    sp_.wait_ge(res_ready, r + 1)
                    sp_.dma_start(out[bass.ts(r, GB)].rearrange("b t d -> t b d"), res[:, :, :]) \
                       .then_inc(stored, 16)

            stretch(sp_, step, L_LEAD, 1, L_TAIL)
            sp_.wait_ge(stored, 16 * NG)

        @block.gpsimd
        def _(pool):
            pool.memset(mhalf_w[:, :], -0.5).then_inc(poolc, 1)
            pool.memset(coef[:, :], 1.0).then_inc(poolset, 1)
            pool.memset(mhalf[:, :], -0.5).then_inc(poolc, 1)
            pool.memset(wz_hi[:, :], 0.0).then_inc(poolset, 1)
            pool.memset(wz_lo[:, :], 0.0).then_inc(poolset, 1)
            pool.memset(ut_hi[:, :, :], 0.0).then_inc(utset, 1)
            pool.wait_ge(m2_ready, 1)
            pool.wait_ge(poolc, 2)
            pool.tensor_tensor(inv[:, :], m2[:, :], mhalf_w[:, :], ALU.pow).then_inc(inv_ready, 1)
            pool.memset(convb16[:, :], 0.0).then_inc(poolset, 1)
            pool.memset(ones16[:, :], 0.0).then_inc(poolset, 1)

            def step(k, slot):
                w, f, c = k, k - 1, k - 3
                ws, fs, cs_ = slot, (slot - 1) % 2, (slot - 1) % 2
                if live(w):
                    pool.wait_ge(coef_ready, 1)
                    if after(w, 2):
                        pool.wait_ge(h_ps, w - 1)
                    pool.tensor_tensor(wsc[:, ws], w1c[:, None, :].to_broadcast([NK, GB, HID]),
                                       coef[:, bass.ts(w, GB), None].to_broadcast([NK, GB, HID]),
                                       ALU.mult).then_inc(wsc_ready, 1)
                if at(k, 0):
                    pool.memset(ut_lo[:, :, :], 0.0).then_inc(utset, 1)
                if live(f):
                    pool.wait_ge(var1_ready, f + 1)
                    if after(f, 2):
                        pool.wait_ge(hn_ready, f - 1)
                    pool.tensor_tensor(rstd1[:, fs], var1[:, fs], mhalf[:, :], ALU.pow).then_inc(rstd1_ready, 1)
                if live(c):
                    pool.wait_ge(h1_ready, c + 1)
                    if after(c, 2):
                        pool.wait_ge(ssq2_ready, c - 1)
                    pool.tensor_tensor(csq[:, cs_], h[:, c, :, 1, :], h[:, c, :, 1, :], ALU.mult) \
                        .then_inc(csq_ready, 1)
                if live(c):
                    pool.wait_ge(var2_ready, c + 1)
                    if after(c, 2):
                        pool.wait_ge(u_ready, c - 1)
                    pool.tensor_tensor(rstd2[:, cs_], var2[:, cs_], mhalf[:, :], ALU.pow).then_inc(rstd2_ready, 1)
                if at(k, 3):
                    pool.memset(ones[:, :], 1.0).then_inc(poolset, 1)
                    pool.memset(euler[:, :], float(np.e)).then_inc(poolc, 1)
                    pool.memset(combT[:, :], 0.0).then_inc(poolset, 1)
                    pool.wait_ge(scaled, 2)
                    pool.tensor_tensor(ew1_lo[:, :], ew1[:, :], ew1_hi[:, :], ALU.subtract) \
                        .then_inc(expert_weights, 1)

            stretch(pool, step, T_LEAD, 2, T_TAIL)
            pool.wait_ge(cs_ready, 1)

            def lstep(k, slot):
                m, o, f, r = k, k - 1, k - 2, k - 3
                if live(r):
                    pool.wait_ge(prod_ready, NP * r + NP)
                    pool.wait_ge(acc_sum, (NP - 1) * r + (NP - 2))
                    if after(r, 1):
                        pool.wait_ge(out_ps, r)
                    pool.tensor_tensor(acc[:, :], prod[:, 0, :], prod[:, NP - 1, :], ALU.add).then_inc(acc_sum, 1)
                if live(o):
                    pool.wait_ge(ysq_ready, o + 1)
                    if after(o, 1):
                        pool.wait_ge(yssq_ps, o)
                    pool.tensor_tensor(ysum[:, :], ysq[:, 0, :], ysq[:, 1, :], ALU.add).then_inc(ysum_ready, 1)
                if live(f):
                    pool.wait_ge(gap_ready, f + 1)
                    pool.tensor_tensor(egap[:, :], euler[:, :], gap[:, :], ALU.pow).then_inc(egap_ready, 1)
                if live(m):
                    pool.wait_ge(xs_ready, 2 * m + 2)
                    if after(m, 1):
                        pool.wait_ge(y_ps, 2 * m)
                    pool.tensor_tensor(xdt[:, :, :, :].rearrange("p b h d -> p (b h) d"),
                                       xs[:, :, :, :].rearrange("p b h d -> p (b h) d"),
                                       dt[:, bass.ts(m, GB * NH), None].to_broadcast([128, GB * NH, HD]),
                                       ALU.mult).then_inc(xdt_ready, 1)
                    pool.tensor_tensor(xd[:, :, :, :], xs[:, :, :, :],
                                       dskip[:, None, :, None].to_broadcast([128, GB, NH, HD]),
                                       ALU.mult).then_inc(xd_ready, 1)
                if live(o):
                    pool.wait_ge(yvar_ready, o + 1)
                    pool.tensor_tensor(yrstd[:, :], yvar[:, :], mhalf[:, :], ALU.pow).then_inc(yrstd_ready, 1)
                if live(o):
                    pool.wait_ge(h2_ready, o + 1)
                    pool.tensor_tensor(hsq2[:, :, :], h[:, o, :, 1, :], h[:, o, :, 1, :], ALU.mult) \
                        .then_inc(hsq2_ready, 1)
                    pool.wait_ge(var3_ready, o + 1)
                    pool.tensor_tensor(rstd3[:, :], var3[:, :], mhalf[:, :], ALU.pow).then_inc(rstd3_ready, 1)
                if live(f):
                    for p in range(1, NP - 1):
                        pool.wait_ge(prod_ready, NP * f + (p + 1))
                        if p > 1:
                            pool.wait_ge(acc_sum, (NP - 1) * f + (p - 1))
                        pool.tensor_tensor(prod[:, 0, :], prod[:, 0, :], prod[:, p, :], ALU.add) \
                            .then_inc(acc_sum, 1)

            stretch(pool, lstep, L_LEAD, 1, L_TAIL)

        @block.scalar
        def _(act):
            for dst, src in big_loads:
                act.dma_start(dst, src, allow_slow_non_contiguous=True).then_inc(bigloaded, 16)
            act.wait_ge(loaded, 16 * NSMALL)

            def step(k, slot):
                f, b, d = k - 1, k - 2, k - 4
                fs, bs = (slot - 1) % 2, slot
                if live(f):
                    act.wait_ge(h_ps, f + 1)
                    if after(f, 2):
                        act.wait_ge(ssq1_ready, f - 1)
                    act.activation(hsq[:, fs].rearrange("p b c -> p (b c)"), bank[fs][:, :], ACT.Square) \
                       .then_inc(hsq_ready, 1)
                if live(d):
                    act.wait_ge(uT_ps, d + 1)
                    act.wait_ge(utset, 1)
                    uT = bank[5][:, :].rearrange("p (b t) -> p b t", b=GB)
                    act.activation(ut_hi[0:D, bass.ts(d, GB), PAD:PAD + T], uT[0:D], ACT.Copy) \
                       .then_inc(uhi_ready, 1)
                    act.activation(ut_hi[D:128, bass.ts(d, GB), PAD + 1:PAD + T], uT[D:128, :, 0:T - 1], ACT.Copy) \
                       .then_inc(uhi_ready, 1)
                if live(b):
                    act.wait_ge(hnT_ps, b + 1)
                    if after(b, 2):
                        act.wait_ge(h1_ps, b - 1)
                    act.activation(gel[:, bs, :], bank[2 + bs][:, :], ACT.Gelu, bias=beta[:, :],
                                   scale=gamma[:, :]).then_inc(gel_ready, 1)
                if at(k, 2):
                    act.wait_ge(bigloaded, 16 * NBIG)
                    act.activation(ew1[:, :], ew1[:, :], ACT.Copy, scale=WSCALE).then_inc(scaled, 1)
                    act.wait_ge(scaled, 1)
                    act.activation(ew1_hi[:, :], ew1[:, :], ACT.Copy).then_inc(scaled, 1)

            stretch(act, step, T_LEAD, 2, T_TAIL)
            act.activation(aneg[:, :], aneg[:, :], ACT.Exp).then_inc(aexp, 1)

            act.wait_ge(sp_dve, 1)
            act.activation(sp[1][:, :], sp[1][:, :], ACT.Exp).then_inc(sp_act, 1)
            act.wait_ge(sp_dve, 2)
            act.activation(sp[0][:, :], sp[2][:, :], ACT.Ln).then_inc(sp_act, 1)

            def lstep(k, slot):
                m, o, f = k, k - 1, k - 2

                def relu(q):
                    if live(f):
                        act.wait_ge(hid_ps, NQ * f + (q + 1))
                        if q >= 4 or after(f, 1):
                            act.wait_ge(down_done, NQ * f + (q - 3))
                        act.activation(hid[:, q % 4, :], bank[4 + q % 2][:, :], ACT.Relu,
                                       bias=eb1[:, half(q):half(q) + 1]) \
                           .then_inc(hid_act, 1)

                def silu_x(i):
                    act.wait_ge(x_ps, 2 * m + (i + 1))
                    if i == 0 and after(m, 1):
                        act.wait_ge(xd_ready, m)
                    act.activation(xs[:, 2 * i:2 * i + 2].rearrange("p b h d -> p (b h d)"), bank[i][:, :],
                                   ACT.Silu, scale=1.0 / WSCALE).then_inc(xs_ready, 1)

                def silu_z(i):
                    act.wait_ge(z_ps, 2 * m + (i + 1))
                    if i == 0 and after(m, 1):
                        act.wait_ge(yg_ready, 2 * m)
                    act.activation(zs[:, i, :], bank[2 + i][:, :], ACT.Silu, scale=1.0 / WSCALE) \
                       .then_inc(zs_ready, 1)

                def spread(p):
                    if live(f):
                        act.wait_ge(share_ps, NP * f + (p + 1))
                        if p == 0 and after(f, 1):
                            act.wait_ge(prod_ready, NP * f)
                        act.activation(share[:, p, :], bank[SHARE_BANK[p]][:, :], ACT.Copy).then_inc(share_ready, 1)

                def decay(b):
                    if live(m):
                        act.wait_ge(exponent_ready, GB * m + (b + 1))
                        act.activation(dec[:, b], dec[:, b], ACT.Exp).then_inc(decay_ready, 1)

                if live(m):
                    silu_x(0)
                if live(f):
                    act.wait_ge(u2T_ps, f + 1)
                    if after(f, 1):
                        act.wait_ge(hid_ps, NQ * f)
                    act.activation(u2T[:, :], bank[2][:, :], ACT.Copy).then_inc(u2hi_ready, 1)
                if live(m):
                    silu_x(1)
                if live(o):
                    act.wait_ge(yg_ready, 2 * o + 2)
                    if after(o, 1):
                        act.wait_ge(ysum_ready, o)
                    act.activation(ysq[:, :, :], yg[:, :, :], ACT.Square).then_inc(ysq_ready, 1)
                if live(m):
                    silu_z(0)
                relu(0)
                if live(m):
                    act.wait_ge(bc_ps, m + 1)
                    if after(m, 1):
                        act.wait_ge(g_ps, m)
                    act.activation(bT[:, :], bank[0][0:NS, :], ACT.Silu, bias=convb_bc[0:NS, :],
                                   scale=1.0 / WSCALE).then_inc(bc_ready, 1)
                    act.activation(cT[:, :], bank[0][NS:128, :], ACT.Silu, bias=convb_bc[NS:128, :],
                                   scale=1.0 / WSCALE).then_inc(bc_ready, 1)
                relu(2)
                if live(f):
                    act.wait_ge(combT_ps, f + 1)
                    act.wait_ge(poolset, 7)
                    if after(f, 1):
                        act.wait_ge(share_ps, NP * f)
                    act.activation(combT[0:E, :], bank[3][0:E, :], ACT.Copy).then_inc(combT_hi, 1)
                relu(4)
                if live(m):
                    silu_z(1)
                spread(0)
                relu(6)
                spread(1)
                decay(0)
                decay(1)
                relu(8)
                spread(2)
                decay(2)
                decay(3)
                relu(10)
                spread(3)
                relu(12)
                relu(14)

            stretch(act, lstep, L_LEAD, 1, L_TAIL)

        @block.vector
        def _(dve):
            count = [0]

            def link(ins):
                count[0] += 1
                ins.then_inc(dvec, 1)
                dve.wait_ge(dvec, count[0])

            dve.wait_ge(ids_loaded, 16 * NIDS)
            dve.tensor_copy(idsf[:, :], ids[:, :]).then_inc(ids_ready, 1)
            link(dve.tensor_reduce(rowsum[0:NK, 0:1], w1x[:, :], AX.X, ALU.add))
            link(dve.tensor_scalar(rowsum[0:NK, 1:2], rowsum[0:NK, 0:1], -1.0 / HID, None, ALU.mult))
            link(dve.tensor_scalar(w1c[:, :], w1x[:, :], rowsum[0:NK, 1:2], None, ALU.add))
            dve.wait_ge(spec_ps, 1)
            link(dve.tensor_scalar(re[:, :], bank[0][0:3 * NF, 0:NSEQ], 1.0 / 127.5, dc[:, :], ALU.mult, ALU.add))
            link(dve.tensor_scalar(im[:, :], bank[0][0:3 * NF, NSEQ:2 * NSEQ], 1.0 / 127.5, None, ALU.mult))
            link(dve.tensor_tensor(m2[:, :], re[:, :], re[:, :], ALU.mult))
            link(dve.tensor_tensor(im2[:, :], im[:, :], im[:, :], ALU.mult))
            link(dve.tensor_tensor(m2[:, :], m2[:, :], im2[:, :], ALU.add))
            link(dve.tensor_scalar(zero[:, :], m2[:, :], 0.0, None, ALU.is_equal))
            link(dve.tensor_tensor(im2[:, :], m2[:, :], zero[:, :], ALU.add))
            link(dve.tensor_copy(m2[:, :], im2[:, :]))
            dve.sem_inc(m2_ready, 1)
            dve.wait_ge(inv_ready, 1)
            dve.wait_ge(poolset, 1)
            link(dve.tensor_tensor(im2[0:NF, :], m2[0:NF, :], zero[0:NF, :], ALU.subtract))
            link(dve.scalar_tensor_tensor(coef[0:NF, :], im2[0:NF, :], freq[:, :], inv[0:NF, :],
                                          ALU.mult, ALU.mult))
            link(dve.tensor_tensor(coef[NF:2 * NF, :], im[NF:2 * NF, :], inv[NF:2 * NF, :], ALU.mult))
            link(dve.tensor_tensor(re[2 * NF:, :], re[2 * NF:, :], inv[2 * NF:, :], ALU.mult))
            dve.tensor_tensor(coef[2 * NF:3 * NF, :], re[2 * NF:, :], zero[2 * NF:, :], ALU.add) \
               .then_inc(coef_ready, 1)
            dve.wait_ge(loaded, 16 * NSMALL)
            for src, dst in ((w2x[:, 0, :], w2x[:, 1, :]), (b2x[:, 0, :], b2x[:, 1, :])):
                link(dve.tensor_reduce(rowsum[:, 0:1], src, AX.X, ALU.add))
                link(dve.tensor_scalar(rowsum[:, 1:2], rowsum[:, 0:1], -1.0 / D, None, ALU.mult))
                link(dve.tensor_scalar(dst, src, rowsum[:, 1:2], None, ALU.add))
            dve.sem_inc(tok_weights, 1)
            link(dve.tensor_scalar(win[:, :], win[:, :], WSCALE, None, ALU.mult))
            dve.wait_ge(poolset, 3)
            for d0, s0, n in ((0, 0, DI), (DI, DI + NXBC, NH)):
                link(dve.tensor_copy(wz_hi[0:D, d0:d0 + n], win[0:D, s0:s0 + n]))
                link(dve.tensor_tensor(wz_lo[0:D, d0:d0 + n], win[0:D, s0:s0 + n], wz_hi[0:D, d0:d0 + n],
                                       ALU.subtract))
            dve.sem_inc(dt_weights, 1)

            def conv_weights():
                for a in range(2):
                    link(dve.tensor_tensor(wtmp[:, :], win[:, DI:DI + NXBC], taps[:, a, :], ALU.mult))
                    link(dve.tensor_copy(wc_hi[:, a, :], wtmp[:, :]))
                    link(dve.tensor_tensor(wc_lo[:, a, :], wtmp[:, :], wc_hi[:, a, :], ALU.subtract))
                link(dve.tensor_scalar(convb_row[:, :], convb_row[:, :], WSCALE, None, ALU.mult))
                dve.wait_ge(poolset, 5)
                link(dve.tensor_copy(convb16[0:1, :], convb_row[:, :]))
                link(dve.tensor_tensor(convb16[LOW:LOW + 1, :], convb_row[:, :], convb16[0:1, :], ALU.subtract))
                dve.memset(ones16[0:1, :], 1.0).then_inc(mix_weights, 1)
                dve.memset(ones16[LOW:LOW + 1, :], 1.0).then_inc(mix_weights, 1)

            def late_weights():
                dve.wait_ge(bigloaded, 16 * NBIG)
                for a in range(2):
                    link(dve.tensor_scalar(wo[:, a, 0, :], wo[:, a, 0, :], normw[:, a:a + 1], None, ALU.mult))
                    link(dve.tensor_reduce(rowsum[:, 0:1], wo[:, a, 0, :], AX.X, ALU.add))
                    link(dve.tensor_scalar(rowsum[:, 1:2], rowsum[:, 0:1], -1.0 / D, None, ALU.mult))
                    link(dve.tensor_scalar(wo[:, a, 1, :], wo[:, a, 0, :], rowsum[:, 1:2], None, ALU.add))
                link(dve.tensor_scalar(wg[:, :], wg[:, :], WSCALE, None, ALU.mult))
                link(dve.tensor_copy(wg_hi[:, :], wg[:, :]))
                link(dve.tensor_tensor(wg_lo[:, :], wg[:, :], wg_hi[:, :], ALU.subtract))
                link(dve.tensor_scalar(eb1[:, :], eb1[:, :], WSCALE, None, ALU.mult))
                link(dve.tensor_scalar(ew2[:, :, :], ew2[:, :, :], 1.0 / WSCALE, None, ALU.mult))
                dve.sem_inc(expert_weights, 1)

            def step(k, slot):
                f, b, c, d, e = k - 1, k - 2, k - 3, k - 4, k - 5
                fs, bs, cs_, ds_ = (slot - 1) % 2, slot, (slot - 1) % 2, slot
                if live(b):
                    dve.wait_ge(rstd1_ready, b + 1)
                    if after(b, 2):
                        dve.wait_ge(hnT_ps, b - 1)
                    dve.tensor_tensor(hn[:, bs], bank[bs][:, :].rearrange("p (b c) -> p b c", b=GB),
                                      rstd1[:, bs, :, None].to_broadcast([128, GB, HID]),
                                      ALU.mult).then_inc(hn_ready, 1)
                if live(f):
                    dve.wait_ge(hsq_ready, f + 1)
                    dve.tensor_reduce(ssq1[:, fs], hsq[:, fs], AX.X, ALU.add).then_inc(ssq1_ready, 1)
                    dve.wait_ge(ssq1_ready, f + 1)
                    dve.tensor_scalar(var1[:, fs], ssq1[:, fs], 1.0 / HID, LN_EPS, ALU.mult, ALU.add) \
                       .then_inc(var1_ready, 1)
                if live(d):
                    dve.wait_ge(rstd2_ready, d + 1)
                    if after(d, 2):
                        dve.wait_ge(uT_ps, d - 1)
                    for i in range(2):
                        ins = dve.tensor_tensor(udup[:, ds_, :, i, :], h[:, d, :, 1, :],
                                                rstd2[:, ds_, :, None].to_broadcast([128, GB, D]), ALU.mult)
                    ins.then_inc(u_ready, 1)
                if live(e):
                    dve.wait_ge(dt_ps, e + 1)
                    dve.tensor_scalar(dt[:, bass.ts(e, GB * NH)], bank[6][:, 0:GB * NH], 1.0 / WSCALE, None,
                                      ALU.mult).then_inc(dt_copied, 1)
                if live(c):
                    dve.wait_ge(h1_ps, c + 1)
                    dve.tensor_tensor(h[:, c], bank[4][:, :].rearrange("p (b i d) -> p b i d", b=GB, i=2),
                                      b2x[:, None, :, :].to_broadcast([128, GB, 2, D]), ALU.add) \
                       .then_inc(h1_ready, 1)
                if live(d):
                    uT = bank[5][:, :].rearrange("p (b t) -> p b t", b=GB)
                    dve.wait_ge(utset, 2)
                    dve.wait_ge(uhi_ready, 2 * d + 1)
                    dve.tensor_tensor(ut_lo[0:D, bass.ts(d, GB), PAD:PAD + T], uT[0:D],
                                      ut_hi[0:D, bass.ts(d, GB), PAD:PAD + T], ALU.subtract) \
                       .then_inc(ulo_ready, 1)
                    dve.wait_ge(uhi_ready, 2 * d + 2)
                    dve.tensor_tensor(ut_lo[D:128, bass.ts(d, GB), PAD + 1:PAD + T], uT[D:128, :, 0:T - 1],
                                      ut_hi[D:128, bass.ts(d, GB), PAD + 1:PAD + T], ALU.subtract) \
                       .then_inc(ulo_ready, 1)
                if live(c):
                    dve.wait_ge(csq_ready, c + 1)
                    dve.tensor_reduce(ssq2[:, cs_], csq[:, cs_], AX.X, ALU.add).then_inc(ssq2_ready, 1)
                    dve.wait_ge(ssq2_ready, c + 1)
                    dve.tensor_scalar(var2[:, cs_], ssq2[:, cs_], 1.0 / D, LN_EPS, ALU.mult, ALU.add) \
                       .then_inc(var2_ready, 1)
                if at(k, 0):
                    conv_weights()
                if at(k, 1):
                    late_weights()

            stretch(dve, step, T_LEAD, 2, T_TAIL)

            dve.wait_ge(dt_copied, NG)
            dve.wait_ge(aexp, 1)
            link(dve.tensor_scalar(aneg[:, :], aneg[:, :], -1.0, None, ALU.mult))
            v = dt[:, :].rearrange("p (b h) -> p b h", h=NH)
            link(dve.tensor_tensor(v, v, dtbias[:, None, :].to_broadcast([128, NSEQ, NH]), ALU.add))
            dve.scalar_tensor_tensor(sp[1][:, :], dt[:, :], -1.0, dt[:, :], ALU.mult, ALU.min).then_inc(sp_dve, 1)
            dve.wait_ge(sp_act, 1)
            dve.tensor_scalar(sp[2][:, :], sp[1][:, :], 1.0, None, ALU.add).then_inc(sp_dve, 1)
            dve.wait_ge(sp_act, 2)
            w, e_, lnw = sp[2], sp[1], sp[0]
            link(dve.tensor_scalar(csT[:, :, :].rearrange("p a t -> p (a t)"), w[:, :], 1.0, None, ALU.is_equal))
            one = csT[:, :, :].rearrange("p a t -> p (a t)")
            link(dve.tensor_tensor(lnw[:, :], lnw[:, :], one, ALU.add))
            link(dve.tensor_tensor(lnw[:, :], lnw[:, :], e_[:, :], ALU.mult))
            link(dve.scalar_tensor_tensor(w[:, :], w[:, :], -1.0, one, ALU.add, ALU.add))
            link(dve.reciprocal(e_[:, :], w[:, :]))
            link(dve.tensor_tensor(lnw[:, :], lnw[:, :], e_[:, :], ALU.mult))
            link(dve.scalar_tensor_tensor(dt[:, :], dt[:, :], 0.0, lnw[:, :], ALU.max, ALU.add))
            link(dve.tensor_tensor(sp[1][:, :].rearrange("p (b h) -> p b h", h=NH), v,
                                   aneg[:, None, :].to_broadcast([128, NSEQ, NH]), ALU.mult))
            dve.sem_inc(sp_dve, 1)
            dve.wait_ge(cs_ps, 1)
            dve.tensor_copy(cs[:, :], bank[6][:, 0:NSEQ * NH]).then_inc(cs_ready, 1)
            dve.wait_ge(csT_ps, 1)
            dve.tensor_copy(csT[:, :, :].rearrange("p a t -> p (a t)"), bank[7][:, 0:2 * T]).then_inc(csT_ready, 1)

            def lstep(k, slot):
                m, o, f, r = k, k - 1, k - 2, k - 3

                def relu(q):
                    if live(f):
                        dve.wait_ge(hid_ps, NQ * f + (q + 1))
                        if q >= 4 or after(f, 1):
                            dve.wait_ge(down_done, NQ * f + (q - 3))
                        dve.tensor_scalar(hid[:, q % 4, :], bank[4 + q % 2][:, :], eb1[:, half(q):half(q) + 1], 0.0,
                                          ALU.add, ALU.max).then_inc(hid_dve, 1)

                def weigh(p):
                    if live(f):
                        dve.wait_ge(down_done, NQ * f + (4 * p + 4))
                        if p == 0 and after(f, 1):
                            dve.wait_ge(acc_sum, (NP - 1) * f)
                        dve.wait_ge(share_ready, NP * f + (p + 1))
                        dve.scalar_tensor_tensor(prod[:, p, :], bank[6 + p % 2][:, :], eb2[:, p:p + 1],
                                                 share[:, p, :], ALU.add, ALU.mult).then_inc(prod_ready, 1)

                def exponents(b):
                    if live(m):
                        if b == 0:
                            dve.wait_ge(csb_loaded, 16 * m + 16)
                            if after(m, 1):
                                dve.wait_ge(y_ps, 2 * m)
                        for i in range(NH):
                            col = (b * NH + i)
                            ins = dve.scalar_tensor_tensor(dec[:, b, i, :], csb[:, col, :],
                                                           cs[:, bass.ds(m * (GB * NH) + col, 1)], mask[:, :],
                                                           ALU.subtract, ALU.min)
                        ins.then_inc(exponent_ready, 1)

                def mix(b):
                    if live(m):
                        if b == 0:
                            dve.wait_ge(g_ps, m + 1)
                        dve.wait_ge(decay_ready, GB * m + (b + 1))
                        dve.tensor_tensor(dec[:, b], dec[:, b],
                                          bank[1][:, None, b * T:(b + 1) * T].to_broadcast([128, NH, T]),
                                          ALU.mult).then_inc(mix_ready, 1)

                def gate_y(i):
                    if live(m):
                        dve.wait_ge(y_ps, 2 * m + (i + 1))
                        dve.wait_ge(zs_ready, 2 * m + 2)
                        if i == 0 and after(m, 1):
                            dve.wait_ge(o_ps, m)
                        dve.tensor_tensor(yg[:, i, :], bank[2 + i][:, :], zs[:, i, :], ALU.mult) \
                           .then_inc(yg_ready, 1)

                if live(f):
                    dve.wait_ge(u2hi_ready, f + 1)
                    dve.tensor_tensor(u2T[D:128, :], bank[2][D:128, :], u2T[D:128, :], ALU.subtract) \
                       .then_inc(u2lo_ready, 1)
                exponents(0)
                if live(f):
                    dve.wait_ge(s_ps, f + 1)
                    dve.scalar_tensor_tensor(score[:, :, :], bank[3][:, 0:GB * E].rearrange("p (b e) -> p b e", b=GB),
                                             1.0 / WSCALE, bg[:, None, :].to_broadcast([128, GB, E]),
                                             ALU.mult, ALU.add).then_inc(gate, 1)
                    dve.wait_ge(gate, 7 * f + 1)
                exponents(1)
                if live(f):
                    for b in range(GB):
                        ins = dve.max(top[:, b, :], score[:, b, :])
                    ins.then_inc(gate, 1)
                    dve.wait_ge(gate, 7 * f + 2)
                    if after(f, 1):
                        dve.wait_ge(egap_ready, f)
                    dve.tensor_tensor(gap[:, :], top[:, :, 1], top[:, :, 0], ALU.subtract).then_inc(gap_ready, 1)
                    for b in range(GB):
                        ins = dve.max_index(topi[:, b, :], top[:, b, :], score[:, b, :])
                    ins.then_inc(gate, 1)
                relu(1)
                if live(f):
                    dve.wait_ge(gate, 7 * f + 3)
                    dve.tensor_copy(topf[:, :, :], topi[:, :, 0:2]).then_inc(gate, 1)
                    dve.wait_ge(egap_ready, f + 1)
                    dve.tensor_scalar(gsum[:, :], egap[:, :], 1.0, None, ALU.add).then_inc(gate_sum, 1)
                    dve.wait_ge(gate_sum, 2 * f + 1)
                    dve.reciprocal(prob[:, 0, :], gsum[:, :]).then_inc(gate_sum, 1)
                    dve.wait_ge(gate_sum, 2 * f + 2)
                    dve.tensor_tensor(prob[:, 1, :], egap[:, :], prob[:, 0, :], ALU.mult).then_inc(gate, 1)
                    dve.wait_ge(gate, 7 * f + 4)
                    for i in range(2):
                        ins = dve.tensor_tensor(pick[:, i], iota[:, None, :].to_broadcast([128, GB, E]),
                                                topf[:, :, i, None].to_broadcast([128, GB, E]), ALU.is_equal)
                    ins.then_inc(gate, 1)
                    dve.wait_ge(gate, 7 * f + 6)
                    ins = dve.tensor_tensor(pick[:, :], pick[:, :],
                                            prob[:, :, :, None].to_broadcast([128, 2, GB, E]), ALU.mult)
                    ins.then_inc(gate_mul, 1)
                    dve.wait_ge(gate_mul, f + 1)
                    if after(f, 1):
                        dve.wait_ge(combT_ps, f)
                    dve.tensor_tensor(comb[:, :, :], pick[:, 0], pick[:, 1], ALU.add).then_inc(gate, 1)
                relu(3)
                if live(f):
                    dve.wait_ge(combT_hi, f + 1)
                    dve.tensor_tensor(combT[LOW:LOW + E, :], bank[3][0:E, :], combT[0:E, :], ALU.subtract) \
                       .then_inc(combT_lo, 1)
                relu(5)
                exponents(2)
                relu(7)
                exponents(3)
                if live(o):
                    dve.wait_ge(yssq_ps, o + 1)
                    dve.tensor_scalar(yvar[:, :], bank[1][:, 0:GB], 1.0 / DI, LN_EPS, ALU.mult, ALU.add) \
                       .then_inc(yvar_ready, 1)
                weigh(0)
                relu(9)
                if live(o):
                    dve.wait_ge(o_ps, o + 1)
                    dve.wait_ge(yrstd_ready, o + 1)
                    dve.tensor_tensor(hadd[:, :, :, :], bank[0][:, :].rearrange("p (b i d) -> p b i d", b=GB, i=2),
                                      yrstd[:, :, None, None].to_broadcast([128, GB, 2, D]),
                                      ALU.mult).then_inc(hadd_ready, 1)
                    dve.wait_ge(hadd_ready, o + 1)
                    dve.tensor_tensor(h[:, o], h[:, o], hadd[:, :, :, :], ALU.add).then_inc(h2_ready, 1)
                mix(0)
                relu(11)
                weigh(1)
                mix(1)
                if live(o):
                    dve.wait_ge(hsq2_ready, o + 1)
                    dve.tensor_reduce(ssq3[:, :], hsq2[:, :, :], AX.X, ALU.add).then_inc(ssq3_ready, 1)
                    dve.wait_ge(ssq3_ready, o + 1)
                    dve.tensor_scalar(var3[:, :], ssq3[:, :], 1.0 / D, LN_EPS, ALU.mult, ALU.add) \
                       .then_inc(var3_ready, 1)
                mix(2)
                relu(13)
                mix(3)
                weigh(2)
                relu(15)
                if live(o):
                    dve.wait_ge(rstd3_ready, o + 1)
                    if after(o, 1):
                        dve.wait_ge(u2T_ps, o)
                    for i in range(2):
                        ins = dve.tensor_tensor(u2[:, :, i, :], h[:, o, :, 1, :],
                                                rstd3[:, :, None].to_broadcast([128, GB, D]), ALU.mult)
                    ins.then_inc(u2_ready, 1)
                if live(r):
                    dve.wait_ge(out_ps, r + 1)
                    if after(r, 1):
                        dve.wait_ge(stored, 16 * r)
                    dve.tensor_tensor(res[:, :, :], bank[0][:, 0:GB * D].rearrange("p (b d) -> p b d", b=GB),
                                      h[:, r, :, 0, :], ALU.add).then_inc(res_ready, 1)
                gate_y(0)
                gate_y(1)
                weigh(3)

            stretch(dve, lstep, L_LEAD, 1, L_TAIL)

        @block.tensor
        def _(pe):
            pe.wait_ge(ids_loaded, 16 * NIDS)
            pe.wait_ge(ids_ready, 1)
            pe.matmul(bank[0][0:3 * NF, 0:NSEQ], dft[:, 0, :], idsf[:, :], start=True, stop=True)
            pe.matmul(bank[0][0:3 * NF, NSEQ:2 * NSEQ], dft[:, 1, :], idsf[:, :], start=True, stop=True) \
              .then_inc(spec_ps, 1)
            pe.wait_ge(loaded, 16 * NSMALL)

            def step(k, slot):
                f, b, c, d, e = k - 1, k - 2, k - 3, k - 4, k - 5
                fs, bs, cs_, ds_ = (slot - 1) % 2, slot, (slot - 1) % 2, slot
                if live(f):
                    pe.wait_ge(wsc_ready, f + 1)
                    if after(f, 2):
                        pe.wait_ge(hn_ready, f - 1)
                        pe.wait_ge(hsq_ready, f - 1)
                    pe.matmul(bank[fs][:, :], shift[:, :], wsc[:, fs].rearrange("p b c -> p (b c)"),
                              start=True, stop=True).then_inc(h_ps, 1)
                if live(e):
                    if at(e, 0):
                        pe.wait_ge(dt_weights, 1)
                    pe.wait_ge(ulo_ready, 2 * e + 2)
                    if after(e, 1):
                        pe.wait_ge(dt_copied, e)
                    for j in range(GB):
                        for n, (u, w_) in enumerate(((ut_hi, wz_hi), (ut_hi, wz_lo), (ut_lo, wz_hi))):
                            ins = pe.matmul(bank[6][:, j * NH:(j + 1) * NH], u[:, e * GB + j, PAD:PAD + T],
                                            w_[:, DI:DI + NH], start=(n == 0), stop=(n == 2))
                    ins.then_inc(dt_ps, 1)
                if live(c):
                    if at(c, 0):
                        pe.wait_ge(tok_weights, 1)
                    pe.wait_ge(gel_ready, c + 1)
                    if after(c, 1):
                        pe.wait_ge(h1_ready, c)
                    for j in range(GB):
                        ins = pe.matmul(bank[4][:, j * 2 * D:(j + 1) * 2 * D], gel[:, cs_, j * T:(j + 1) * T],
                                        w2x[:, :, :].rearrange("p i d -> p (i d)"), start=True, stop=True)
                    ins.then_inc(h1_ps, 1)
                if live(d):
                    pe.wait_ge(u_ready, d + 1)
                    if after(d, 1):
                        pe.wait_ge(ulo_ready, 2 * d)
                    for j in range(GB):
                        ins = pe.transpose(bank[5][:, j * T:(j + 1) * T],
                                           udup[:, ds_, j].rearrange("p i d -> p (i d)"), ident[:, :])
                    ins.then_inc(uT_ps, 1)
                if live(b):
                    pe.wait_ge(hn_ready, b + 1)
                    if after(b, 2):
                        pe.wait_ge(gel_ready, b - 1)
                    for j in range(GB):
                        ins = pe.transpose(bank[2 + bs][:, j * T:(j + 1) * T], hn[:, bs, j, :], ident[:, :])
                    ins.then_inc(hnT_ps, 1)

            stretch(pe, step, T_LEAD, 2, T_TAIL)

            pe.wait_ge(mix_weights, 2)

            def running_sums():
                pe.wait_ge(dt_copied, NG)
                pe.wait_ge(sp_dve, 3)
                pe.matmul(bank[6][:, 0:NSEQ * NH], upto[:, :], sp[1][:, :], start=True, stop=True) \
                  .then_inc(cs_ps, 1)
                pe.wait_ge(cs_ready, 1)
                for a in range(2):
                    ins = pe.transpose(bank[7][:, a * T:(a + 1) * T], cs[:, a * 128:(a + 1) * 128], ident[:, :])
                ins.then_inc(csT_ps, 1)

            def lstep(k, slot):
                m, o, f, r = k, k - 1, k - 2, k - 3

                def project_x(i):
                    if i == 0 and after(m, 4):
                        pe.wait_ge(res_ready, m - 3)
                    elif i == 0 and after(m, 2):
                        pe.wait_ge(hadd_ready, m - 1)
                    elif i == 0 and after(m, 1):
                        pe.wait_ge(bc_ready, 2 * m)
                    if i == 1 and after(m, 1):
                        pe.wait_ge(mix_ready, GB * m)
                    pe.matmul(bank[i][:, :], ones16[:, :], convb16[:, None, :].to_broadcast([128, 2, DI]),
                              start=True, stop=False, skip_group_check=True)
                    for j in range(2):
                        seq = m * GB + (2 * i + j)
                        for a, c0 in ((0, PAD), (1, PAD - 2)):
                            for u, w_ in ((ut_hi, wc_hi), (ut_hi, wc_lo), (ut_lo, wc_hi)):
                                ins = pe.matmul(bank[i][:, j * DI:(j + 1) * DI], u[:, seq, c0:c0 + T],
                                                w_[:, a, 0:DI], start=False,
                                                stop=(a == 1 and u is ut_lo), skip_group_check=True)
                    ins.then_inc(x_ps, 1)

                def project_z(i):
                    for n, (u, w_) in enumerate(((ut_hi, wz_hi), (ut_lo, wz_hi), (ut_hi, wz_lo))):
                        ins = pe.matmul(bank[2 + i][:, :], w_[:, i * 128:(i + 1) * 128],
                                        u[:, bass.ts(m, GB), PAD:PAD + T], start=(n == 0), stop=(n == 2))
                    ins.then_inc(z_ps, 1)

                def project_bc():
                    pe.wait_ge(xs_ready, 2 * m + 1)
                    n = 0
                    for a, c0 in ((0, PAD), (1, PAD - 2)):
                        for u, w_ in ((ut_hi, wc_hi), (ut_lo, wc_hi), (ut_hi, wc_lo)):
                            ins = pe.matmul(bank[0][:, :], w_[:, a, DI:NXBC], u[:, bass.ts(m, GB), c0:c0 + T],
                                            start=(n == 0), stop=(n == 5))
                            n += 1
                    ins.then_inc(bc_ps, 1)

                def up(q):
                    if q == 0:
                        pe.wait_ge(u2lo_ready, f + 1)
                    if q >= 2 or after(f, 1):
                        done = hid_act if q % 2 == 0 else hid_dve
                        pe.wait_ge(done, (NQ // 2) * f + q // 2)
                    for n, w_ in enumerate((ew1_hi, ew1_lo)):
                        ins = pe.matmul(bank[4 + q % 2][:, :], w_[:, half(q) * 128:(half(q) + 1) * 128], u2T[:, :],
                                        start=(n == 0), stop=(n == 1))
                    ins.then_inc(hid_ps, 1)

                def down(q):
                    p, e, j = q // 4, q % 2, (q % 4) // 2
                    done = hid_act if q % 2 == 0 else hid_dve
                    pe.wait_ge(done, (NQ // 2) * f + (q // 2 + 1))
                    if q % 4 == 0 and (p >= 2 or after(f, 1)):
                        pe.wait_ge(prod_ready, NP * f + (p - 1))
                    pe.matmul(bank[6 + p % 2][e * D:(e + 1) * D, :], ew2[:, half(q), :], hid[:, q % 4, :],
                              start=(j == 0), stop=(j == 1)).then_inc(down_done, 1)

                def spread(p):
                    if p == 0:
                        pe.wait_ge(combT_lo, f + 1)
                    pe.matmul(bank[SHARE_BANK[p]][:, :], select[:, p, :], combT[:, :], start=True, stop=True) \
                      .then_inc(share_ps, 1)

                if live(m):
                    project_x(0)
                if live(f):
                    pe.wait_ge(u2_ready, f + 1)
                    if live(o):
                        pe.wait_ge(yg_ready, 2 * o + 2)
                    elif after(f, 1):
                        pe.wait_ge(share_ready, NP * f)
                    for j in range(GB):
                        ins = pe.transpose(bank[2][:, j * T:(j + 1) * T], u2[:, j].rearrange("p i d -> p (i d)"),
                                           ident[:, :])
                    ins.then_inc(u2T_ps, 1)
                if live(m):
                    project_x(1)
                if live(f):
                    if at(k, 2):
                        pe.wait_ge(expert_weights, 2)
                    pe.wait_ge(u2lo_ready, f + 1)
                    for j in range(GB):
                        for n, w_ in enumerate((wg_hi, wg_lo)):
                            ins = pe.matmul(bank[3][:, j * E:(j + 1) * E], u2T[:, j * T:(j + 1) * T], w_[:, :],
                                            start=(n == 0), stop=(n == 1))
                    ins.then_inc(s_ps, 1)
                if live(m):
                    if not live(f) and live(o):
                        pe.wait_ge(yg_ready, 2 * o + 2)
                    project_z(0)
                for n in range(NQ // 2):
                    if live(f):
                        up(2 * n)
                        up(2 * n + 1)
                        if n:
                            down(2 * n - 2)
                            down(2 * n - 1)
                    if n == 0 and live(m):
                        project_bc()
                    if n == 1 and live(f):
                        pe.wait_ge(gate, 7 * f + 7)
                        for j in range(GB):
                            ins = pe.transpose(bank[3][0:E, j * T:(j + 1) * T], comb[:, j, :], ident[:, :])
                        ins.then_inc(combT_ps, 1)
                    if n == 2 and live(m):
                        if live(f):
                            pe.wait_ge(combT_lo, f + 1)
                        project_z(1)
                    if n == 2 and live(f):
                        if live(m):
                            pe.wait_ge(xs_ready, 2 * m + 2)
                        elif live(o):
                            pe.wait_ge(mix_ready, GB * o + GB)
                        spread(0)
                    if n == 3 and live(f):
                        if live(m):
                            pe.wait_ge(zs_ready, 2 * m + 2)
                        spread(1)
                    if n == 3 and live(o):
                        pe.wait_ge(ysum_ready, o + 1)
                        if live(f):
                            pe.wait_ge(share_ready, NP * f + 1)
                        elif live(m):
                            pe.wait_ge(xs_ready, 2 * m + 2)
                        for j in range(GB):
                            ins = pe.matmul(bank[1][:, j:j + 1], ysum[:, j * T:(j + 1) * T], ones[:, :],
                                            start=True, stop=True)
                        ins.then_inc(yssq_ps, 1)
                    if n == 3 and live(o):
                        if live(m):
                            pe.wait_ge(bc_ready, 2 * m + 2)
                        elif after(o, 3):
                            pe.wait_ge(res_ready, o - 2)
                        for j in range(GB):
                            for i in range(2):
                                ins = pe.matmul(bank[0][:, j * 2 * D:(j + 1) * 2 * D], yg[:, i, j * T:(j + 1) * T],
                                                wo[:, i].rearrange("p i d -> p (i d)"), start=(i == 0), stop=(i == 1))
                        ins.then_inc(o_ps, 1)
                    if n == 4 and live(f):
                        spread(2)
                    if n == 4 and at(k, 0):
                        running_sums()
                    if n == 4 and live(m):
                        pe.wait_ge(bc_ready, 2 * m + 2)
                        if live(o):
                            pe.wait_ge(yvar_ready, o + 1)
                        else:
                            pe.wait_ge(xs_ready, 2 * m + 2)
                        for j in range(GB):
                            ins = pe.matmul(bank[1][:, j * T:(j + 1) * T], bT[:, j * T:(j + 1) * T],
                                            cT[:, j * T:(j + 1) * T], start=True, stop=True)
                        ins.then_inc(g_ps, 1)
                    if n == 5 and live(f):
                        pe.wait_ge(share_ready, NP * f + 2)
                        spread(3)
                    if n == 6 and live(r):
                        pe.wait_ge(acc_sum, (NP - 1) * (r + 1))
                        if live(o):
                            pe.wait_ge(hadd_ready, o + 1)
                        elif after(r, 1):
                            pe.wait_ge(res_ready, r)
                        for j in range(GB):
                            ins = pe.matmul(bank[0][:, j * D:(j + 1) * D], acc[:, j * T:(j + 1) * T], pairs[:, :],
                                            start=True, stop=True)
                        ins.then_inc(out_ps, 1)
                if live(m):
                    pe.wait_ge(xd_ready, m + 1)
                    if live(f):
                        pe.wait_ge(share_ready, NP * f + NP)
                    else:
                        pe.wait_ge(zs_ready, 2 * m + 2)
                    for i in range(2):
                        for j in range(GB):
                            pe.matmul(bank[2 + i][:, j * T:(j + 1) * T],
                                      xd[:, j, 2 * i:2 * i + 2, :].rearrange("p h d -> p (h d)"), ident[:, :],
                                      is_transpose=True, start=(j == 0), stop=False, skip_group_check=True)
                if live(f):
                    down(NQ - 2)
                    down(NQ - 1)
                if live(m):
                    pe.wait_ge(xdt_ready, m + 1)
                    for i in range(2):
                        for j in range(GB):
                            pe.wait_ge(mix_ready, GB * m + (j + 1))
                            for hh in range(2):
                                ins = pe.matmul(bank[2 + i][hh * HD:(hh + 1) * HD, j * T:(j + 1) * T],
                                                xdt[:, j, 2 * i + hh, :], dec[:, j, 2 * i + hh, :],
                                                start=False, stop=True, skip_group_check=True)
                        ins.then_inc(y_ps, 1)

            stretch(pe, lstep, L_LEAD, 1, L_TAIL)


CONSTS = constants()


def kernel(**a):
    from concourse import bacc
    from concourse.bass_utils import run_bass_kernel_spmd

    def lay(x):
        return np.ascontiguousarray(np.asarray(x))

    arrays = {
        "ids": lay(np.asarray(a["x"]).T),
        "freq": lay(a["L0_tok_freq_bands"]), "tw1": lay(a["L0_tok_w1"]), "tb1": lay(a["L0_tok_b1"]),
        "gamma": lay(a["L0_tok_gamma"]), "beta": lay(a["L0_tok_beta"]),
        "tw2": lay(a["L0_tok_w2"]), "tb2": lay(a["L0_tok_b2"]),
        "winT": lay(np.asarray(a["L0_attn_in_proj_w"]).T),
        "convT": lay(np.asarray(a["L0_attn_conv_w"])[:, 0, :].T), "convb": lay(a["L0_attn_conv_b"]),
        "dtbias": lay(a["L0_attn_dt_bias"]), "alog": lay(a["L0_attn_A_log"]), "dskip": lay(a["L0_attn_D"]),
        "normw": lay(a["L0_attn_norm_w"]), "woT": lay(np.asarray(a["L0_attn_out_proj_w"]).T),
        "wgT": lay(np.asarray(a["L0_ffn_Wg"]).T), "bg": lay(a["L0_ffn_bg"]),
        "ew1T": lay(np.asarray(a["L0_ffn_W1"]).transpose(2, 0, 1).reshape(D, E * EH)),
        "eb1": lay(a["L0_ffn_b1"]),
        "ew2T": lay(np.asarray(a["L0_ffn_W2"]).transpose(0, 2, 1).reshape(E * EH, D)),
        "eb2": lay(a["L0_ffn_b2"]),
        **CONSTS,
    }
    nc = bacc.Bacc("TRN2", target_bir_lowering=False, num_devices=1)
    inp = {n: nc.dram_tensor(f"in_{n}", list(x.shape), mybir.dt.from_np(x.dtype), kind="ExternalInput").ap()
           for n, x in arrays.items()}
    out = nc.dram_tensor("out_tower", [NSEQ, T, D], F32, kind="ExternalOutput").ap()
    build(nc, inp, out)
    r = run_bass_kernel_spmd(nc, [{f"in_{n}": x for n, x in arrays.items()}], core_ids=[0])
    return r.results[0]["out_tower"]
```

```python
from contextlib import ExitStack

import numpy as np
import concourse.bass as bass
from concourse import mybir

F32 = mybir.dt.float32
F16 = mybir.dt.float16
I32 = mybir.dt.int32
U32 = mybir.dt.uint32
ALU = mybir.AluOpType
ACT = mybir.ActivationFunctionType
AX = mybir.AxisListType

NSEQ, T = 64, 128
D, HID = 64, 128
NF = 32
DI, NH, HD, NS, KW = 256, 4, 64, 64, 4
NXBC = DI + 2 * NS
NIN = DI + NXBC + NH
E, EH = 8, 256
GB = 4
NG = NSEQ // GB
GT = GB * T
NK = 3 * NF + 1
PAD = 3
SW = PAD + T + 1
NQ = 2 * E
LN_EPS = 1e-5
WSCALE = 256.0
MASKED = -1e30
NCH = 4
NP = E // 2


def constants():
    t = np.arange(T, dtype=np.float64)
    f = np.arange(NF, dtype=np.float64)
    ang = 2 * np.pi / T * ((t[:, None] * f[None, :]) % T)
    cos, sin = np.cos(ang), np.sin(ang)
    dft = np.zeros((T, 2, 3 * NF), np.float32)
    dft[:, 0] = np.tile(cos, (1, 3))
    dft[:, 1] = np.tile(-sin, (1, 3))
    shift = np.ones((NK, T), np.float32)
    shift[NF:2 * NF] = cos.T
    shift[2 * NF:3 * NF] = sin.T
    dc = np.zeros((3 * NF, 1), np.float32)
    dc[::NF] = -float(T)
    s = np.arange(T)
    upto = (s[:, None] <= s[None, :])
    return {
        "dft": dft.reshape(T, -1), "shift": shift, "dc": dc,
        "upto": upto.astype(np.float32),
        "mask": np.where(upto, 0.0, MASKED).astype(np.float32),
        "ident": np.eye(128, dtype=np.float32),
        "pairs": np.concatenate([np.eye(D, dtype=np.float32)] * 2),
        "iota": np.tile(np.arange(E, dtype=np.float32), (128, 1)),
    }


def build(nc, inp, out):
    with ExitStack() as ctx:
        def sb(name, shape, dt=F32):
            return ctx.enter_context(nc.sbuf_tensor(name, shape, dt))

        def sem(name):
            return ctx.enter_context(nc.semaphore(name))

        bank = [ctx.enter_context(nc.psum_tensor(f"bank{i}", [128, 512], F32)) for i in range(8)]

        ident = sb("ident", [128, 128])
        mask = sb("mask", [128, T])
        upto = sb("upto", [128, T])
        iota = sb("iota", [128, E])
        dft = sb("dft_sb", [128, 2, 3 * NF])
        shift = sb("shift_sb", [NK, T])
        dc = sb("dc_sb", [3 * NF, 1])
        ids = sb("ids", [128, NSEQ], I32)
        idsf = sb("idsf", [128, NSEQ])
        freq = sb("freq", [NF, 1])
        w1x = sb("w1x", [NK, HID])
        w1c = sb("w1c", [NK, HID])
        gamma = sb("gamma", [HID, 1])
        beta = sb("beta", [HID, 1])
        w2x = sb("w2x", [HID, 2, D])
        b2x = sb("b2x", [128, 2, D])
        wc_hi = sb("wc_hi", [128, KW, NXBC], F16)
        wc_lo = sb("wc_lo", [128, KW // 2, NXBC], F16)
        wz_hi = sb("wz_hi", [128, DI + NH], F16)
        wz_lo = sb("wz_lo", [128, DI + NH], F16)
        ones = sb("ones_col", [128, 1])
        dtbias = sb("dtbias", [128, NH])
        aneg = sb("aneg", [128, NH])
        dskip = sb("dskip", [128, NH])
        normw = sb("normw", [128, 2])
        wo = sb("wo", [128, 2, 2, D])
        wg = sb("wg", [128, E])
        wg_hi = sb("wg_hi", [128, E], F16)
        wg_lo = sb("wg_lo", [128, E], F16)
        bg = sb("bg", [128, E])
        ew1_hi = sb("ew1_hi", [128, E * EH], F16)
        ew1_lo = sb("ew1_lo", [128, E * EH], F16)
        eb1 = sb("eb1", [128, NQ])
        ew2 = sb("ew2", [128, NQ, D])
        eb2 = sb("eb2", [128, NP])
        pairs = sb("pairs_sb", [128, D])
        mhalf = sb("mhalf", [128, GB])
        euler = sb("euler", [128, GB])
        rowsum = sb("rowsum", [128, 8])

        re = sb("re", [3 * NF, NSEQ])
        im = sb("im", [3 * NF, NSEQ])
        m2 = sb("m2", [3 * NF, NSEQ])
        im2 = sb("im2", [3 * NF, NSEQ])
        zero = sb("zero", [3 * NF, NSEQ])
        mhalf_w = sb("mhalf_w", [3 * NF, NSEQ])
        inv = sb("inv", [3 * NF, NSEQ])
        coef = sb("coef", [NK, NSEQ])

        h = sb("h", [128, NG, GB, 2, D])
        ut_parts = sb("ut_parts", [128, NSEQ, SW], F16)
        ut_pair = sb("ut_pair", [128, NSEQ, SW], F16)
        dt = sb("dt", [128, NSEQ * NH])
        cs = sb("cs", [128, NSEQ * NH])

        wsc = sb("wsc", [NK, 2, GB, HID])
        hsq = sb("hsq", [128, 2, GB, HID])
        ssq1 = sb("ssq1", [128, 2, GB])
        var1 = sb("var1", [128, 2, GB])
        rstd1 = sb("rstd1", [128, 2, GB])
        hn = sb("hn", [128, 2, GB, HID])
        gel = sb("gel", [HID, 2, GT])
        csq = sb("csq", [128, 2, GB, D])
        ssq2 = sb("ssq2", [128, 2, GB])
        var2 = sb("var2", [128, 2, GB])
        rstd2 = sb("rstd2", [128, 2, GB])
        udup = sb("udup", [128, 2, GB, 2, D])

        csT = sb("csT", [128, 2, T])
        cs_dram = nc.dram_tensor("cs_dram", [NSEQ * NH, T], F32).ap()

        csb = sb("csb", [128, GB * NH, T])
        dec = sb("dec", [128, GB, NH, T])
        xs = sb("xs", [128, 2, GB, NH, HD])
        dskip_eye = sb("dskip_eye", [128, NH, T])
        zs = sb("zs", [128, 2, GT])
        bT = sb("bT", [NS, GT])
        cT = sb("cT", [NS, GT])
        yg = sb("yg", [128, 2, GT])
        ysq = sb("ysq", [128, 2, GT])
        ysum = sb("ysum", [128, GT])
        yvar = sb("yvar", [128, GB])
        yrstd = sb("yrstd", [128, GB])
        hadd = sb("hadd", [128, GB, 2, D])
        hsq2 = sb("hsq2", [128, GB, D])
        ssq3 = sb("ssq3", [128, GB])
        var3 = sb("var3", [128, GB])
        rstd3 = sb("rstd3", [128, GB])
        u2 = sb("u2", [128, GB, 2, D])
        u2T = sb("u2T", [128, GT], F16)
        score = sb("score", [128, GB, E])
        top = sb("top", [128, GB, 8])
        topi = sb("topi", [128, GB, 8], U32)
        topf = sb("topf", [128, GB, 2])
        gap = sb("gap", [128, GB])
        egap = sb("egap", [128, GB])
        gsum = sb("gsum", [128, GB])
        prob = sb("prob", [128, 2, GB])
        pick = sb("pick", [128, 2, GB, E])
        comb = sb("comb", [128, GB, E])
        combT = sb("combT", [E, GT])
        share_dram = nc.dram_tensor("share_dram", [E, GT], F32).ap()
        share = sb("share", [128, NP, GT])
        hid = sb("hid", [128, 4, GT])
        prod = sb("prod", [128, NP, GT])
        acc = sb("acc", [128, GT])
        res = sb("res", [128, GB, D])

        ew1 = dec[:, :, :, :].rearrange("p b h t -> p (b h t)")
        csb_flat = csb[:, :, :].rearrange("p a t -> p (a t)")
        win = csb_flat[:, 0:NIN]
        wlast = csb_flat[:, NIN:2 * NIN]
        bias_row = csb_flat[:, 2 * NIN:2 * NIN + NXBC]
        prod_flat = prod[:, :, :].rearrange("p a t -> p (a t)")
        taps = prod_flat[:, 0:KW * NXBC].rearrange("p (a c) -> p a c", a=KW)
        share_flat = share[:, :, :].rearrange("p a t -> p (a t)")
        sp = [share_flat[:, i * NSEQ * NH:(i + 1) * NSEQ * NH] for i in range(3)]

        ids_loaded = sem("ids_loaded")
        token_loaded = sem("token_loaded")
        mixer_loaded = sem("mixer_loaded")
        bigloaded = sem("bigloaded")
        poolset = sem("poolset")
        utset = sem("utset")
        poolc = sem("poolc")
        dvec = sem("dvec")
        tok_weights = sem("tok_weights")
        dt_weights = sem("dt_weights")
        mix_weights = sem("mix_weights")
        scaled = sem("scaled")
        expert_weights = sem("expert_weights")
        spec_ps = sem("spec_ps")
        m2_ready = sem("m2_ready")
        inv_ready = sem("inv_ready")
        coef_ready = sem("coef_ready")
        ids_ready = sem("ids_ready")
        aexp = sem("aexp")
        wsc_ready = sem("wsc_ready")
        h_ps = sem("h_ps")
        ssq1_ready = sem("ssq1_ready")
        var1_ready = sem("var1_ready")
        rstd1_ready = sem("rstd1_ready")
        hn_ready = sem("hn_ready")
        hnT_ps = sem("hnT_ps")
        gel_ready = sem("gel_ready")
        h1_ps = sem("h1_ps")
        h1_ready = sem("h1_ready")
        csq_ready = sem("csq_ready")
        ssq2_ready = sem("ssq2_ready")
        var2_ready = sem("var2_ready")
        rstd2_ready = sem("rstd2_ready")
        u_ready = sem("u_ready")
        uT_ps = sem("uT_ps")
        uhi_ready = sem("uhi_ready")
        ulo_ready = sem("ulo_ready")
        pair_ready = sem("pair_ready")
        dt_ps = sem("dt_ps")
        dt_copied = sem("dt_copied")
        sp_dve = sem("sp_dve")
        sp_act = sem("sp_act")
        cs_ps = sem("cs_ps")
        cs_ready = sem("cs_ready")
        csT_ps = sem("csT_ps")
        csT_ready = sem("csT_ready")
        cs_saved = sem("cs_saved")
        csb_loaded = sem("csb_loaded")
        exponent_ready = sem("exponent_ready")
        decay_ready = sem("decay_ready")
        x_ps = sem("x_ps")
        xs_ready = sem("xs_ready")
        z_ps = sem("z_ps")
        zs_ready = sem("zs_ready")
        bc_ps = sem("bc_ps")
        bc_ready = sem("bc_ready")
        skip_ready = sem("skip_ready")
        bias_zeroed = sem("bias_zeroed")
        bias_loaded = sem("bias_loaded")
        const_rows = sem("const_rows")
        g_ps = sem("g_ps")
        mix_ready = sem("mix_ready")
        y_ps = sem("y_ps")
        yg_ready = sem("yg_ready")
        ysq_ready = sem("ysq_ready")
        ysum_ready = sem("ysum_ready")
        yssq_ps = sem("yssq_ps")
        yvar_ready = sem("yvar_ready")
        yrstd_ready = sem("yrstd_ready")
        o_ps = sem("o_ps")
        hadd_ready = sem("hadd_ready")
        h2_ready = sem("h2_ready")
        hsq2_ready = sem("hsq2_ready")
        ssq3_ready = sem("ssq3_ready")
        var3_ready = sem("var3_ready")
        rstd3_ready = sem("rstd3_ready")
        u2_ready = sem("u2_ready")
        u2T_ps = sem("u2T_ps")
        u2hi_ready = sem("u2hi_ready")
        u2lo_ready = sem("u2lo_ready")
        s_ps = sem("s_ps")
        gate = sem("gate")
        gate_sum = sem("gate_sum")
        gate_mul = sem("gate_mul")
        gap_ready = sem("gap_ready")
        egap_ready = sem("egap_ready")
        combT_ps = sem("combT_ps")
        combT_ready = sem("combT_ready")
        share_saved = sem("share_saved")
        share_loaded = sem("share_loaded")
        hid_ps = sem("hid_ps")
        hid_act = sem("hid_act")
        hid_dve = sem("hid_dve")
        down_done = sem("down_done")
        prod_ready = sem("prod_ready")
        acc_sum = sem("acc_sum")
        out_ps = sem("out_ps")
        res_ready = sem("res_ready")
        stored = sem("stored")

        block = ctx.enter_context(nc.Block())

        ids_loads = [
            (ids[:, :], inp["ids"]), (dft[:, :, :].rearrange("p a b -> p (a b)"), inp["dft"]),
            (dc[:, :], inp["dc"]), (freq[:, :], inp["freq"].rearrange("(p a) -> p a", a=1)),
            (w1x[0:2 * NF, :], inp["tw1"]), (w1x[2 * NF:3 * NF, :], inp["tw1"][NF:2 * NF, :]),
            (w1x[3 * NF:NK, :], inp["tb1"].rearrange("(a p) -> a p", a=1)),
            (shift[:, :], inp["shift"]),
        ]
        token_loads = [
            (ident[:, :], inp["ident"]),
            (w2x[:, 0, :], inp["tw2"]), (b2x[:, 0, :], inp["tb2"].partition_broadcast(128)),
            (gamma[:, :], inp["gamma"].rearrange("(p a) -> p a", a=1)),
            (beta[:, :], inp["beta"].rearrange("(p a) -> p a", a=1)),
        ]
        mixer_loads = [
            (win[0:D, :], inp["winT"]), (win[D:128, :], inp["winT"]),
            (wlast[:, :], inp["winT"][D - 1].partition_broadcast(128)),
            (taps[:, :, :], inp["convT"].partition_broadcast(128)),
        ]
        big_loads = [
            (dtbias[:, :], inp["dtbias"].partition_broadcast(128)),
            (aneg[:, :], inp["alog"].partition_broadcast(128)),
            (dskip[:, :], inp["dskip"].partition_broadcast(128)),
            (mask[:, :], inp["mask"]), (upto[:, :], inp["upto"]), (iota[:, :], inp["iota"]),
            (pairs[:, :], inp["pairs"]),
            (normw[:, :], inp["normw"].rearrange("(a p) -> p a", a=2)),
            (wo[:, 0, 0, :], inp["woT"][0:128, :]), (wo[:, 1, 0, :], inp["woT"][128:256, :]),
            (wg[0:D, :], inp["wgT"]), (wg[D:128, :], inp["wgT"]),
            (bg[:, :], inp["bg"].partition_broadcast(128)),
            (ew1[0:D, :], inp["ew1T"]), (ew1[D:128, :], inp["ew1T"]),
            (eb1[:, :], inp["eb1"].rearrange("e (j p) -> p (e j)", j=2)),
            (ew2[:, :, :], inp["ew2T"].rearrange("(q p) d -> p q d", p=128)),
            (eb2[:, :], inp["eb2"].rearrange("(p e) d -> (e d) p", e=2)),
        ]

        NIDS, NTOKEN, NMIXER, NBIG = len(ids_loads), len(token_loads), len(mixer_loads), len(big_loads)
        DVE_TURNS = [1, 3, 5, 7, 9]

        def half(q):
            return 2 * (2 * (q // 4) + q % 2) + (q % 4) // 2

        def hid_done(q, f):
            on_act = [t for t in range(NQ) if t not in DVE_TURNS]
            done, turns = (hid_dve, DVE_TURNS) if q in DVE_TURNS else (hid_act, on_act)
            return done, len(turns) * f + (turns.index(q) + 1)

        def live(g):
            return not isinstance(g, int) or 0 <= g < NG

        def at(k, n):
            return isinstance(k, int) and k == n

        def after(g, n):
            return not isinstance(g, int) or g >= n

        def stretch(eng, step, lead, unroll, end, steps, extra={}):
            def written_out(k):
                step(k, k % unroll)
                if k in extra:
                    extra[k]()

            for k in range(lead):
                written_out(k)
            with eng.Fori(0, (end - lead) // unroll) as i:
                for s in range(unroll):
                    step(i * unroll + (lead + s), (lead + s) % unroll)
            for k in range(end, steps):
                written_out(k)

        def half_cols(a):
            return slice(a * NSEQ * NH // 2, (a + 1) * NSEQ * NH // 2)

        def down_bank(k, p):
            return bank[p if p >= 2 and at(k, NG + 1) else 6 + p % 2]

        HALF = NG // 2 + 5
        T_LEAD, T_END, T_STEPS = 8, 12, NG + 6
        L_LEAD, L_STEPS = 4, NG + 3

        @block.sync
        def _(sp_):
            for dst, src in ids_loads:
                sp_.dma_start(dst, src, allow_slow_non_contiguous=True).then_inc(ids_loaded, 16)
            for dst, src in token_loads:
                sp_.dma_start(dst, src, allow_slow_non_contiguous=True).then_inc(token_loaded, 16)
            for dst, src in mixer_loads:
                sp_.dma_start(dst, src, allow_slow_non_contiguous=True).then_inc(mixer_loaded, 16)
            sp_.wait_ge(bias_zeroed, 1)
            sp_.dma_start(bias_row[D - 1:D, :], inp["convb"].rearrange("(a c) -> a c", a=1)) \
               .then_inc(bias_loaded, 16)

            def save_sums(a):
                sp_.wait_ge(csT_ready, a + 1)
                sp_.dma_start(cs_dram[a * 128:(a + 1) * 128, :], csT[:, a, :]).then_inc(cs_saved, 16)
                sp_.wait_ge(cs_saved, 16 * (a + 1))

            save_sums(0)

            def step(k, slot):
                m, f, r = k, k - 2, k - 4
                if at(k, 3):
                    save_sums(1)
                if live(m):
                    if after(m, 1):
                        sp_.wait_ge(exponent_ready, m * GB)
                    sp_.dma_start(csb[:, :, :], cs_dram[bass.ts(m, GB * NH), :].partition_broadcast(128)) \
                       .then_inc(csb_loaded, 16)
                if live(r):
                    sp_.wait_ge(res_ready, r + 1)
                    sp_.dma_start(out[bass.ts(r, GB)].rearrange("b t d -> t b d"), res[:, :, :]) \
                       .then_inc(stored, 16)
                if live(f):
                    sp_.wait_ge(combT_ready, f + 1)
                    if after(f, 1):
                        sp_.wait_ge(share_loaded, 32 * f)
                    sp_.dma_start(share_dram, combT[:, :]).then_inc(share_saved, 16)
                    if after(f, 1):
                        sp_.wait_ge(prod_ready, NP * f)
                    sp_.wait_ge(share_saved, 16 * f + 16)
                    for e in range(2):
                        sp_.dma_start(share[e * D:(e + 1) * D, :, :],
                                      share_dram.rearrange("(p e) t -> e p t", e=2)[e].partition_broadcast(D)) \
                           .then_inc(share_loaded, 16)

            stretch(sp_, step, L_LEAD, 1, NG, L_STEPS + 1)
            sp_.wait_ge(stored, 16 * NG)

        @block.gpsimd
        def _(pool):
            pool.memset(mhalf_w[:, :], -0.5).then_inc(poolc, 1)
            pool.memset(coef[:, :], 1.0).then_inc(poolset, 1)
            pool.memset(mhalf[:, :], -0.5).then_inc(poolc, 1)
            pool.memset(wz_lo[:, :], 0.0).then_inc(poolset, 1)
            pool.memset(bias_row[:, :], 0.0).then_inc(bias_zeroed, 1)
            pool.memset(ut_parts[:, :, 0:PAD], 0.0).then_inc(utset, 1)
            pool.memset(ut_pair[:, :, 0:PAD + 1], 0.0).then_inc(utset, 1)
            pool.memset(udup[:, :, :, :, D - 1:D], 1.0).then_inc(const_rows, 1)
            pool.wait_ge(m2_ready, 1)
            pool.wait_ge(poolc, 2)

            def inverse(c):
                cols = bass.ts(c, NSEQ // NCH)
                pool.tensor_tensor(inv[:, cols], m2[:, cols], mhalf_w[:, cols], ALU.pow).then_inc(inv_ready, 1)

            inverse(0)

            def step(k, slot):
                w, f, c = k, k - 1, k - 3
                ws, fs, cs_ = slot, (slot - 1) % 2, (slot - 1) % 2
                if live(w):
                    if isinstance(w, int):
                        pool.wait_ge(coef_ready, w // (NG // NCH) + 1)
                    if after(w, 2):
                        pool.wait_ge(h_ps, w - 1)
                    pool.tensor_tensor(wsc[:, ws], w1c[:, None, :].to_broadcast([NK, GB, HID]),
                                       coef[:, bass.ts(w, GB), None].to_broadcast([NK, GB, HID]),
                                       ALU.mult).then_inc(wsc_ready, 1)
                if isinstance(k, int) and k < NCH - 1:
                    inverse(k + 1)
                if live(c):
                    pool.wait_ge(h1_ready, c + 1)
                    if after(c, 2):
                        pool.wait_ge(ssq2_ready, c - 1)
                    pool.tensor_tensor(csq[:, cs_], h[:, c, :, 1, :], h[:, c, :, 1, :], ALU.mult) \
                        .then_inc(csq_ready, 1)
                if live(f):
                    pool.wait_ge(var1_ready, f + 1)
                    if after(f, 2):
                        pool.wait_ge(hn_ready, f - 1)
                    pool.tensor_tensor(rstd1[:, fs], var1[:, fs], mhalf[:, :], ALU.pow).then_inc(rstd1_ready, 1)
                if live(c):
                    pool.wait_ge(var2_ready, c + 1)
                    if after(c, 2):
                        pool.wait_ge(u_ready, c - 1)
                    pool.tensor_tensor(rstd2[:, cs_], var2[:, cs_], mhalf[:, :], ALU.pow).then_inc(rstd2_ready, 1)
                if at(k, NG):
                    pool.wait_ge(bigloaded, 16 * NBIG)
                    pool.tensor_tensor(dskip_eye[:, :, :], ident[:, None, :].to_broadcast([128, NH, T]),
                                       dskip[:, :, None].to_broadcast([128, NH, T]), ALU.mult).then_inc(skip_ready, 1)
                    pool.memset(ones[:, :], 1.0).then_inc(poolset, 1)
                    pool.memset(euler[:, :], float(np.e)).then_inc(poolc, 1)

            stretch(pool, step, T_LEAD, 2, T_END, T_STEPS)
            pool.wait_ge(scaled, 2)
            pool.tensor_tensor(ew1_lo[:, :], ew1[:, :], ew1_hi[:, :], ALU.subtract) \
                .then_inc(expert_weights, 1)

            def lstep(k, slot):
                m, o, f, r = k, k - 1, k - 2, k - 3

                def skip(b):
                    if live(m):
                        pool.wait_ge(mix_ready, GB * m + (b + 1))
                        pool.tensor_tensor(dec[:, b], dec[:, b], dskip_eye[:, :, :], ALU.add).then_inc(skip_ready, 1)

                def add_pair(p):
                    if live(f) and not at(k, NG + 1):
                        pool.wait_ge(prod_ready, NP * f + (p + 1))
                        if p > 1:
                            pool.wait_ge(acc_sum, (NP - 1) * f + (p - 1))
                        pool.tensor_tensor(prod[:, 0, :], prod[:, 0, :], prod[:, p, :], ALU.add) \
                            .then_inc(acc_sum, 1)

                if live(r) and not at(k, L_STEPS - 1):
                    pool.wait_ge(prod_ready, NP * r + NP)
                    pool.wait_ge(acc_sum, (NP - 1) * r + (NP - 2))
                    if after(r, 1):
                        pool.wait_ge(out_ps, r)
                    pool.tensor_tensor(acc[:, :], prod[:, 0, :], prod[:, NP - 1, :], ALU.add).then_inc(acc_sum, 1)
                if live(f):
                    pool.wait_ge(gap_ready, f + 1)
                    pool.tensor_tensor(egap[:, :], euler[:, :], gap[:, :], ALU.pow).then_inc(egap_ready, 1)
                if live(o):
                    pool.wait_ge(ysq_ready, o + 1)
                    if after(o, 1):
                        pool.wait_ge(yssq_ps, o)
                    pool.tensor_tensor(ysum[:, :], ysq[:, 0, :], ysq[:, 1, :], ALU.add).then_inc(ysum_ready, 1)
                if live(o):
                    pool.wait_ge(yvar_ready, o + 1)
                    pool.tensor_tensor(yrstd[:, :], yvar[:, :], mhalf[:, :], ALU.pow).then_inc(yrstd_ready, 1)
                skip(0)
                skip(1)
                skip(2)
                if live(o):
                    pool.wait_ge(h2_ready, o + 1)
                    pool.tensor_tensor(hsq2[:, :, :], h[:, o, :, 1, :], h[:, o, :, 1, :], ALU.mult) \
                        .then_inc(hsq2_ready, 1)
                skip(3)
                if live(o):
                    pool.wait_ge(var3_ready, o + 1)
                    pool.tensor_tensor(rstd3[:, :], var3[:, :], mhalf[:, :], ALU.pow).then_inc(rstd3_ready, 1)
                add_pair(1)
                add_pair(2)

            stretch(pool, lstep, L_LEAD, 1, NG, L_STEPS)

        @block.scalar
        def _(act):
            for dst, src in big_loads:
                act.dma_start(dst, src, allow_slow_non_contiguous=True).then_inc(bigloaded, 16)
            act.wait_ge(token_loaded, 16 * NTOKEN)

            def step(k, slot):
                f, b, d = k - 1, k - 2, k - 5
                fs, bs = (slot - 1) % 2, slot
                if live(f):
                    act.wait_ge(h_ps, f + 1)
                    if after(f, 2):
                        act.wait_ge(var1_ready, f - 1)
                    for j in range(GB):
                        ins = act.activation(hsq[:, fs, j, :], bank[fs][:, j * T:(j + 1) * T], ACT.Square,
                                             accum_out=ssq1[:, fs, j:j + 1])
                    ins.then_inc(ssq1_ready, 1)
                if live(d):
                    act.wait_ge(uT_ps, d + 1)
                    act.wait_ge(utset, 2)
                    uT = bank[5][:, :].rearrange("p (b t) -> p b t", b=GB)
                    act.activation(ut_pair[D:128, bass.ts(d, GB), PAD + 1:PAD + T + 1], uT[D:128], ACT.Copy) \
                       .then_inc(uhi_ready, 1)
                    act.activation(ut_parts[0:D, bass.ts(d, GB), PAD:PAD + T], uT[0:D], ACT.Copy) \
                       .then_inc(uhi_ready, 1)
                if live(b):
                    act.wait_ge(hnT_ps, b + 1)
                    if after(b, 2):
                        act.wait_ge(h1_ps, b - 1)
                    act.activation(gel[:, bs, :], bank[2 + bs][:, :], ACT.Gelu, bias=beta[:, :],
                                   scale=gamma[:, :]).then_inc(gel_ready, 1)
                if live(d):
                    act.wait_ge(uhi_ready, 2 * d + 2)
                    act.activation(ut_pair[0:D, bass.ts(d, GB), PAD:PAD + T],
                                   ut_parts[0:D, bass.ts(d, GB), PAD:PAD + T], ACT.Copy).then_inc(pair_ready, 1)
                if at(k, NG + 1):
                    act.wait_ge(bigloaded, 16 * NBIG)
                    act.activation(ew1[:, :], ew1[:, :], ACT.Copy, scale=WSCALE).then_inc(scaled, 1)
                if at(k, NG + 2):
                    act.wait_ge(scaled, 1)
                    act.activation(ew1_hi[:, :], ew1[:, :], ACT.Copy).then_inc(scaled, 1)

            def soft_exp(a):
                if a == 0:
                    act.wait_ge(bigloaded, 16 * NBIG)
                    act.activation(aneg[:, :], aneg[:, :], ACT.Exp).then_inc(aexp, 1)
                act.wait_ge(sp_dve, 3 * a + 1)
                act.activation(sp[1][:, half_cols(a)], sp[1][:, half_cols(a)], ACT.Exp).then_inc(sp_act, 1)

            def soft_ln(a):
                act.wait_ge(sp_dve, 3 * a + 2)
                act.activation(sp[0][:, half_cols(a)], sp[2][:, half_cols(a)], ACT.Ln).then_inc(sp_act, 1)

            stretch(act, step, T_LEAD, 2, T_END, T_STEPS,
                    {HALF: lambda: soft_exp(0), HALF + 2: lambda: soft_ln(0)})

            def lstep(k, slot):
                m, o, f = k, k - 1, k - 2

                def relu(q):
                    if live(f):
                        act.wait_ge(hid_ps, NQ * f + (q + 1))
                        if q >= 4 or after(f, 1):
                            act.wait_ge(down_done, NQ * f + (q - 3))
                        act.activation(hid[:, q % 4, :], bank[4 + q % 2][:, :], ACT.Relu,
                                       bias=eb1[:, half(q):half(q) + 1]) \
                           .then_inc(hid_act, 1)

                def silu_x(i):
                    if i == 0 and after(m, 2):
                        act.wait_ge(y_ps, 2 * m - 2)
                    act.wait_ge(x_ps, 2 * m + (i + 1))
                    act.activation(xs[:, slot, 2 * i:2 * i + 2].rearrange("p b h d -> p (b h d)"), bank[2 * i][:, :],
                                   ACT.Silu, scale=1.0 / WSCALE).then_inc(xs_ready, 1)

                def silu_z(i):
                    act.wait_ge(z_ps, 2 * m + (i + 1))
                    if i == 0 and after(m, 1):
                        act.wait_ge(yg_ready, 2 * m)
                    act.activation(zs[:, i, :], bank[3 - i][:, :], ACT.Silu, scale=1.0 / WSCALE) \
                       .then_inc(zs_ready, 1)

                def decay(b):
                    if live(m):
                        act.wait_ge(exponent_ready, GB * m + (b + 1))
                        act.activation(dec[:, b], dec[:, b], ACT.Exp).then_inc(decay_ready, 1)

                if live(m):
                    silu_x(0)
                if live(m):
                    silu_z(0)
                    silu_x(1)
                if live(o):
                    act.wait_ge(yg_ready, 2 * o + 2)
                    if after(o, 1):
                        act.wait_ge(ysum_ready, o)
                    act.activation(ysq[:, :, :], yg[:, :, :], ACT.Square).then_inc(ysq_ready, 1)
                relu(0)
                if live(m):
                    act.wait_ge(bc_ps, m + 1)
                    if after(m, 1):
                        act.wait_ge(g_ps, m)
                    act.activation(bT[:, :], bank[0][0:NS, :], ACT.Silu,
                                   scale=1.0 / WSCALE).then_inc(bc_ready, 1)
                    act.activation(cT[:, :], bank[0][NS:128, :], ACT.Silu,
                                   scale=1.0 / WSCALE).then_inc(bc_ready, 1)
                relu(2)
                if live(f):
                    act.wait_ge(combT_ps, f + 1)
                    if after(f, 1):
                        act.wait_ge(share_saved, 16 * f)
                    act.activation(combT[:, :], bank[1][0:E, :], ACT.Copy).then_inc(combT_ready, 1)
                relu(4)
                if live(m):
                    silu_z(1)
                relu(6)
                for b in range(GB):
                    decay(b)
                if at(k, 0):
                    soft_exp(1)
                    soft_ln(1)
                relu(8)
                relu(10)
                relu(11)
                relu(12)
                relu(13)
                relu(14)
                relu(15)

            stretch(act, lstep, L_LEAD, 2, NG, L_STEPS)

        @block.vector
        def _(dve):
            count = [0]

            def link(ins):
                count[0] += 1
                ins.then_inc(dvec, 1)
                dve.wait_ge(dvec, count[0])

            dve.wait_ge(ids_loaded, 16 * NIDS)
            dve.tensor_copy(idsf[:, :], ids[:, :]).then_inc(ids_ready, 1)
            link(dve.tensor_reduce(rowsum[0:NK, 0:1], w1x[:, :], AX.X, ALU.add))
            link(dve.tensor_scalar(rowsum[0:NK, 1:2], rowsum[0:NK, 0:1], -1.0 / HID, None, ALU.mult))
            link(dve.tensor_scalar(w1c[:, :], w1x[:, :], rowsum[0:NK, 1:2], None, ALU.add))
            dve.wait_ge(spec_ps, 1)
            link(dve.tensor_scalar(re[:, :], bank[0][0:3 * NF, 0:NSEQ], 1.0 / 127.5, dc[:, :], ALU.mult, ALU.add))
            link(dve.tensor_scalar(im[:, :], bank[0][0:3 * NF, NSEQ:2 * NSEQ], 1.0 / 127.5, None, ALU.mult))
            link(dve.tensor_tensor(m2[:, :], re[:, :], re[:, :], ALU.mult))
            link(dve.tensor_tensor(im2[:, :], im[:, :], im[:, :], ALU.mult))
            link(dve.tensor_tensor(m2[:, :], m2[:, :], im2[:, :], ALU.add))
            link(dve.tensor_scalar(zero[:, :], m2[:, :], 0.0, None, ALU.is_equal))
            link(dve.tensor_tensor(im2[:, :], m2[:, :], zero[:, :], ALU.add))
            link(dve.tensor_copy(m2[:, :], im2[:, :]))
            dve.sem_inc(m2_ready, 1)

            def coefficients(c):
                cols = bass.ts(c, NSEQ // NCH)
                dve.wait_ge(inv_ready, c + 1)
                link(dve.tensor_tensor(im2[0:NF, cols], m2[0:NF, cols], zero[0:NF, cols], ALU.subtract))
                link(dve.scalar_tensor_tensor(coef[0:NF, cols], im2[0:NF, cols], freq[:, :], inv[0:NF, cols],
                                              ALU.mult, ALU.mult))
                link(dve.tensor_tensor(coef[NF:2 * NF, cols], im[NF:2 * NF, cols], inv[NF:2 * NF, cols], ALU.mult))
                link(dve.tensor_tensor(re[2 * NF:, cols], re[2 * NF:, cols], inv[2 * NF:, cols], ALU.mult))
                dve.tensor_tensor(coef[2 * NF:3 * NF, cols], re[2 * NF:, cols], zero[2 * NF:, cols], ALU.add) \
                   .then_inc(coef_ready, 1)

            dve.wait_ge(poolset, 1)
            coefficients(0)
            dve.wait_ge(token_loaded, 16 * NTOKEN)
            for src, dst in ((w2x[:, 0, :], w2x[:, 1, :]), (b2x[:, 0, :], b2x[:, 1, :])):
                link(dve.tensor_reduce(rowsum[:, 0:1], src, AX.X, ALU.add))
                link(dve.tensor_scalar(rowsum[:, 1:2], rowsum[:, 0:1], -1.0 / D, None, ALU.mult))
                link(dve.tensor_scalar(dst, src, rowsum[:, 1:2], None, ALU.add))
            dve.sem_inc(tok_weights, 1)

            def input_weights():
                dve.wait_ge(mixer_loaded, 16 * NMIXER)
                link(dve.tensor_tensor(win[:, :], win[:, :], wlast[:, :], ALU.subtract))
                link(dve.tensor_scalar(win[:, :], win[:, :], WSCALE, None, ALU.mult))
                dve.wait_ge(poolset, 2)
                for d0, s0, n in ((0, 0, DI), (DI, DI + NXBC, NH)):
                    link(dve.tensor_copy(wz_hi[:, d0:d0 + n], win[:, s0:s0 + n]))
                    link(dve.tensor_tensor(wz_lo[0:D, d0:d0 + n], win[0:D, s0:s0 + n], wz_hi[0:D, d0:d0 + n],
                                           ALU.subtract))
                dve.sem_inc(dt_weights, 1)

            def conv_weights(j):
                tap = taps[:, KW - 1 - j, :]
                link(dve.tensor_tensor(tap, win[:, DI:DI + NXBC], tap, ALU.mult))
                if j == 0:
                    dve.wait_ge(bias_loaded, 16)
                    link(dve.scalar_tensor_tensor(tap, bias_row[:, :], WSCALE, tap, ALU.mult, ALU.add))
                link(dve.tensor_copy(wc_hi[:, j, :], tap))
                rows = slice(0, D) if j % 2 == 0 else slice(D, 128)
                link(dve.tensor_tensor(wc_lo[rows, j // 2, :], tap[rows], wc_hi[rows, j, :], ALU.subtract))
                dve.sem_inc(mix_weights, 1)

            def late_weights():
                dve.wait_ge(bigloaded, 16 * NBIG)
                for a in range(2):
                    link(dve.tensor_scalar(wo[:, a, 0, :], wo[:, a, 0, :], normw[:, a:a + 1], None, ALU.mult))
                    link(dve.tensor_reduce(rowsum[:, 0:1], wo[:, a, 0, :], AX.X, ALU.add))
                    link(dve.tensor_scalar(rowsum[:, 1:2], rowsum[:, 0:1], -1.0 / D, None, ALU.mult))
                    link(dve.tensor_scalar(wo[:, a, 1, :], wo[:, a, 0, :], rowsum[:, 1:2], None, ALU.add))
                link(dve.tensor_scalar(wg[:, :], wg[:, :], WSCALE, None, ALU.mult))
                link(dve.tensor_copy(wg_hi[:, :], wg[:, :]))
                link(dve.tensor_tensor(wg_lo[:, :], wg[:, :], wg_hi[:, :], ALU.subtract))
                link(dve.tensor_scalar(eb1[:, :], eb1[:, :], WSCALE, None, ALU.mult))
                link(dve.tensor_scalar(ew2[:, :, :], ew2[:, :, :], 1.0 / WSCALE, None, ALU.mult))
                dve.sem_inc(expert_weights, 1)

            def step(k, slot):
                f, b, c, d, q, e = k - 1, k - 2, k - 3, k - 4, k - 5, k - 6
                fs, bs, cs_, ds_ = (slot - 1) % 2, slot, (slot - 1) % 2, slot
                if live(b):
                    dve.wait_ge(rstd1_ready, b + 1)
                    if after(b, 2):
                        dve.wait_ge(hnT_ps, b - 1)
                    dve.tensor_tensor(hn[:, bs], bank[bs][:, :].rearrange("p (b c) -> p b c", b=GB),
                                      rstd1[:, bs, :, None].to_broadcast([128, GB, HID]),
                                      ALU.mult).then_inc(hn_ready, 1)
                if live(c):
                    dve.wait_ge(h1_ps, c + 1)
                    dve.tensor_tensor(h[:, c], bank[4][:, :].rearrange("p (b i d) -> p b i d", b=GB, i=2),
                                      b2x[:, None, :, :].to_broadcast([128, GB, 2, D]), ALU.add) \
                       .then_inc(h1_ready, 1)
                if live(d):
                    dve.wait_ge(rstd2_ready, d + 1)
                    if after(d, 2):
                        dve.wait_ge(uT_ps, d - 1)
                    dve.tensor_tensor(udup[:, ds_, :, :, 0:D - 1],
                                      h[:, d, :, 1, None, 0:D - 1].to_broadcast([128, GB, 2, D - 1]),
                                      rstd2[:, ds_, :, None, None].to_broadcast([128, GB, 2, D - 1]),
                                      ALU.mult).then_inc(u_ready, 1)
                if live(f):
                    dve.wait_ge(ssq1_ready, f + 1)
                    dve.tensor_scalar(var1[:, fs], ssq1[:, fs], 1.0 / HID, LN_EPS, ALU.mult, ALU.add) \
                       .then_inc(var1_ready, 1)
                if live(q):
                    uT = bank[5][:, :].rearrange("p (b t) -> p b t", b=GB)
                    dve.wait_ge(uhi_ready, 2 * q + 1)
                    dve.tensor_tensor(ut_parts[D:128, bass.ts(q, GB), PAD:PAD + T], uT[D:128],
                                      ut_pair[D:128, bass.ts(q, GB), PAD + 1:PAD + T + 1], ALU.subtract) \
                       .then_inc(ulo_ready, 1)
                if live(e):
                    dve.wait_ge(dt_ps, e + 1)
                    dve.tensor_scalar(dt[:, bass.ts(e, GB * NH)], bank[6][:, 0:GB * NH], 1.0 / WSCALE, None,
                                      ALU.mult).then_inc(dt_copied, 1)
                if live(c):
                    dve.wait_ge(csq_ready, c + 1)
                    dve.tensor_reduce(ssq2[:, cs_], csq[:, cs_], AX.X, ALU.add).then_inc(ssq2_ready, 1)
                    dve.wait_ge(ssq2_ready, c + 1)
                    dve.tensor_scalar(var2[:, cs_], ssq2[:, cs_], 1.0 / D, LN_EPS, ALU.mult, ALU.add) \
                       .then_inc(var2_ready, 1)
                if isinstance(k, int) and k < NCH - 1:
                    coefficients(k + 1)
                if at(k, 1):
                    input_weights()
                if isinstance(k, int) and 2 <= k < 2 + KW:
                    conv_weights(k - 2)

            def soft_start(a):
                dve.wait_ge(dt_copied, NG // 2 * (a + 1))
                if a == 0:
                    dve.wait_ge(bigloaded, 16 * NBIG)
                v = dt[:, half_cols(a)].rearrange("p (b h) -> p b h", h=NH)
                link(dve.tensor_tensor(v, v, dtbias[:, None, :].to_broadcast([128, NSEQ // 2, NH]), ALU.add))
                dve.scalar_tensor_tensor(sp[1][:, half_cols(a)], dt[:, half_cols(a)], -1.0, dt[:, half_cols(a)],
                                         ALU.mult, ALU.min).then_inc(sp_dve, 1)

            def soft_middle(a):
                dve.wait_ge(sp_act, 2 * a + 1)
                dve.tensor_scalar(sp[2][:, half_cols(a)], sp[1][:, half_cols(a)], 1.0, None, ALU.add) \
                   .then_inc(sp_dve, 1)
                if a == 0:
                    dve.wait_ge(aexp, 1)
                    link(dve.tensor_scalar(aneg[:, :], aneg[:, :], -1.0, None, ALU.mult))

            def soft_end(a):
                dve.wait_ge(sp_act, 2 * a + 2)
                lnw, e_, w = (t[:, half_cols(a)] for t in sp)
                one = csT[:, a, :]
                link(dve.tensor_scalar(one, w, 1.0, None, ALU.is_equal))
                link(dve.tensor_tensor(lnw, lnw, one, ALU.add))
                link(dve.tensor_tensor(lnw, lnw, e_, ALU.mult))
                link(dve.scalar_tensor_tensor(w, w, -1.0, one, ALU.add, ALU.add))
                link(dve.reciprocal(e_, w))

            def soft_last(a):
                lnw, e_, w = (t[:, half_cols(a)] for t in sp)
                link(dve.tensor_tensor(lnw, lnw, e_, ALU.mult))
                link(dve.scalar_tensor_tensor(dt[:, half_cols(a)], dt[:, half_cols(a)], 0.0, lnw, ALU.max, ALU.add))
                link(dve.tensor_tensor(e_.rearrange("p (b h) -> p b h", h=NH),
                                       dt[:, half_cols(a)].rearrange("p (b h) -> p b h", h=NH),
                                       aneg[:, None, :].to_broadcast([128, NSEQ // 2, NH]), ALU.mult))
                dve.sem_inc(sp_dve, 1)

            def take_sums(a):
                dve.wait_ge(cs_ps, a + 1)
                dve.tensor_copy(cs[:, half_cols(a)], bank[7][:, 0:128]).then_inc(cs_ready, 1)

            def take_transposed(a):
                dve.wait_ge(csT_ps, a + 1)
                dve.tensor_copy(csT[:, a, :], bank[7][:, 128:256]).then_inc(csT_ready, 1)

            stretch(dve, step, T_LEAD, 2, T_END, T_STEPS,
                    {HALF: lambda: soft_start(0), HALF + 2: lambda: soft_middle(0), HALF + 3: lambda: soft_end(0),
                     HALF + 4: lambda: soft_last(0), HALF + 5: lambda: take_sums(0),
                     HALF + 6: lambda: take_transposed(0)})
            soft_start(1)
            late_weights()

            def lstep(k, slot):
                m, o, f, r = k, k - 1, k - 2, k - 3

                def relu(q):
                    if live(f):
                        dve.wait_ge(hid_ps, NQ * f + (q + 1))
                        if q >= 4 or after(f, 1):
                            dve.wait_ge(down_done, NQ * f + (q - 3))
                        dve.tensor_scalar(hid[:, q % 4, :], bank[4 + q % 2][:, :], eb1[:, half(q):half(q) + 1], 0.0,
                                          ALU.add, ALU.max).then_inc(hid_dve, 1)

                def weigh(p, f):
                    if live(f):
                        dve.wait_ge(down_done, NQ * f + (4 * p + 4))
                        if p == 0 and after(f, 1):
                            dve.wait_ge(acc_sum, (NP - 1) * f)
                        dve.wait_ge(share_loaded, 32 * f + 32)
                        dve.scalar_tensor_tensor(prod[:, p, :], down_bank(f + 2, p)[:, :], eb2[:, p:p + 1],
                                                 share[:, p, :], ALU.add, ALU.mult).then_inc(prod_ready, 1)

                def exponents(b):
                    if live(m):
                        if b == 0:
                            dve.wait_ge(csb_loaded, 16 * m + 16)
                            if at(k, 0):
                                dve.wait_ge(expert_weights, 2)
                            if after(m, 1):
                                dve.wait_ge(y_ps, 2 * m)
                        for i in range(NH):
                            col = (b * NH + i)
                            ins = dve.scalar_tensor_tensor(dec[:, b, i, :], csb[:, col, :],
                                                           cs[:, bass.ds(m * (GB * NH) + col, 1)], mask[:, :],
                                                           ALU.subtract, ALU.min)
                        ins.then_inc(exponent_ready, 1)

                def mix(b):
                    if live(m):
                        if b == 0:
                            dve.wait_ge(g_ps, m + 1)
                        dve.wait_ge(decay_ready, GB * m + (b + 1))
                        for i in range(NH):
                            ins = dve.scalar_tensor_tensor(dec[:, b, i, :], dec[:, b, i, :],
                                                           dt[:, bass.ds(m * (GB * NH) + (b * NH + i), 1)],
                                                           bank[1][:, b * T:(b + 1) * T], ALU.mult, ALU.mult)
                        ins.then_inc(mix_ready, 1)

                def gate_y(i):
                    if live(m):
                        dve.wait_ge(y_ps, 2 * m + (i + 1))
                        dve.wait_ge(zs_ready, 2 * m + 2)
                        if i == 0 and after(m, 1):
                            dve.wait_ge(o_ps, m)
                        dve.tensor_tensor(yg[:, i, :], bank[2 + i][:, :], zs[:, i, :], ALU.mult) \
                           .then_inc(yg_ready, 1)

                if live(f):
                    dve.wait_ge(u2T_ps, f + 1)
                    if after(f, 1):
                        dve.wait_ge(hid_ps, NQ * f)
                    dve.tensor_copy(u2T[:, :], bank[1][:, :]).then_inc(u2hi_ready, 1)
                    dve.wait_ge(u2hi_ready, f + 1)
                    dve.tensor_tensor(u2T[D:128, :], bank[1][D:128, :], u2T[D:128, :], ALU.subtract) \
                       .then_inc(u2lo_ready, 1)
                weigh(3, r)
                if live(f):
                    dve.wait_ge(s_ps, f + 1)
                    dve.scalar_tensor_tensor(score[:, :, :], bank[1][:, 0:GB * E].rearrange("p (b e) -> p b e", b=GB),
                                             1.0 / WSCALE, bg[:, None, :].to_broadcast([128, GB, E]),
                                             ALU.mult, ALU.add).then_inc(gate, 1)
                    dve.wait_ge(gate, 7 * f + 1)
                exponents(0)
                if live(f):
                    for b in range(GB):
                        ins = dve.max(top[:, b, :], score[:, b, :])
                    ins.then_inc(gate, 1)
                    dve.wait_ge(gate, 7 * f + 2)
                    if after(f, 1):
                        dve.wait_ge(egap_ready, f)
                    dve.tensor_tensor(gap[:, :], top[:, :, 1], top[:, :, 0], ALU.subtract).then_inc(gap_ready, 1)
                    for b in range(GB):
                        ins = dve.max_index(topi[:, b, :], top[:, b, :], score[:, b, :])
                    ins.then_inc(gate, 1)
                relu(1)
                if live(f):
                    dve.wait_ge(gate, 7 * f + 3)
                    dve.tensor_copy(topf[:, :, :], topi[:, :, 0:2]).then_inc(gate, 1)
                    dve.wait_ge(egap_ready, f + 1)
                    dve.tensor_scalar(gsum[:, :], egap[:, :], 1.0, None, ALU.add).then_inc(gate_sum, 1)
                    dve.wait_ge(gate_sum, 2 * f + 1)
                    dve.reciprocal(prob[:, 0, :], gsum[:, :]).then_inc(gate_sum, 1)
                    dve.wait_ge(gate_sum, 2 * f + 2)
                    dve.tensor_tensor(prob[:, 1, :], egap[:, :], prob[:, 0, :], ALU.mult).then_inc(gate, 1)
                    dve.wait_ge(gate, 7 * f + 4)
                    for i in range(2):
                        ins = dve.tensor_tensor(pick[:, i], iota[:, None, :].to_broadcast([128, GB, E]),
                                                topf[:, :, i, None].to_broadcast([128, GB, E]), ALU.is_equal)
                    ins.then_inc(gate, 1)
                    dve.wait_ge(gate, 7 * f + 6)
                    ins = dve.tensor_tensor(pick[:, :], pick[:, :],
                                            prob[:, :, :, None].to_broadcast([128, 2, GB, E]), ALU.mult)
                    ins.then_inc(gate_mul, 1)
                    dve.wait_ge(gate_mul, f + 1)
                    if after(f, 1):
                        dve.wait_ge(combT_ps, f)
                    dve.tensor_tensor(comb[:, :, :], pick[:, 0], pick[:, 1], ALU.add).then_inc(gate, 1)
                if at(k, 2):
                    take_sums(1)
                relu(3)
                if at(k, 2):
                    take_transposed(1)
                relu(5)
                exponents(1)
                relu(7)
                exponents(2)
                exponents(3)
                if at(k, 1):
                    soft_end(1)
                    soft_last(1)
                if live(o):
                    dve.wait_ge(yssq_ps, o + 1)
                    dve.tensor_scalar(yvar[:, :], bank[2][:, 0:GB], 1.0 / DI, LN_EPS, ALU.mult, ALU.add) \
                       .then_inc(yvar_ready, 1)
                mix(0)
                mix(1)
                relu(9)
                weigh(0, f)
                mix(2)
                if live(o):
                    dve.wait_ge(o_ps, o + 1)
                    dve.wait_ge(yrstd_ready, o + 1)
                    dve.tensor_tensor(hadd[:, :, :, :], bank[0][:, :].rearrange("p (b i d) -> p b i d", b=GB, i=2),
                                      yrstd[:, :, None, None].to_broadcast([128, GB, 2, D]),
                                      ALU.mult).then_inc(hadd_ready, 1)
                    dve.wait_ge(hadd_ready, o + 1)
                    dve.tensor_tensor(h[:, o], h[:, o], hadd[:, :, :, :], ALU.add).then_inc(h2_ready, 1)
                mix(3)
                if at(k, 0):
                    soft_middle(1)
                weigh(1, f)
                if live(o):
                    dve.wait_ge(hsq2_ready, o + 1)
                    dve.tensor_reduce(ssq3[:, :], hsq2[:, :, :], AX.X, ALU.add).then_inc(ssq3_ready, 1)
                    dve.wait_ge(ssq3_ready, o + 1)
                    dve.tensor_scalar(var3[:, :], ssq3[:, :], 1.0 / D, LN_EPS, ALU.mult, ALU.add) \
                       .then_inc(var3_ready, 1)
                weigh(2, f)
                if live(o):
                    dve.wait_ge(rstd3_ready, o + 1)
                    if after(o, 1):
                        dve.wait_ge(u2T_ps, o)
                    dve.tensor_tensor(u2[:, :, :, :], h[:, o, :, 1, None, :].to_broadcast([128, GB, 2, D]),
                                      rstd3[:, :, None, None].to_broadcast([128, GB, 2, D]),
                                      ALU.mult).then_inc(u2_ready, 1)
                if live(r):
                    dve.wait_ge(out_ps, r + 1)
                    if after(r, 1):
                        dve.wait_ge(stored, 16 * r)
                    dve.tensor_tensor(res[:, :, :], bank[0][:, 0:GB * D].rearrange("p (b d) -> p b d", b=GB),
                                      h[:, r, :, 0, :], ALU.add).then_inc(res_ready, 1)
                gate_y(0)
                gate_y(1)

            stretch(dve, lstep, L_LEAD, 1, NG, L_STEPS)

        @block.tensor
        def _(pe):
            pe.wait_ge(ids_loaded, 16 * NIDS)
            pe.wait_ge(ids_ready, 1)
            pe.matmul(bank[0][0:3 * NF, 0:NSEQ], dft[:, 0, :], idsf[:, :], start=True, stop=True)
            pe.matmul(bank[0][0:3 * NF, NSEQ:2 * NSEQ], dft[:, 1, :], idsf[:, :], start=True, stop=True) \
              .then_inc(spec_ps, 1)
            pe.wait_ge(token_loaded, 16 * NTOKEN)

            def step(k, slot):
                f, b, c, d, e = k - 1, k - 2, k - 3, k - 5, k - 6
                fs, bs, cs_, ds_ = (slot - 1) % 2, slot, (slot - 1) % 2, (slot - 1) % 2
                if live(f):
                    pe.wait_ge(wsc_ready, f + 1)
                    if after(f, 2):
                        pe.wait_ge(hn_ready, f - 1)
                        pe.wait_ge(ssq1_ready, f - 1)
                    pe.matmul(bank[fs][:, :], shift[:, :], wsc[:, fs].rearrange("p b c -> p (b c)"),
                              start=True, stop=True).then_inc(h_ps, 1)
                if live(c):
                    if at(c, 0):
                        pe.wait_ge(tok_weights, 1)
                    pe.wait_ge(gel_ready, c + 1)
                    if after(c, 1):
                        pe.wait_ge(h1_ready, c)
                    for j in range(GB):
                        ins = pe.matmul(bank[4][:, j * 2 * D:(j + 1) * 2 * D], gel[:, cs_, j * T:(j + 1) * T],
                                        w2x[:, :, :].rearrange("p i d -> p (i d)"), start=True, stop=True)
                    ins.then_inc(h1_ps, 1)
                if live(d):
                    if at(d, 0):
                        pe.wait_ge(const_rows, 1)
                    pe.wait_ge(u_ready, d + 1)
                    if after(d, 1):
                        pe.wait_ge(ulo_ready, d)
                        pe.wait_ge(uhi_ready, 2 * d)
                    for j in range(GB):
                        ins = pe.transpose(bank[5][:, j * T:(j + 1) * T],
                                           udup[:, ds_, j].rearrange("p i d -> p (i d)"), ident[:, :])
                    ins.then_inc(uT_ps, 1)
                if live(b):
                    pe.wait_ge(hn_ready, b + 1)
                    if after(b, 2):
                        pe.wait_ge(gel_ready, b - 1)
                    for j in range(GB):
                        ins = pe.transpose(bank[2 + bs][:, j * T:(j + 1) * T], hn[:, bs, j, :], ident[:, :])
                    ins.then_inc(hnT_ps, 1)
                if live(e):
                    if at(e, 0):
                        pe.wait_ge(dt_weights, 1)
                    pe.wait_ge(ulo_ready, e + 1)
                    pe.wait_ge(uhi_ready, 2 * e + 2)
                    if after(e, 1):
                        pe.wait_ge(dt_copied, e)
                    for j in range(GB):
                        for n, w_ in enumerate((wz_hi, wz_lo)):
                            ins = pe.matmul(bank[6][:, j * NH:(j + 1) * NH], ut_parts[:, e * GB + j, PAD:PAD + T],
                                            w_[:, DI:DI + NH], start=(n == 0), stop=(n == 1))
                    ins.then_inc(dt_ps, 1)

            def running_sums(a):
                pe.wait_ge(sp_dve, 3 * a + 3)
                if a == 1:
                    pe.wait_ge(csT_ready, 1)
                pe.matmul(bank[7][:, 0:128], upto[:, :], sp[1][:, half_cols(a)], start=True, stop=True) \
                  .then_inc(cs_ps, 1)

            def turn_sums(a):
                pe.wait_ge(cs_ready, a + 1)
                pe.transpose(bank[7][:, 128:256], cs[:, half_cols(a)], ident[:, :]).then_inc(csT_ps, 1)

            stretch(pe, step, T_LEAD, 2, T_END, T_STEPS,
                    {HALF + 5: lambda: running_sums(0), HALF + 6: lambda: turn_sums(0)})

            pe.wait_ge(mix_weights, KW)
            pe.wait_ge(pair_ready, NG)

            conv_parts = [(ut_parts, PAD - j, wc_hi[:, j, :]) for j in range(KW)] + \
                         [(ut_pair, PAD - 2 * j, wc_lo[:, j, :]) for j in range(KW // 2)]

            def lstep(k, slot):
                m, o, f, r = k, k - 1, k - 2, k - 3

                def project_x(i):
                    if i == 0 and after(m, 4):
                        pe.wait_ge(res_ready, m - 3)
                    elif i == 0 and after(m, 2):
                        pe.wait_ge(hadd_ready, m - 1)
                    elif i == 0 and after(m, 1):
                        pe.wait_ge(bc_ready, 2 * m)
                    if i == 1 and live(o):
                        pe.wait_ge(yg_ready, 2 * o + 1)
                    for j in range(2):
                        seq = m * GB + (2 * i + j)
                        for n, (u, c0, w_) in enumerate(conv_parts):
                            ins = pe.matmul(bank[2 * i][:, j * DI:(j + 1) * DI], u[:, seq, c0:c0 + T],
                                            w_[:, 0:DI], start=(n == 0), stop=(n == len(conv_parts) - 1))
                    ins.then_inc(x_ps, 1)

                def project_z(i):
                    if i == 0 and live(o):
                        pe.wait_ge(yg_ready, 2 * o + 2)
                    if i == 1:
                        pe.wait_ge(xs_ready, 2 * m + 2)
                    for n, w_ in enumerate((wz_hi, wz_lo)):
                        ins = pe.matmul(bank[3 - i][:, :], w_[:, i * 128:(i + 1) * 128],
                                        ut_parts[:, bass.ts(m, GB), PAD:PAD + T], start=(n == 0), stop=(n == 1))
                    ins.then_inc(z_ps, 1)

                def project_bc():
                    pe.wait_ge(xs_ready, 2 * m + 1)
                    for n, (u, c0, w_) in enumerate(conv_parts):
                        ins = pe.matmul(bank[0][:, :], w_[:, DI:NXBC], u[:, bass.ts(m, GB), c0:c0 + T],
                                        start=(n == 0), stop=(n == len(conv_parts) - 1))
                    ins.then_inc(bc_ps, 1)

                def up(q):
                    if q == 0:
                        pe.wait_ge(u2lo_ready, f + 1)
                    if q >= 2:
                        pe.wait_ge(*hid_done(q - 2, f))
                    elif after(f, 1):
                        pe.wait_ge(*hid_done(NQ + q - 2, f - 1))
                    for n, w_ in enumerate((ew1_hi, ew1_lo)):
                        ins = pe.matmul(bank[4 + q % 2][:, :], w_[:, half(q) * 128:(half(q) + 1) * 128], u2T[:, :],
                                        start=(n == 0), stop=(n == 1))
                    ins.then_inc(hid_ps, 1)

                def down(q):
                    p, e, j = q // 4, q % 2, (q % 4) // 2
                    pe.wait_ge(*hid_done(q, f))
                    if q % 4 == 0 and p >= 2 and at(k, NG + 1):
                        pe.wait_ge(yvar_ready, NG)
                    elif q % 4 == 0 and (p >= 2 or after(f, 1)):
                        pe.wait_ge(prod_ready, NP * f + (p - 1))
                    if q == 4 and at(k, 2):
                        pe.wait_ge(csT_ready, 2)
                    pe.matmul(down_bank(k, p)[e * D:(e + 1) * D, :], ew2[:, half(q), :], hid[:, q % 4, :],
                              start=(j == 0), stop=(j == 1)).then_inc(down_done, 1)

                if live(f):
                    pe.wait_ge(u2_ready, f + 1)
                    if live(o):
                        pe.wait_ge(mix_ready, GB * o + GB)
                    for j in range(GB):
                        ins = pe.transpose(bank[1][:, j * T:(j + 1) * T], u2[:, j].rearrange("p i d -> p (i d)"),
                                           ident[:, :])
                    ins.then_inc(u2T_ps, 1)
                if live(m):
                    project_x(0)
                    project_z(0)
                if live(f):
                    if at(k, 2):
                        pe.wait_ge(expert_weights, 2)
                    pe.wait_ge(u2lo_ready, f + 1)
                    for j in range(GB):
                        for n, w_ in enumerate((wg_hi, wg_lo)):
                            ins = pe.matmul(bank[1][:, j * E:(j + 1) * E], u2T[:, j * T:(j + 1) * T], w_[:, :],
                                            start=(n == 0), stop=(n == 1))
                    ins.then_inc(s_ps, 1)
                if live(m):
                    project_x(1)
                for n in range(NQ // 2):
                    if live(f):
                        up(2 * n)
                        up(2 * n + 1)
                        if n:
                            down(2 * n - 2)
                            down(2 * n - 1)
                    if n == 0 and at(k, 2):
                        running_sums(1)
                    if n == 0 and live(m):
                        project_bc()
                    if n == 1 and at(k, 2):
                        turn_sums(1)
                    if n == 1 and live(f):
                        pe.wait_ge(gate, 7 * f + 7)
                        for j in range(GB):
                            ins = pe.transpose(bank[1][0:E, j * T:(j + 1) * T], comb[:, j, :], ident[:, :])
                        ins.then_inc(combT_ps, 1)
                    if n == 2 and live(m):
                        project_z(1)
                    if n == 3 and live(m):
                        pe.wait_ge(bc_ready, 2 * m + 2)
                        if live(f):
                            pe.wait_ge(combT_ready, f + 1)
                        elif live(o):
                            pe.wait_ge(mix_ready, GB * m)
                        for j in range(GB):
                            ins = pe.matmul(bank[1][:, j * T:(j + 1) * T], bT[:, j * T:(j + 1) * T],
                                            cT[:, j * T:(j + 1) * T], start=True, stop=True)
                        ins.then_inc(g_ps, 1)
                    if n == 3 and live(o):
                        pe.wait_ge(ysum_ready, o + 1)
                        if live(m):
                            pe.wait_ge(zs_ready, 2 * m + 2)
                        elif not live(f):
                            pe.wait_ge(yg_ready, 2 * o + 2)
                        for j in range(GB):
                            ins = pe.matmul(bank[2][:, j:j + 1], ysum[:, j * T:(j + 1) * T], ones[:, :],
                                            start=True, stop=True)
                        ins.then_inc(yssq_ps, 1)
                    if n == 3 and live(o):
                        if live(m):
                            pe.wait_ge(bc_ready, 2 * m + 2)
                        elif after(o, 3):
                            pe.wait_ge(res_ready, o - 2)
                        for j in range(GB):
                            for i in range(2):
                                ins = pe.matmul(bank[0][:, j * 2 * D:(j + 1) * 2 * D], yg[:, i, j * T:(j + 1) * T],
                                                wo[:, i].rearrange("p i d -> p (i d)"), start=(i == 0), stop=(i == 1))
                        ins.then_inc(o_ps, 1)
                    if n == 6 and live(r):
                        if at(k, L_STEPS - 1):
                            parts = [prod[:, p, :] for p in range(NP)]
                            pe.wait_ge(prod_ready, NP * NG)
                        else:
                            parts = [acc[:, :]]
                            pe.wait_ge(acc_sum, (NP - 1) * (r + 1))
                        if live(o):
                            pe.wait_ge(hadd_ready, o + 1)
                        elif after(r, 1):
                            pe.wait_ge(res_ready, r)
                        for j in range(GB):
                            for n_, part in enumerate(parts):
                                ins = pe.matmul(bank[0][:, j * D:(j + 1) * D], part[:, j * T:(j + 1) * T],
                                                pairs[:, :], start=(n_ == 0), stop=(n_ == len(parts) - 1))
                        ins.then_inc(out_ps, 1)
                if live(f):
                    down(NQ - 2)
                    down(NQ - 1)
                if live(m):
                    pe.wait_ge(zs_ready, 2 * m + 2)
                    if live(o):
                        pe.wait_ge(yvar_ready, o + 1)
                    for i in range(2):
                        for j in range(GB):
                            if i == 0:
                                pe.wait_ge(skip_ready, GB * m + (j + 2))
                            for hh in range(2):
                                ins = pe.matmul(bank[2 + i][hh * HD:(hh + 1) * HD, j * T:(j + 1) * T],
                                                xs[:, slot, j, 2 * i + hh, :], dec[:, j, 2 * i + hh, :],
                                                start=True, stop=True)
                        ins.then_inc(y_ps, 1)

            stretch(pe, lstep, L_LEAD, 2, NG, L_STEPS)


CONSTS = constants()


def kernel(**a):
    from concourse import bacc
    from concourse.bass_utils import run_bass_kernel_spmd

    def lay(x):
        return np.ascontiguousarray(np.asarray(x))

    arrays = {
        "ids": lay(np.asarray(a["x"]).T),
        "freq": lay(a["L0_tok_freq_bands"]), "tw1": lay(a["L0_tok_w1"]), "tb1": lay(a["L0_tok_b1"]),
        "gamma": lay(a["L0_tok_gamma"]), "beta": lay(a["L0_tok_beta"]),
        "tw2": lay(a["L0_tok_w2"]), "tb2": lay(a["L0_tok_b2"]),
        "winT": lay(np.asarray(a["L0_attn_in_proj_w"]).T),
        "convT": lay(np.asarray(a["L0_attn_conv_w"])[:, 0, :].T), "convb": lay(a["L0_attn_conv_b"]),
        "dtbias": lay(a["L0_attn_dt_bias"]), "alog": lay(a["L0_attn_A_log"]), "dskip": lay(a["L0_attn_D"]),
        "normw": lay(a["L0_attn_norm_w"]), "woT": lay(np.asarray(a["L0_attn_out_proj_w"]).T),
        "wgT": lay(np.asarray(a["L0_ffn_Wg"]).T), "bg": lay(a["L0_ffn_bg"]),
        "ew1T": lay(np.asarray(a["L0_ffn_W1"]).transpose(2, 0, 1).reshape(D, E * EH)),
        "eb1": lay(a["L0_ffn_b1"]),
        "ew2T": lay(np.asarray(a["L0_ffn_W2"]).transpose(0, 2, 1).reshape(E * EH, D)),
        "eb2": lay(a["L0_ffn_b2"]),
        **CONSTS,
    }
    nc = bacc.Bacc("TRN2", target_bir_lowering=False, num_devices=1)
    inp = {n: nc.dram_tensor(f"in_{n}", list(x.shape), mybir.dt.from_np(x.dtype), kind="ExternalInput").ap()
           for n, x in arrays.items()}
    out = nc.dram_tensor("out_tower", [NSEQ, T, D], F32, kind="ExternalOutput").ap()
    build(nc, inp, out)
    r = run_bass_kernel_spmd(nc, [{f"in_{n}": x for n, x in arrays.items()}], core_ids=[0])
    return r.results[0]["out_tower"]
```
